# Optimizing a Trainium2 kernel written in Bass

```python
import numpy as np
import jax
import jax.numpy as jnp

def _softmax(x, axis=-1):
    return jax.nn.softmax(x, axis=axis)

def _gelu(x):
    return jax.nn.gelu(x, approximate=True)

def _silu(x):
    return jax.nn.silu(x)

def _sigmoid(x):
    return jax.nn.sigmoid(x)

def _layernorm(x, axis=-1, eps=1e-05):
    m = jnp.mean(x, axis=axis, keepdims=True)
    v = jnp.var(x, axis=axis, keepdims=True)
    return (x - m) / jnp.sqrt(v + eps)

def _scatter_add(tgt, idx, src, axis=0):
    return tgt.at[idx].add(src)

def _segment_sum(src, seg, n):
    return jax.ops.segment_sum(src, seg, n)
kernel_name = 'mk_seq_postln_d2_jaxref_r8_1aa134'

def setup_inputs(seed: int=0):
    np.random.seed(seed)
    _w = jnp.asarray

    def _L0_attn_setup():
        import jax, jax.numpy as jnp
        import numpy as np
        DIM = 128
        NUM_HEADS = 16
        HEAD_DIM = DIM // NUM_HEADS
        EPS = 1e-06

        def rmsnorm(x, w):
            norm = jax.lax.rsqrt(jnp.mean(x * x, axis=-1, keepdims=True) + EPS)
            return x * norm * w
        key = jax.random.key(seed)
        ks = jax.random.split(key, 10)
        s = 0.02
        inp = {'x': jax.random.normal(ks[0], (2, 256, DIM), dtype=jnp.float32), 'Wq': jax.random.normal(ks[1], (DIM, DIM), dtype=jnp.float32) * s, 'bq': jnp.zeros((DIM,), dtype=jnp.float32), 'Wk': jax.random.normal(ks[2], (DIM, DIM), dtype=jnp.float32) * s, 'bk': jnp.zeros((DIM,), dtype=jnp.float32), 'Wv': jax.random.normal(ks[3], (DIM, DIM), dtype=jnp.float32) * s, 'bv': jnp.zeros((DIM,), dtype=jnp.float32), 'Wo': jax.random.normal(ks[4], (DIM, DIM), dtype=jnp.float32) * s, 'bo': jnp.zeros((DIM,), dtype=jnp.float32), 'norm_q_w': jnp.ones((DIM,), dtype=jnp.float32), 'norm_k_w': jnp.ones((DIM,), dtype=jnp.float32)}
        return inp
    _L0_attn_in = _L0_attn_setup()

    def _L0_ffn_setup():
        import jax, jax.numpy as jnp
        import numpy as np
        B, N, DIM = (2, 256, 128)
        HEADS, DIM_HEAD, EXPERTS = (8, 64, 8)
        SCALE = DIM_HEAD ** (-0.5)
        key = jax.random.key(seed)
        ks = jax.random.split(key, 6)
        dim_inner = HEADS * DIM_HEAD
        return {'x': jax.random.normal(ks[0], (B, N, DIM), jnp.float32), 'w_q': jax.random.normal(ks[1], (DIM, dim_inner), jnp.float32) * 0.02, 'w_k': jax.random.normal(ks[2], (DIM, dim_inner), jnp.float32) * 0.02, 'w_gate': jax.random.normal(ks[3], (DIM, HEADS * EXPERTS), jnp.float32) * 0.02, 'value_experts': jax.random.normal(ks[4], (EXPERTS, HEADS, DIM, DIM_HEAD), jnp.float32) * 0.02, 'output_experts': jax.random.normal(ks[5], (EXPERTS, HEADS, DIM_HEAD, DIM), jnp.float32) * 0.02}
    _L0_ffn_in = _L0_ffn_setup()

    def _L1_attn_setup():
        import jax, jax.numpy as jnp
        import numpy as np
        EMBED = 128
        EXPAND = 128
        B, T = (4, 256)
        PI = 3.141592653589793
        EPS = 1e-05

        def _gla_scan(q, k, v, g):
            Bq, Tq, H, Dk = q.shape
            Dv = v.shape[-1]
            scale = Dk ** (-0.5)

            def step(S, inp):
                qt, kt, vt, gt = inp
                S = S * jnp.exp(gt)[..., None] + kt[..., None] * vt[..., None, :]
                o = jnp.einsum('bhk,bhkv->bhv', qt * scale, S)
                return (S, o)
            S0 = jnp.zeros((Bq, H, Dk, Dv), q.dtype)
            seq = tuple((jnp.moveaxis(a, 1, 0) for a in (q, k, v, g)))
            _, out = jax.lax.scan(step, S0, seq)
            return jnp.moveaxis(out, 0, 1)
        key = jax.random.key(seed)
        ks = jax.random.split(key, 8)
        std = 0.02
        return {'x': jax.random.normal(ks[0], (B, T, EMBED), jnp.float32), 'wq': jax.random.normal(ks[1], (EMBED, EMBED), jnp.float32) * std, 'wk': jax.random.normal(ks[2], (EMBED, EMBED), jnp.float32) * std, 'wv': jax.random.normal(ks[3], (EMBED, EMBED), jnp.float32) * std, 'wo': jax.random.normal(ks[4], (EMBED, EMBED), jnp.float32) * std, 'wg1': jax.random.normal(ks[5], (EMBED, EXPAND), jnp.float32) * std, 'wg2': jax.random.normal(ks[6], (EXPAND, EMBED), jnp.float32) * std, 'norm_w': jnp.ones((EMBED,), jnp.float32)}
    _L1_attn_in = _L1_attn_setup()

    def _L1_ffn_setup():
        import jax, jax.numpy as jnp
        import numpy as np
        B, S, D = (4, 256, 128)
        EXP = 4
        H = EXP * D
        E = 8
        TOP_K = 2
        key = jax.random.key(seed)
        ks = jax.random.split(key, 8)
        scale1 = 1.0 / np.sqrt(D)
        scale2 = 1.0 / np.sqrt(H)
        x = jax.random.normal(ks[0], (B, S, D), dtype=jnp.float32)
        W1 = jax.random.uniform(ks[1], (E, D, H), jnp.float32, -scale1, scale1)
        b1 = jax.random.uniform(ks[2], (E, H), jnp.float32, -scale1, scale1)
        W2 = jax.random.uniform(ks[3], (E, H, D), jnp.float32, -scale2, scale2)
        b2 = jax.random.uniform(ks[4], (E, D), jnp.float32, -scale2, scale2)
        Wr = jax.random.uniform(ks[5], (D, E), jnp.float32, -scale1, scale1)
        br = jax.random.uniform(ks[6], (E,), jnp.float32, -scale1, scale1)
        return {'input_emb': x, 'W1': W1, 'b1': b1, 'W2': W2, 'b2': b2, 'Wr': Wr, 'br': br}
    _L1_ffn_in = _L1_ffn_setup()
    _d = {'L0_attn_x': _L0_attn_in['x'], 'L0_attn_Wq': _L0_attn_in['Wq'], 'L0_attn_bq': _L0_attn_in['bq'], 'L0_attn_Wk': _L0_attn_in['Wk'], 'L0_attn_bk': _L0_attn_in['bk'], 'L0_attn_Wv': _L0_attn_in['Wv'], 'L0_attn_bv': _L0_attn_in['bv'], 'L0_attn_Wo': _L0_attn_in['Wo'], 'L0_attn_bo': _L0_attn_in['bo'], 'L0_attn_norm_q_w': _L0_attn_in['norm_q_w'], 'L0_attn_norm_k_w': _L0_attn_in['norm_k_w'], 'L0_ffn_w_q': _L0_ffn_in['w_q'], 'L0_ffn_w_k': _L0_ffn_in['w_k'], 'L0_ffn_w_gate': _L0_ffn_in['w_gate'], 'L0_ffn_value_experts': _L0_ffn_in['value_experts'], 'L0_ffn_output_experts': _L0_ffn_in['output_experts'], 'L1_attn_wq': _L1_attn_in['wq'], 'L1_attn_wk': _L1_attn_in['wk'], 'L1_attn_wv': _L1_attn_in['wv'], 'L1_attn_wo': _L1_attn_in['wo'], 'L1_attn_wg1': _L1_attn_in['wg1'], 'L1_attn_wg2': _L1_attn_in['wg2'], 'L1_attn_norm_w': _L1_attn_in['norm_w'], 'L1_ffn_W1': _L1_ffn_in['W1'], 'L1_ffn_b1': _L1_ffn_in['b1'], 'L1_ffn_W2': _L1_ffn_in['W2'], 'L1_ffn_b2': _L1_ffn_in['b2'], 'L1_ffn_Wr': _L1_ffn_in['Wr'], 'L1_ffn_br': _L1_ffn_in['br']}
    _x0 = _d['L0_attn_x']
    _d['L0_attn_x'] = jax.random.normal(jax.random.fold_in(jax.random.key(seed), 1), (4, 512, 128), dtype=_x0.dtype)
    del _x0
    return _d

def reference(L0_attn_x, L0_attn_Wq, L0_attn_bq, L0_attn_Wk, L0_attn_bk, L0_attn_Wv, L0_attn_bv, L0_attn_Wo, L0_attn_bo, L0_attn_norm_q_w, L0_attn_norm_k_w, L0_ffn_w_q, L0_ffn_w_k, L0_ffn_w_gate, L0_ffn_value_experts, L0_ffn_output_experts, L1_attn_wq, L1_attn_wk, L1_attn_wv, L1_attn_wo, L1_attn_wg1, L1_attn_wg2, L1_attn_norm_w, L1_ffn_W1, L1_ffn_b1, L1_ffn_W2, L1_ffn_b2, L1_ffn_Wr, L1_ffn_br):

    def _L0_attn_ref(x, Wq, bq, Wk, bk, Wv, bv, Wo, bo, norm_q_w, norm_k_w):
        import jax, jax.numpy as jnp
        import numpy as np
        DIM = 128
        NUM_HEADS = 16
        HEAD_DIM = DIM // NUM_HEADS
        EPS = 1e-06

        def rmsnorm(x, w):
            norm = jax.lax.rsqrt(jnp.mean(x * x, axis=-1, keepdims=True) + EPS)
            return x * norm * w
        B, S, D = x.shape
        scale = HEAD_DIM ** (-0.5)
        q = x @ Wq.T + bq
        k = x @ Wk.T + bk
        v = x @ Wv.T + bv
        q = rmsnorm(q, norm_q_w)
        k = rmsnorm(k, norm_k_w)
        q = q.reshape(B, S, NUM_HEADS, HEAD_DIM)
        k = k.reshape(B, S, NUM_HEADS, HEAD_DIM)
        v = v.reshape(B, S, NUM_HEADS, HEAD_DIM)
        attn = jnp.einsum('bqhd,bkhd->bhqk', q, k) * scale
        attn = jax.nn.softmax(attn, axis=-1)
        out = jnp.einsum('bhqk,bkhd->bqhd', attn, v).reshape(B, S, D)
        return out @ Wo.T + bo

    def _L0_ffn_ref(x, w_q, w_k, w_gate, value_experts, output_experts):
        import jax, jax.numpy as jnp
        import numpy as np
        B, N, DIM = (2, 256, 128)
        HEADS, DIM_HEAD, EXPERTS = (8, 64, 8)
        SCALE = DIM_HEAD ** (-0.5)
        b, n, _ = x.shape
        q = (x @ w_q).reshape(b, n, HEADS, DIM_HEAD).transpose(0, 2, 1, 3)
        k = (x @ w_k).reshape(b, n, HEADS, DIM_HEAD).transpose(0, 2, 1, 3)
        gates = jax.nn.sigmoid((x @ w_gate).reshape(b, n, HEADS, EXPERTS).transpose(0, 2, 1, 3))
        sel = jnp.argmax(gates, axis=-1)
        gm = jax.nn.one_hot(sel, EXPERTS, dtype=x.dtype) * gates
        values = jnp.einsum('bhne,ehdk,bnd->bhnk', gm, value_experts, x)
        sim = jnp.einsum('bhid,bhjd->bhij', q * SCALE, k)
        causal_mask = jnp.triu(jnp.ones((n, n), dtype=bool), 1)
        sim = jnp.where(causal_mask, jnp.finfo(sim.dtype).min, sim)
        attn = jax.nn.softmax(sim, axis=-1)
        out = jnp.einsum('bhij,bhjk->bhik', attn, values)
        out = jnp.einsum('bhne,ehkd,bhnk->bhnd', gm, output_experts, out)
        return out.sum(axis=1)

    def _L1_attn_ref(x, wq, wk, wv, wo, wg1, wg2, norm_w):
        import jax, jax.numpy as jnp
        import numpy as np
        EMBED = 128
        EXPAND = 128
        B, T = (4, 256)
        PI = 3.141592653589793
        EPS = 1e-05

        def _gla_scan(q, k, v, g):
            Bq, Tq, H, Dk = q.shape
            Dv = v.shape[-1]
            scale = Dk ** (-0.5)

            def step(S, inp):
                qt, kt, vt, gt = inp
                S = S * jnp.exp(gt)[..., None] + kt[..., None] * vt[..., None, :]
                o = jnp.einsum('bhk,bhkv->bhv', qt * scale, S)
                return (S, o)
            S0 = jnp.zeros((Bq, H, Dk, Dv), q.dtype)
            seq = tuple((jnp.moveaxis(a, 1, 0) for a in (q, k, v, g)))
            _, out = jax.lax.scan(step, S0, seq)
            return jnp.moveaxis(out, 0, 1)
        Bx, Tx, E = x.shape
        d = EXPAND
        H = E // d
        q = jax.nn.silu(x @ wq)
        k = jax.nn.sigmoid(x @ wk)
        v = x @ wv
        f = 1.0 - k
        log_f = jnp.log(f)
        q4 = q.reshape(Bx, Tx, H, d)
        k4 = k.reshape(Bx, Tx, H, d)
        v4 = v.reshape(Bx, Tx, H, d)
        f4 = f.reshape(Bx, Tx, H, d)
        g4 = log_f.reshape(Bx, Tx, H, d)
        sign_f = jnp.sign(f4 - 0.5)
        theta = jnp.cumsum(sign_f, axis=1) * PI
        sin, cos = (jnp.sin(theta), jnp.cos(theta))
        qr = jnp.concatenate([q4 * cos, q4 * sin], axis=-1)
        kr = jnp.concatenate([k4 * cos, k4 * sin], axis=-1)
        g = jnp.concatenate([g4, g4], axis=-1)
        out = _gla_scan(qr, kr, v4, g)
        out = out.reshape(Bx, Tx, E)
        gate = jax.nn.sigmoid(x @ wg1 @ wg2)
        out = out * gate
        mu = jnp.mean(out, axis=-1, keepdims=True)
        var = jnp.mean(jnp.square(out - mu), axis=-1, keepdims=True)
        out = (out - mu) * jax.lax.rsqrt(var + EPS) * norm_w
        return out @ wo

    def _L1_ffn_ref(input_emb, W1, b1, W2, b2, Wr, br):
        import jax, jax.numpy as jnp
        import numpy as np
        B, S, D = (4, 256, 128)
        EXP = 4
        H = EXP * D
        E = 8
        TOP_K = 2
        logits = jnp.einsum('bsd,de->bse', input_emb, Wr) + br
        route_w = jax.nn.softmax(logits, axis=-1)
        _, topk_idx = jax.lax.top_k(route_w, TOP_K)
        mask = jax.nn.one_hot(topk_idx, E, dtype=route_w.dtype).sum(-2)
        routed = route_w * mask
        routed = routed / routed.sum(axis=-1, keepdims=True)
        h = jax.nn.relu(jnp.einsum('bsd,edh->ebsh', input_emb, W1) + b1[:, None, None, :])
        expert_out = jnp.einsum('ebsh,ehd->ebsd', h, W2) + b2[:, None, None, :]
        return jnp.einsum('bse,ebsd->bsd', routed, expert_out)
    x = L0_attn_x
    x = _layernorm(x + _L0_attn_ref(x, L0_attn_Wq, L0_attn_bq, L0_attn_Wk, L0_attn_bk, L0_attn_Wv, L0_attn_bv, L0_attn_Wo, L0_attn_bo, L0_attn_norm_q_w, L0_attn_norm_k_w), axis=-1)
    x = _layernorm(x + _L0_ffn_ref(x, L0_ffn_w_q, L0_ffn_w_k, L0_ffn_w_gate, L0_ffn_value_experts, L0_ffn_output_experts), axis=-1)
    x = _layernorm(x + _L1_attn_ref(x, L1_attn_wq, L1_attn_wk, L1_attn_wv, L1_attn_wo, L1_attn_wg1, L1_attn_wg2, L1_attn_norm_w), axis=-1)
    x = _layernorm(x + _L1_ffn_ref(x, L1_ffn_W1, L1_ffn_b1, L1_ffn_W2, L1_ffn_b2, L1_ffn_Wr, L1_ffn_br), axis=-1)
    return x

_drawn_inputs = setup_inputs


def setup_inputs(seed=0):
    import zlib

    import numpy as np

    out = dict(_drawn_inputs(seed))
    spreads = {'L0_attn_bq': (0.0, 0.8),
     'L0_attn_bk': (0.0, 0.8),
     'L0_attn_bv': (0.0, 0.268),
     'L0_attn_bo': (0.0, 0.1),
     'L0_attn_norm_q_w': (1.0, 0.6),
     'L0_attn_norm_k_w': (1.0, 0.6),
     'L1_attn_norm_w': (1.0, 0.2)}
    factors = {'L0_attn_Wq': 6.835,
     'L0_attn_Wk': 5.782,
     'L0_attn_Wv': 5.689,
     'L0_ffn_w_q': 8.0,
     'L0_ffn_w_k': 8.0,
     'L0_ffn_w_gate': 6.981,
     'L0_ffn_value_experts': 7.58,
     'L0_ffn_output_experts': 7.398,
     'L1_attn_wg1': 6.668,
     'L1_attn_wg2': 6.131,
     'L1_ffn_b1': 3.789,
     'L1_ffn_b2': 3.192}
    for name, (base, spread) in spreads.items():
        noise = np.random.default_rng([zlib.crc32(name.encode()), seed]).standard_normal(out[name].shape)
        drawn = base * np.exp(spread * noise) if base else spread * noise
        out[name] = jnp.asarray(drawn.astype(out[name].dtype))
    for name, factor in factors.items():
        out[name] = (out[name] * factor).astype(out[name].dtype)
    return out
```

```python
from contextlib import ExitStack

import numpy as np
import concourse.bass as bass
from concourse import mybir

F32, BF16, F32R, U32 = mybir.dt.float32, mybir.dt.bfloat16, mybir.dt.float32r, mybir.dt.uint32
ALU, ACT, AX = mybir.AluOpType, mybir.ActivationFunctionType, mybir.AxisListType

B, S, D = 4, 512, 128
P = 128
T = S // P
H0, HD = 16, 8
GROUP = 4
GROUPS = H0 // GROUP
PARTS = 3
PROD_ROWS = PARTS * PARTS * HD
STACK_ROWS = PROD_ROWS + PARTS
VW = 32
HF, FD, EF = 8, 64, 8
HE = HF * EF
HALF = HF // 2
PAD = 96
PAIRS = EF // 2
NEG = -3.0e38
LEVELS = 9
IN_TILE = 7
PI1, PI2, PI3 = 3.140625, 9.67502593994140625e-4, 1.509957990978376e-7
PI = 3.1415927410125732
EM, HID = 8, 512
HC = HID // P
RING = 8
LNS = 5

SCORE0, PROB0, MISC, ACC = 0, 3, 6, 7

PER = dict(
    fw_in=32, mw_in=32, ones_in=1, vals_one=1, x_in=32, proj=3, lin=4, msq=2, rs=4, qk_split=2, scr_out=32 * 3, stack_in=16 * 4, vaug=4, s_out=H0 * T,
    s_max=H0 * T, m_t=GROUPS, m_rows=GROUPS, m_out=GROUPS * 16, m_in0=16, m_in1=16, m_in2=16, m_in3=16, st_out=H0 * T, st_exp=H0 * T, pv=H0 * T,
    o_sb=GROUPS, o_t=GROUPS, o_norm=GROUPS, at_t=1, at_sb=1, attn_y=1, xb=1,
    ln_var=LNS, ln_rs=2 * LNS, ln_out=LNS, ln_t=3, ln_sb=3,
    fp=2 * HF, fp_hi=2 * HF, fp_lo=2 * HF, gate_p=1, gate_e=1, gate_done=1, gm_t=1, gm_sb=1,
    fs=HF * T, fs_max=HF * T, fm_cut=2, fm_t=2, fm_sb=2, ve=T * EF, ve_first=T, ve_sel=T * (EF - 1), vals_in=T,
    fst=HF * T, fst_exp=HF * T, fst_cut=HF * T, fpv=HF * T, fo_lo=HF, fo_hi=HF, mask=HF * PAIRS, g_in=HF * PAIRS,
    oe=HF * PAIRS, fo_sb=1, fo_t=1,
    g_proj=4, g_exp=2, g_v=1, g_h1=1, lv_in=LEVELS + 1, lv_mm=LEVELS + 1, lv_out=LEVELS + 1, g_o=1,
    gg_p=1, gg_e=1, gn=1, gn_t=1, gn_sb=1, gla_p=1,
    r_p=1, r_m=1, r_e=1, r_done=1, r_t=1, r_sb=1, w1=EM * HC, relu_a=EM * HC // 2, relu_v=EM * HC // 2,
    w2=EM * HC, rb=EM, oe_b=EM, moe_mul=EM, moe_acc=1, mo_t=1, stored=16,
)

DVE_STEPS = 170


def build(nc, ins, out, upto=4, steps=None, counts=None, NB=B):
    dve_steps, = steps or (DVE_STEPS,)
    with ExitStack() as ctx:
        def sb(name, shape, dt=F32):
            return ctx.enter_context(nc.sbuf_tensor(name, shape, dt))

        s = {n: ctx.enter_context(nc.semaphore(n)) for n in PER}
        m_in = [s["m_in0"], s["m_in1"], s["m_in2"], s["m_in3"]]
        batch_free = ctx.enter_context(nc.semaphore("batch_free"))
        loaded = ctx.enter_context(nc.semaphore("loaded"))
        const_ready = ctx.enter_context(nc.semaphore("const_ready"))
        passed = ctx.enter_context(nc.semaphore("passed"))
        dve_step = ctx.enter_context(nc.semaphore("dve_step"))

        bank = [ctx.enter_context(nc.psum_tensor(f"bank{i}", [P, 512], F32)) for i in range(8)]
        q_scr = nc.dram_tensor("q_scr", (PARTS, HD, H0, S), BF16).ap()
        m_scr = nc.dram_tensor("m_scr", (GROUPS, PARTS, GROUP * T, P), BF16).ap()
        k_scr = nc.dram_tensor("k_scr", (PARTS, HD, H0, S), BF16).ap()

        w = {}
        loads = []

        def weight(name, shape, dt=F32, src=None, sides=None):
            t = sb(name, shape, dt)
            w[name] = t
            loads.append((t, ins[name]))

        for name in ("wq0", "wk0", "wv0", "wo0", "gwq", "gwk", "gwv", "gwg1", "gwg2", "gwo", "ident", "bv_row",
                     "bo_row", "gn_row"):
            weight(name, [P, P])
        weight("cols", [P, 4])
        weight("fwq", [P, HF, P])
        weight("fwk", [P, HF, P])
        weight("fgate", [P, HE])
        weight("b1c", [P, EM * HC])
        weight("b2c", [P, EM])
        weight("wr", [P, EM])
        weight("br_row", [P, EM])
        weight("ramp", [P, EF])
        weight("picks", [P, HE + EM + HALF])
        weight("cut_row", [P, S])
        weight("level_mask", [P, IN_TILE + 1, P])
        pick_wide = sb("pick_wide", [P, HE * FD], F32R)
        pick_e = sb("pick_e", [PAD, EM], F32R)
        pick_h = sb("pick_h", [PAD, HALF], BF16)
        ident_b = sb("ident_b", [P, P], BF16)
        ones = sb("ones", [P, P])
        experts = sb("experts", [P, 16 * S])
        w["ve"] = experts[:, 0:8 * S].rearrange("p (e n) -> p e n", e=EF)
        w["oe"] = experts[:, 8 * S:].rearrange("p (c n) -> p c n", n=P)
        w["w1"] = experts[:, 0:8 * S].rearrange("p (e n) -> p e n", e=EM)
        w["w2"] = experts[:, 8 * S:].rearrange("p (c n) -> p c n", n=P)
        q_scale = sb("q_scale", [P, 1])
        eps = sb("eps", [P, 2])

        xT = sb("xT", [P, S])
        x_next = sb("x_next", [P, T, P])
        y = sb("y", [P, T, P])
        ln_st = sb("ln_st", [P, T, 6])
        ln_mv = sb("ln_mv", [P, T, 2])
        ln_r = sb("ln_r", [P, 2, T])
        vaug = sb("vaug", [P, T, H0, VW])
        region = sb("region", [P, 16 * S], F32R)
        stack = region[:, :].bitcast(BF16).rearrange("r (n h s) -> r n h s", n=2, h=H0)
        f_q = region[:, 0:HALF * S].rearrange("p (h s) -> p h s", h=HALF)
        f_k = region[:, HALF * S:3 * HALF * S].rearrange("p (h n s) -> p h n s", h=HALF, n=2)
        m_tok = sb("m_tok", [P, H0 * T])
        m_row = sb("m_row", [GROUP * T, GROUPS, PARTS, P], BF16)
        m_rest = sb("m_rest", [P, 2, P])
        probs = sb("probs", [P, RING, S])
        wide = sb("wide", [P, 6, S])
        vals = sb("vals", [P, T, HF, P])
        gm_tok = sb("gm_tok", [P, T, 2, HE], F32R)
        gmT = sb("gmT", [P, S], F32R)
        oh = sb("oh", [P, T * HF, EF])
        gs = sb("gs", [P, 3, T * HE])
        gsm = sb("gsm", [P, 3, T * HF])
        fm_tok = sb("fm_tok", [P, T, HF])
        fm_parts = sb("fm_parts", [P, T, PARTS, HALF], BF16)
        fm_rest = sb("fm_rest", [P, T, HALF])
        rT = sb("rT", [PAD, S], F32R)
        r_tok = sb("r_tok", [P, T, 2, EM], F32R)
        rt = sb("rt", [P, 6, T, EM])
        rt1 = sb("rt1", [P, 4, T])
        fmT = sb("fmT", [PAD, S], BF16)

        gla = vals[:].rearrange("p t h d -> p (t h d)").rearrange("p (n s) -> p n s", s=S)
        qc, kc, pre, suf, at_diag, v_tok = gla[:, 0:2], gla[:, 2:4], gla[:, 4], gla[:, 5], gla[:, 6], gla[:, 7]
        q_lv, k_lv = (probs[:, 0:2], probs[:, 2:4]), (probs[:, 4:6], probs[:, 6:8])
        at_far, at_near, h1T = wide[:, 4], wide[:, 5, 0:2 * P], gs[:].rearrange("p a b -> p (a b)")[:, 0:S]
        parts = probs[:, 0:PARTS, :].bitcast(BF16).rearrange("p n s -> p (n s)").rearrange("p (n c s) -> p n c s", n=2, c=PARTS)

        block = ctx.enter_context(nc.Block())


        @block.sync
        def _(sp):
            for t, src in loads:
                sp.dma_start(t[:], src).then_inc(loaded, 16)
            n_loads[0] = len(loads)
            with sp.Fori(0, NB) as b:
                at = lambda name, n: b * PER[name] + n
                sp.wait_ge(batch_free, b + 1)
                sp.dma_start(xT[:], ins["xT"][bass.ds(b, 1)].rearrange("o p n -> (o p) n")).then_inc(s["x_in"], 16)
                sp.dma_start(y[:], ins["x"][bass.ds(b, 1)].rearrange("o (t p) d -> p (o t) d", p=P)).then_inc(s["x_in"], 16)
                sp.dma_start(experts[:, 0:8 * S], ins["ve"].rearrange("p e n -> p (e n)")).then_inc(s["fw_in"], 16)
                sp.dma_start(experts[:, 8 * S:], ins["oe"].rearrange("p c n -> p (c n)")).then_inc(s["fw_in"], 16)
                for n, scr in enumerate((q_scr, k_scr)):
                    sp.wait_ge(s["qk_split"], at("qk_split", n + 1))
                    for c in range(PARTS):
                        sp.dma_start(scr[c].rearrange("d h s -> h d s"), parts[:, n, c, :]).then_inc(s["scr_out"], 16)
                    sp.wait_ge(s["scr_out"], at("scr_out", 48 * (n + 1)))
                    if n == 0:
                        for c in range(PARTS):
                            dst = stack[PARTS * HD * c:PARTS * HD * (c + 1), 0].rearrange("r h s -> r (h s)")
                            src = scr[c].rearrange("d h s -> d (h s)").unsqueeze(0).to_broadcast([PARTS, HD, H0 * S])
                            sp.dma_start(dst, src).then_inc(s["stack_in"], 16)
                    else:
                        sp.wait_ge(s["ones_in"], at("ones_in", 1))
                        src = scr.rearrange("c d h s -> (c d) (h s)").unsqueeze(0).to_broadcast([PARTS, PARTS * HD, H0 * S])
                        sp.dma_start(stack[0:PROD_ROWS, 1].rearrange("r h s -> r (h s)"), src).then_inc(s["stack_in"], 16)
                for g in range(GROUPS):
                    sp.wait_ge(s["m_rows"], at("m_rows", g + 1))
                    sp.dma_start(m_scr[g].rearrange("c r p -> r c p"), m_row[:, g]).then_inc(s["m_out"], 16)
                    sp.wait_ge(s["m_out"], at("m_out", 16 * (g + 1)))
                    sp.dma_start(stack[PROD_ROWS:STACK_ROWS, 0, GROUP * g:GROUP * (g + 1), :].rearrange("c h s -> c (h s)"),
                                 m_scr[g].rearrange("c r p -> c (r p)")).then_inc(m_in[g], 16)
                if upto >= 4:
                    sp.wait_ge(s["fo_sb"], at("fo_sb", 1))
                    sp.dma_start(experts[:, 0:8 * S], ins["w1"].rearrange("p e n -> p (e n)")).then_inc(s["mw_in"], 16)
                    sp.dma_start(experts[:, 8 * S:], ins["w2"].rearrange("p c n -> p (c n)")).then_inc(s["mw_in"], 16)
                final = {1: ("ln_out", 1), 2: ("ln_out", 2), 3: ("ln_out", 4), 4: ("ln_out", 5)}[upto]
                sp.wait_ge(s["ln_out"], at(*final))
                sp.dma_start(out[bass.ds(b, 1)].rearrange("o (t p) d -> p (o t) d", p=P), x_next[:]).then_inc(s["stored"], 16)
                sp.wait_ge(s["stored"], at("stored", 16))
                sp.sem_inc(batch_free, 1)

        @block.gpsimd
        def _(pool):
            pool.memset(ones[:], 1.0).then_inc(const_ready, 1)
            pool.memset(vaug[:], 1.0).then_inc(const_ready, 1)
            pool.memset(fmT[:], 0.0).then_inc(const_ready, 1)
            pool.memset(rT[:].bitcast(U32), 0).then_inc(const_ready, 1)
            pool.memset(eps[:, 0:1], 1e-6).then_inc(const_ready, 1)
            pool.memset(eps[:, 1:2], 1e-5).then_inc(const_ready, 1)
            pool.wait_ge(const_ready, CONSTS)
            pool.sem_inc(batch_free, 1)
            with pool.Fori(0, NB) as b:
                at = lambda name, n: b * PER[name] + n
                pool.wait_ge(batch_free, b + 1)
                pool.sem_inc(passed, 1)
                pool.memset(stack[64:STACK_ROWS, 1], 1.0).then_inc(s["ones_in"], 1)
                pool.wait_ge(s["ones_in"], at("ones_in", 1))
                pool.wait_ge(s["x_in"], at("x_in", 32))
                pool.tensor_tensor(y[:], y[:], w["bo_row"][:].unsqueeze(1).to_broadcast([P, T, P]), ALU.add).then_inc(s["xb"], 1)
                if upto >= 2:
                    pool.memset(vals[:, :, :, FD:P], 1.0).then_inc(s["vals_one"], 1)
                    for h in range(HF):
                        for kt in range(T):
                            j = h * T + kt
                            pool.wait_ge(s["fst_exp"], at("fst_exp", j + 1))
                            pool.sem_inc(passed, 1)
                            pool.affine_select(out=probs[:, j % RING, 0:P], in_=probs[:, j % RING, 0:P],
                                               compare_op=ALU.is_ge, fill=0.0, base=0, pattern=[[1, P]],
                                               channel_multiplier=-1).then_inc(s["fst_cut"], 1)

        @block.tensor
        def _(pe):
            pe.wait_ge(loaded, 16 * n_loads[0])
            pe.wait_ge(const_ready, CONSTS)
            with pe.Fori(0, NB) as b:
                at = lambda name, n: b * PER[name] + n

                def mm(o, l, r, start=True, stop=True):
                    return pe.matmul(o, lhsT=l, rhs=r, start=start, stop=stop, skip_group_check=True)

                def turn_tiles(dst, src):
                    for t in range(T):
                        last = pe.transpose(dst[:, t * P:(t + 1) * P], src(t), w["ident"][:])
                    return last

                pe.wait_ge(s["x_in"], at("x_in", 32))
                mm(bank[0][:], w["wq0"][:], xT[:]).then_inc(s["proj"], 1)
                mm(bank[1][:], w["wk0"][:], xT[:]).then_inc(s["proj"], 1)
                for t in range(T):
                    last = mm(bank[2][:, t * P:(t + 1) * P], xT[:, t * P:(t + 1) * P], w["wv0"][:])
                last.then_inc(s["proj"], 1)
                for n in range(2):
                    pe.wait_ge(s["lin"], at("lin", 2 * n + 2))
                    mm(bank[3 + n][:], ones[:], wide[:, 2, :] if n == 0 else wide[:, 3, :]).then_inc(s["msq"], 1)

                def scores(g):
                    for hh in range(GROUP):
                        h = GROUP * g + hh
                        for t in range(T):
                            i = h * T + t
                            if i >= 3:
                                pe.wait_ge(s["s_max"], at("s_max", i - 2))
                            mm(bank[SCORE0 + i % 3][:], stack[0:PROD_ROWS, 0, h, t * P:(t + 1) * P],
                               stack[0:PROD_ROWS, 1, h, :]).then_inc(s["s_out"], 1)

                def turn_max(g):
                    pe.wait_ge(s["s_max"], at("s_max", GROUP * T * (g + 1)))
                    if g:
                        pe.wait_ge(s["o_norm"], at("o_norm", g - 1)) if g > 1 else None
                        pe.wait_ge(s["m_rows"], at("m_rows", g))
                    pe.transpose(bank[MISC][0:GROUP * T, 0:P], m_tok[:, GROUP * T * g:GROUP * T * (g + 1)],
                                 w["ident"][:]).then_inc(s["m_t"], 1)

                def st_scores(g, kt):
                    for hh in range(GROUP):
                        h = GROUP * g + hh
                        j = (g * T + kt) * GROUP + hh
                        if j >= 3:
                            pe.wait_ge(s["st_exp"], at("st_exp", j - 2))
                        mm(bank[PROB0 + j % 3][:], stack[0:STACK_ROWS, 1, h, kt * P:(kt + 1) * P],
                           stack[0:STACK_ROWS, 0, h, :]).then_inc(s["st_out"], 1)

                def weigh(g, kt):
                    for hh in range(GROUP):
                        h = GROUP * g + hh
                        j = (g * T + kt) * GROUP + hh
                        pe.wait_ge(s["st_exp"], at("st_exp", j + 1))
                        mm(bank[ACC][32 * hh:32 * (hh + 1), :], vaug[:, kt, h, :], probs[:, j % RING, :],
                           start=(kt == 0), stop=(kt == T - 1)).then_inc(s["pv"], 1)

                def turn_out(g):
                    pe.wait_ge(s["o_sb"], at("o_sb", g + 1))
                    pe.wait_ge(s["m_rows"], at("m_rows", min(g + 2, GROUPS)))
                    turn_tiles(bank[MISC], lambda t: wide[:, 4 + g % 2, t * P:(t + 1) * P]).then_inc(s["o_t"], 1)

                pe.wait_ge(s["stack_in"], at("stack_in", 64))
                pe.wait_ge(s["vaug"], at("vaug", 4))
                scores(0)
                turn_max(0)
                for g in range(GROUPS):
                    if g + 1 < GROUPS:
                        scores(g + 1)
                        turn_max(g + 1)
                    pe.wait_ge(m_in[g], b * 16 + 16)
                    st_scores(g, 0)
                    for kt in range(T):
                        if kt + 1 < T:
                            st_scores(g, kt + 1)
                        if kt == 0 and g:
                            pe.wait_ge(s["o_sb"], at("o_sb", g))
                        weigh(g, kt)
                    turn_out(g)
                pe.wait_ge(s["o_norm"], at("o_norm", GROUPS))
                turn_tiles(bank[MISC], lambda t: x_next[:, t, :]).then_inc(s["at_t"], 1)
                pe.wait_ge(s["at_sb"], at("at_sb", 1))
                for t in range(T):
                    last = mm(bank[0][:, t * P:(t + 1) * P], wide[:, 0, t * P:(t + 1) * P], w["wo0"][:])
                last.then_inc(s["attn_y"], 1)

                def turn_x(n, norm):
                    pe.wait_ge(s["ln_out"], at("ln_out", norm))
                    turn_tiles(bank[MISC], lambda t: x_next[:, t, :]).then_inc(s["ln_t"], 1)

                turn_x(1, 1)

                if upto >= 2:
                    pe.wait_ge(s["ln_sb"], at("ln_sb", 1))
                    for t in range(T):
                        last = mm(bank[3][:, t * HE:(t + 1) * HE], xT[:, t * P:(t + 1) * P], w["fgate"][:])
                    last.then_inc(s["gate_p"], 1)
                    for half in range(2):
                        for i in range(2 * HALF):
                            n = 2 * HALF * half + i
                            if n >= 2:
                                pe.wait_ge(s["fp_lo"], at("fp_lo", n - 1))
                            if half and i < 2:
                                pe.wait_ge(s["g_in"], at("g_in", HALF * PAIRS))
                            mm(bank[n % 2][:], (w["fwk"] if i % 2 else w["fwq"])[:, HALF * half + i // 2, :],
                               xT[:]).then_inc(s["fp"], 1)
                        for i in range(HALF * T * half, HALF * T * (half + 1)):
                            hh, t = i // T - HALF * half, i % T
                            n = (t + 1) * P
                            if i % (HALF * T) < 2:
                                pe.wait_ge(s["fp_lo"], at("fp_lo", 2 * HALF * (half + 1)))
                            if i >= 2:
                                pe.wait_ge(s["fs_max"], at("fs_max", i - 1))
                            mm(bank[i % 2][:, 0:n], f_q[:, hh, t * P:n], f_k[:, hh, 0, 0:n], True, False)
                            mm(bank[i % 2][:, 0:n], f_q[:, hh, t * P:n], f_k[:, hh, 1, 0:n], False, True).then_inc(s["fs"], 1)
                        if half == 0:
                            pe.wait_ge(s["gate_done"], at("gate_done", 1))
                            turn_tiles(bank[MISC], lambda t: gm_tok[:, t].rearrange("p a c -> p (a c)").bitcast(F32)).then_inc(s["gm_t"], 1)
                            pe.wait_ge(s["fw_in"], at("fw_in", 32))
                            pe.wait_ge(s["gate_e"], at("gate_e", 1))
                            for i in range(T * EF):
                                t, e = i // EF, i % EF
                                if i >= 3:
                                    o = i - 3
                                    if o % EF == 0:
                                        pe.wait_ge(s["ve_first"], at("ve_first", o // EF + 1))
                                    else:
                                        pe.wait_ge(s["ve_sel"], at("ve_sel", o // EF * (EF - 1) + o % EF))
                                mm(bank[PROB0 + i % 3][:], xT[:, t * P:(t + 1) * P], w["ve"][:, e, :]).then_inc(s["ve"], 1)
                        pe.wait_ge(s["fm_cut"], at("fm_cut", half + 1))
                        if half == 0:
                            pe.wait_ge(s["gm_sb"], at("gm_sb", 1))
                        else:
                            pe.wait_ge(s["fo_lo"], at("fo_lo", HALF))
                        for t in range(T):
                            last = pe.transpose(bank[MISC][:].bitcast(BF16)[0:PARTS * HALF, t * P:(t + 1) * P],
                                                fm_parts[:, t].rearrange("p a c -> p (a c)"), ident_b[:])
                        last.then_inc(s["fm_t"], 1)
                        if half == 0:
                            pe.wait_ge(s["vals_in"], at("vals_in", T))
                            pe.wait_ge(s["vals_one"], at("vals_one", 1))

                        def f_transposed(h):
                            hh = h - HALF * half
                            for kt in range(T):
                                j = h * T + kt
                                n = S - kt * P
                                if j >= 3:
                                    pe.wait_ge(s["fst_exp"], at("fst_exp", j - 2))
                                o = bank[PROB0 + j % 3][:, 0:n]
                                mm(o, f_k[:, hh, 0, kt * P:(kt + 1) * P], f_q[:, hh, kt * P:S], True, False)
                                mm(o, f_k[:, hh, 1, kt * P:(kt + 1) * P], f_q[:, hh, kt * P:S], False, False)
                                mm(o, pick_h[:, hh:hh + 1].to_broadcast([PAD, P]), fmT[:, kt * P:S], False, True).then_inc(s["fst"], 1)

                        def f_weigh(h):
                            if h >= 2:
                                pe.wait_ge(s["fo_lo"], at("fo_lo", h - 1))
                            for kt in range(T):
                                j = h * T + kt
                                pe.wait_ge(s["fst_cut"], at("fst_cut", j + 1))
                                mm(bank[7 - h % 2][:, kt * P:S], vals[:, kt, h, :], probs[:, j % RING, 0:S - kt * P],
                                   kt == 0, kt == T - 1).then_inc(s["fpv"], 1)

                        def experts_out(h):
                            for pr in range(PAIRS):
                                c = h * PAIRS + pr
                                if c >= 2:
                                    pe.wait_ge(s["g_in"], at("g_in", c - 1))
                                if pr < 2 and h % HALF == 0:
                                    pe.wait_ge(s["fs_max"], at("fs_max", HALF * T * (half + 1)))
                                mm(bank[c % 2][:], pick_wide[:, P * c:P * (c + 1)],
                                   gmT[:]).then_inc(s["mask"], 1)
                                if c % (HALF * PAIRS):
                                    expert_sum(c - 1)

                        def expert_sum(c):
                            pe.wait_ge(s["g_in"], at("g_in", c + 1))
                            mm(bank[2][:], w["oe"][:, c, :], wide[:, c % 2, :], c == 0, c == HF * PAIRS - 1).then_inc(s["oe"], 1)

                        pe.wait_ge(s["fm_sb"], at("fm_sb", half + 1))
                        for h in range(HALF * half, HALF * (half + 1)):
                            f_transposed(h)
                            if h % HALF:
                                experts_out(h - 1)
                            f_weigh(h)
                        experts_out(HALF * half + HALF - 1)
                        expert_sum(HALF * PAIRS * (half + 1) - 1)
                    pe.wait_ge(s["fo_sb"], at("fo_sb", 1))
                    pe.wait_ge(s["fo_lo"], at("fo_lo", HF))
                    turn_tiles(bank[MISC], lambda t: wide[:, 5, t * P:(t + 1) * P]).then_inc(s["fo_t"], 1)
                    turn_x(2, 2)

                if upto >= 3:
                    pe.wait_ge(s["ln_sb"], at("ln_sb", 2))
                    mm(bank[0][:], w["gwq"][:], xT[:]).then_inc(s["g_proj"], 1)
                    mm(bank[1][:], w["gwk"][:], xT[:]).then_inc(s["g_proj"], 1)
                    mm(bank[2][:], w["gwg1"][:], xT[:]).then_inc(s["g_proj"], 1)
                    for t in range(T):
                        last = mm(bank[3][:, t * P:(t + 1) * P], xT[:, t * P:(t + 1) * P], w["gwv"][:])
                    last.then_inc(s["g_proj"], 1)
                    pe.wait_ge(s["g_h1"], at("g_h1", 1))
                    for t in range(T):
                        last = mm(bank[5][:, t * P:(t + 1) * P], h1T[:, t * P:(t + 1) * P], w["gwg2"][:])
                    last.then_inc(s["gg_p"], 1)
                    for lv in range(LEVELS + 1):
                        pe.wait_ge(s["lv_in"], at("lv_in", lv + 1))
                        if lv >= 2:
                            pe.wait_ge(s["lv_out"], at("lv_out", lv - 1))
                        q, k = (qc, kc) if lv == 0 else (q_lv[lv % 2], k_lv[lv % 2])
                        if lv <= IN_TILE:
                            blocks = [(c * P, c * P, P, c * P) for c in range(T)]
                        elif lv == IN_TILE + 1:
                            blocks = [(0, P, P, 0), (2 * P, 3 * P, P, P)]
                        else:
                            blocks = [(0, 2 * P, 2 * P, 0), (P, 2 * P, 2 * P, 2 * P)]
                        for j0, i0, n, o in blocks:
                            for c in range(2):
                                last = mm(bank[6 + lv % 2][:, o:o + n], k[:, c, j0:j0 + P], q[:, c, i0:i0 + n], c == 0, c == 1)
                        last.then_inc(s["lv_mm"], 1)
                    pe.wait_ge(s["lv_out"], at("lv_out", LEVELS + 1))
                    pe.wait_ge(s["g_v"], at("g_v", 1))
                    for i in range(T):
                        for j in range(i + 1):
                            if i == j:
                                a = at_diag[:, i * P:(i + 1) * P]
                            elif i // 2 == j // 2:
                                a = at_near[:, (i // 2) * P:(i // 2 + 1) * P]
                            else:
                                a = at_far[:, 2 * P * j + (i - 2) * P:2 * P * j + (i - 1) * P]
                            last = mm(bank[4][:, i * P:(i + 1) * P], a, v_tok[:, j * P:(j + 1) * P], j == 0, j == i)
                    last.then_inc(s["g_o"], 1)
                    pe.wait_ge(s["gn"], at("gn", 1))
                    turn_tiles(bank[MISC], lambda t: wide[:, 3, t * P:(t + 1) * P]).then_inc(s["gn_t"], 1)
                    pe.wait_ge(s["gn_sb"], at("gn_sb", 1))
                    for t in range(T):
                        last = mm(bank[0][:, t * P:(t + 1) * P], wide[:, 0, t * P:(t + 1) * P], w["gwo"][:])
                    last.then_inc(s["gla_p"], 1)
                    turn_x(3, 4)

                if upto >= 4:
                    pe.wait_ge(s["ln_sb"], at("ln_sb", 3))
                    for t in range(T):
                        last = mm(bank[5][:, t * EM:(t + 1) * EM], xT[:, t * P:(t + 1) * P], w["wr"][:])
                    last.then_inc(s["r_p"], 1)

                    def relu_done(i):
                        name = "relu_v" if i % 2 else "relu_a"
                        return (s["relu_v"] if i % 2 else s["relu_a"]), at(name, i // 2 + 1)

                    def up(i):
                        if i >= 3:
                            pe.wait_ge(*relu_done(i - 3))
                        mm(bank[i % 3][:], w["w1"][:, i // HC, (i % HC) * P:(i % HC + 1) * P], xT[:]).then_inc(s["w1"], 1)

                    pe.wait_ge(s["mw_in"], at("mw_in", 32))
                    up(0)
                    up(1)
                    for i in range(EM * HC):
                        e, c = i // HC, i % HC
                        if i + 2 < EM * HC:
                            up(i + 2)
                        pe.wait_ge(*relu_done(i))
                        if c == 0 and e >= 2:
                            pe.wait_ge(s["oe_b"], at("oe_b", e - 1))
                        mm(bank[PROB0 + e % 2][:], w["w2"][:, i, :], probs[:, i % RING, :], c == 0, c == HC - 1).then_inc(s["w2"], 1)
                        if c == 1:
                            if e == 0:
                                pe.wait_ge(s["r_done"], at("r_done", 1))
                                for t in range(T):
                                    last = pe.transpose(bank[5][0:2 * EM, t * P:(t + 1) * P],
                                                        r_tok[:, t].rearrange("p a c -> p (a c)").bitcast(F32), w["ident"][:])
                                last.then_inc(s["r_t"], 1)
                        if c == 3:
                            if e == 0:
                                pe.wait_ge(s["r_sb"], at("r_sb", 1))
                            if e >= 2:
                                pe.wait_ge(s["moe_mul"], at("moe_mul", e - 1))
                            mm(bank[6 + e % 2][:], pick_e[:, e:e + 1].to_broadcast([PAD, P]), rT[:]).then_inc(s["rb"], 1)
                    pe.wait_ge(s["moe_acc"], at("moe_acc", 1))
                    turn_tiles(bank[5], lambda t: wide[:, 2, t * P:(t + 1) * P]).then_inc(s["mo_t"], 1)

        @block.scalar
        def _(act):
            act.wait_ge(loaded, 16 * n_loads[0])
            act.wait_ge(const_ready, CONSTS)
            with act.Fori(0, NB) as b:
                at = lambda name, n: b * PER[name] + n

                def rstd_rows(n):
                    act.wait_ge(s["ln_var"], at("ln_var", n))
                    act.activation(ln_r[:, 0, :], ln_mv[:, :, 1], ACT.Ln, bias=eps[:, 1:2]).then_inc(s["ln_rs"], 1)
                    act.wait_ge(s["ln_rs"], at("ln_rs", 2 * n - 1))
                    act.activation(ln_r[:, 1, :], ln_r[:, 0, :], ACT.Exp, scale=-0.5).then_inc(s["ln_rs"], 1)

                act.wait_ge(s["proj"], at("proj", 1))
                act.activation(wide[:, 0, :], bank[0][:], ACT.Identity, bias=w["cols"][:, 0:1]).then_inc(s["lin"], 1)
                act.activation(wide[:, 2, :], bank[0][:], ACT.Square, bias=w["cols"][:, 0:1]).then_inc(s["lin"], 1)
                act.wait_ge(s["proj"], at("proj", 2))
                act.activation(wide[:, 1, :], bank[1][:], ACT.Identity, bias=w["cols"][:, 1:2]).then_inc(s["lin"], 1)
                act.activation(wide[:, 3, :], bank[1][:], ACT.Square, bias=w["cols"][:, 1:2]).then_inc(s["lin"], 1)
                for n in range(2):
                    act.wait_ge(s["msq"], at("msq", n + 1))
                    act.activation(wide[:, 4, :] if n == 0 else wide[:, 5, :], bank[3 + n][:], ACT.Ln, bias=eps[:, 0:1], scale=1.0 / D).then_inc(s["rs"], 1)
                for n in range(2):
                    act.wait_ge(s["rs"], at("rs", 2))
                    act.activation(wide[:, 2 + n, :], wide[:, 4 + n, :], ACT.Exp, scale=-0.5).then_inc(s["rs"], 1)
                for j in range(H0 * T):
                    act.wait_ge(s["st_out"], at("st_out", j + 1))
                    if j >= RING:
                        act.wait_ge(s["pv"], at("pv", j - RING + 1))
                    act.activation(probs[:, j % RING, :], bank[PROB0 + j % 3][:], ACT.Exp).then_inc(s["st_exp"], 1)
                act.wait_ge(s["at_t"], at("at_t", 1))
                act.activation(wide[:, 0, :], bank[MISC][:], ACT.Copy).then_inc(s["at_sb"], 1)
                rstd_rows(1)
                act.wait_ge(s["ln_t"], at("ln_t", 1))
                act.activation(xT[:], bank[MISC][:], ACT.Copy).then_inc(s["ln_sb"], 1)


                if upto >= 2:
                    act.wait_ge(s["gate_p"], at("gate_p", 1))
                    act.activation(gs[:, 0, :], bank[3][:, 0:T * HE], ACT.Exp, scale=-1.0).then_inc(s["gate_e"], 1)
                    for half in range(2):
                        for i in range(2 * HALF):
                            n = 2 * HALF * half + i
                            act.wait_ge(s["fp"], at("fp", n + 1))
                            if i % 2 == 0:
                                act.activation(f_q[:, i // 2], bank[n % 2][:], ACT.Copy, scale=float(FD) ** -0.5).then_inc(s["fp_hi"], 1)
                            else:
                                act.activation(f_k[:, i // 2, 0], bank[n % 2][:], ACT.Copy).then_inc(s["fp_hi"], 1)
                        if half == 0:
                            act.wait_ge(s["gm_t"], at("gm_t", 1))
                            act.activation(gmT[:], bank[MISC][:], ACT.Copy).then_inc(s["gm_sb"], 1)
                            for t in range(T):
                                act.wait_ge(s["ve"], at("ve", t * EF + 1))
                                act.activation(vals[:, t, :, 0:FD], bank[PROB0 + (t * EF) % 3][:].rearrange("p (h k) -> p h k", h=HF),
                                               ACT.Copy).then_inc(s["ve_first"], 1)
                        act.wait_ge(s["fm_t"], at("fm_t", half + 1))
                        act.activation(fmT[0:PARTS * HALF, :], bank[MISC][:].bitcast(BF16)[0:PARTS * HALF, 0:S], ACT.Copy).then_inc(s["fm_sb"], 1)

                        def copy_up(h):
                            act.wait_ge(s["fo_lo"], at("fo_lo", h + 1))
                            act.activation(wide[FD:P, 3 + h % 2, :], wide[0:FD, 3 + h % 2, :], ACT.Copy).then_inc(s["fo_hi"], 1)

                        for h in range(HALF * half, HALF * (half + 1)):
                            for kt in range(T):
                                j = h * T + kt
                                act.wait_ge(s["fst"], at("fst", j + 1))
                                if j >= RING:
                                    act.wait_ge(s["fpv"], at("fpv", j - RING + 1))
                                n = S - kt * P
                                act.activation(probs[:, j % RING, 0:n], bank[PROB0 + j % 3][:, 0:n], ACT.Exp).then_inc(s["fst_exp"], 1)
                            if h % HALF:
                                copy_up(h - 1)
                        copy_up(HALF * half + HALF - 1)
                    act.wait_ge(s["oe"], at("oe", HF * PAIRS))
                    act.activation(wide[:, 5, :], bank[2][:], ACT.Copy).then_inc(s["fo_sb"], 1)
                    rstd_rows(2)
                    act.wait_ge(s["ln_t"], at("ln_t", 2))
                    act.activation(xT[:], bank[MISC][:], ACT.Copy).then_inc(s["ln_sb"], 1)

                if upto >= 3:
                    for n in range(2):
                        act.wait_ge(s["g_proj"], at("g_proj", n + 1))
                        act.activation(probs[:, n, :], bank[n][:], ACT.Exp, scale=-1.0).then_inc(s["g_exp"], 1)
                    act.wait_ge(s["g_proj"], at("g_proj", 3))
                    act.activation(h1T, bank[2][:], ACT.Copy).then_inc(s["g_h1"], 1)
                    act.wait_ge(s["g_proj"], at("g_proj", 4))
                    act.activation(v_tok, bank[3][:], ACT.Copy).then_inc(s["g_v"], 1)
                    act.wait_ge(s["gg_p"], at("gg_p", 1))
                    act.activation(wide[:, 3, :], bank[5][:], ACT.Exp, scale=-1.0).then_inc(s["gg_e"], 1)
                    rstd_rows(3)
                    act.wait_ge(s["gn_t"], at("gn_t", 1))
                    act.activation(wide[:, 0, :], bank[MISC][:], ACT.Copy).then_inc(s["gn_sb"], 1)
                    rstd_rows(4)
                    act.wait_ge(s["ln_t"], at("ln_t", 3))
                    act.activation(xT[:], bank[MISC][:], ACT.Copy).then_inc(s["ln_sb"], 1)

                if upto >= 4:
                    def out_bias(e):
                        act.wait_ge(s["w2"], at("w2", HC * (e + 1)))
                        if e >= 2:
                            act.wait_ge(s["moe_mul"], at("moe_mul", e - 1))
                        act.activation(wide[:, e % 2, :], bank[PROB0 + e % 2][:], ACT.Identity, bias=w["b2c"][:, e:e + 1]).then_inc(s["oe_b"], 1)

                    for e in range(EM):
                        for i in (HC * e, HC * e + 2):
                            act.wait_ge(s["w1"], at("w1", i + 1))
                            if i >= RING:
                                act.wait_ge(s["w2"], at("w2", i - RING + 1))
                            act.activation(probs[:, i % RING, :], bank[i % 3][:], ACT.Relu, bias=w["b1c"][:, i:i + 1]).then_inc(s["relu_a"], 1)
                            if i == 0:
                                act.wait_ge(s["r_m"], at("r_m", 1))
                                act.activation(rt[:, 1], rt[:, 0], ACT.Exp).then_inc(s["r_e"], 1)
                        if e == 0:
                            act.wait_ge(s["r_t"], at("r_t", 1))
                            act.activation(rT[0:2 * EM, :], bank[5][0:2 * EM, :], ACT.Copy).then_inc(s["r_sb"], 1)
                        if e:
                            out_bias(e - 1)
                    out_bias(EM - 1)
                    rstd_rows(5)

        @block.vector
        def _(dve):
            dve.wait_ge(loaded, 16 * n_loads[0])
            dve.tensor_copy(ident_b[:], w["ident"][:]).then_inc(const_ready, 1)
            dve.tensor_scalar(q_scale[:], w["cols"][:, 2:3], float(HD) ** -0.5, None, ALU.mult).then_inc(const_ready, 1)
            dve.tensor_copy(pick_wide[:].rearrange("p (r k) -> p r k", k=FD),
                            w["picks"][:, 0:HE].unsqueeze(2).to_broadcast([P, HE, FD])).then_inc(const_ready, 1)
            dve.tensor_copy(pick_e[:], w["picks"][0:PAD, HE:HE + EM]).then_inc(const_ready, 1)
            dve.tensor_copy(pick_h[:], w["picks"][0:PAD, HE + EM:]).then_inc(const_ready, 1)
            dve.wait_ge(const_ready, CONSTS)
            with dve.Fori(0, NB) as b:
                at = lambda name, n: b * PER[name] + n
                chain = [0]

                def link(ins_):
                    chain[0] += 1
                    ins_.then_inc(dve_step, 1)
                    dve.wait_ge(dve_step, b * dve_steps + chain[0])

                def layer_norm(n, into, scale_row=None):
                    for t in range(T):
                        link(dve.bn_stats(ln_st[:, t, :], y[:, t, :]))
                    dve.sem_inc(passed, 1)
                    for t in range(T):
                        last = dve.bn_aggr(ln_mv[:, t, :], ln_st[:, t, :])
                    last.then_inc(s["ln_var"], 1)
                    dve.wait_ge(s["ln_rs"], at("ln_rs", 2 * n))
                    for t in range(T):
                        last = dve.tensor_scalar(into[:, t, :], y[:, t, :], ln_mv[:, t, 0:1], ln_r[:, 1, t:t + 1],
                                                 ALU.subtract, ALU.mult)
                    last.then_inc(s["ln_out"], 1)
                    dve.wait_ge(s["ln_out"], at("ln_out", n))

                dve.wait_ge(s["proj"], at("proj", 3))
                for t in range(T):
                    dve.tensor_tensor(vaug[:, t, :, 0:HD], bank[2][:, t * P:(t + 1) * P].rearrange("p (h d) -> p h d", d=HD),
                                      w["bv_row"][:].rearrange("p (h d) -> p h d", d=HD), ALU.add).then_inc(s["vaug"], 1)
                for n in range(2):
                    dve.wait_ge(s["rs"], at("rs", 3 + n))
                    nrm, rest_ = wide[:, 4 + n, :], wide[:, 2 + n, :]
                    link(dve.scalar_tensor_tensor(nrm, wide[:, n, :], q_scale[:, 0:1] if n == 0 else w["cols"][:, 3:4],
                                                  wide[:, 2 + n, :], ALU.mult, ALU.mult))
                    link(dve.tensor_copy(parts[:, n, 0, :], nrm))
                    link(dve.tensor_tensor(rest_, nrm, parts[:, n, 0, :], ALU.subtract))
                    link(dve.tensor_copy(parts[:, n, 1, :], rest_))
                    dve.tensor_tensor(parts[:, n, 2, :], rest_, parts[:, n, 1, :], ALU.subtract).then_inc(s["qk_split"], 1)

                def take_max(g):
                    for i in range(GROUP * T * g, GROUP * T * (g + 1)):
                        dve.wait_ge(s["s_out"], at("s_out", i + 1))
                        dve.tensor_reduce(m_tok[:, i:i + 1], bank[SCORE0 + i % 3][:], AX.X, ALU.max).then_inc(s["s_max"], 1)

                def split_max(g):
                    dve.wait_ge(s["m_t"], at("m_t", g + 1))
                    src, k = bank[MISC][0:GROUP * T, 0:P], GROUP * T
                    link(dve.tensor_scalar(m_row[:, g, 0, :], src, -1.0, None, ALU.mult))
                    link(dve.scalar_tensor_tensor(m_rest[0:k, 0, :], src, -1.0, m_row[:, g, 0, :], ALU.mult, ALU.subtract))
                    link(dve.tensor_copy(m_row[:, g, 1, :], m_rest[0:k, 0, :]))
                    dve.tensor_tensor(m_row[:, g, 2, :], m_rest[0:k, 0, :], m_row[:, g, 1, :], ALU.subtract).then_inc(s["m_rows"], 1)

                def take_out(g):
                    dve.wait_ge(s["pv"], at("pv", GROUP * T * (g + 1)))
                    if g >= 2:
                        dve.wait_ge(s["o_t"], at("o_t", g - 1))
                    dve.tensor_copy(wide[:, 4 + g % 2, :], bank[ACC][:]).then_inc(s["o_sb"], 1)

                def norm_out(g):
                    dve.wait_ge(s["o_t"], at("o_t", g + 1))
                    v = bank[MISC][:].rearrange("p (t h c) -> p t h c", t=T, c=VW)
                    rec = m_rest[:, 1, 0:GROUP * T].rearrange("p (t h) -> p t h", t=T)
                    link(dve.reciprocal(rec, v[:, :, :, HD]))
                    dve.tensor_tensor(x_next[:, :, g * 32:(g + 1) * 32].rearrange("p t (h d) -> p t h d", d=HD),
                                      v[:, :, :, 0:HD], rec.unsqueeze(3).to_broadcast([P, T, GROUP, HD]),
                                      ALU.mult).then_inc(s["o_norm"], 1)

                take_max(0)
                split_max(0)
                for g in range(GROUPS):
                    if g + 1 < GROUPS:
                        take_max(g + 1)
                        split_max(g + 1)
                    take_out(g)
                    norm_out(g)
                dve.wait_ge(s["attn_y"], at("attn_y", 1))
                dve.wait_ge(s["xb"], at("xb", 1))
                link(dve.tensor_tensor(y[:].rearrange("p t d -> p (t d)"), bank[0][:], y[:].rearrange("p t d -> p (t d)"), ALU.add))
                layer_norm(1, x_next)

                flat_y = y[:].rearrange("p t d -> p (t d)")
                flat_x = x_next[:].rearrange("p t d -> p (t d)")

                def first_max(src, top, eq, cand, top2, onehot):
                    n = src.shape[1]
                    wide_ = lambda a: a.unsqueeze(2).to_broadcast([P, n, EF])
                    link(dve.tensor_reduce(top, src, AX.X, ALU.max))
                    link(dve.tensor_tensor(eq, src, wide_(top), ALU.is_equal))
                    link(dve.tensor_tensor(cand, eq, w["ramp"][:].unsqueeze(1).to_broadcast([P, n, EF]), ALU.mult))
                    link(dve.tensor_reduce(top2, cand, AX.X, ALU.max))
                    link(dve.tensor_tensor(onehot, cand, wide_(top2), ALU.is_equal))

                if upto >= 2:
                    dve.wait_ge(s["gate_e"], at("gate_e", 1))
                    g3 = lambda i: gs[:, i, :].rearrange("p (n e) -> p n e", e=EF)
                    link(dve.tensor_scalar(gs[:, 1, :], gs[:, 0, :], 1.0, None, ALU.add))
                    link(dve.reciprocal(gs[:, 2, :], gs[:, 1, :]))
                    first_max(g3(2), gsm[:, 0, :], g3(1), g3(0), gsm[:, 1, :], oh[:])
                    link(dve.tensor_tensor(gs[:, 1, :], gs[:, 2, :], oh[:].rearrange("p n e -> p (n e)"), ALU.mult))
                    gsrc = gs[:, 1, :].rearrange("p (t c) -> p t c", t=T)
                    link(dve.tensor_copy(gm_tok[:, :, 0, :], gsrc))
                    dve.tensor_tensor(gm_tok[:, :, 1, :], gsrc, gm_tok[:, :, 0, :].bitcast(F32), ALU.subtract).then_inc(s["gate_done"], 1)
                    for half in range(2):
                        for i in range(2 * HALF):
                            n = 2 * HALF * half + i
                            dve.wait_ge(s["fp_hi"], at("fp_hi", n + 1))
                            if i % 2 == 0:
                                hi = f_q[FD:P, i // 2]
                                dve.scalar_tensor_tensor(hi, bank[n % 2][FD:P, :], float(FD) ** -0.5, hi.bitcast(F32),
                                                         ALU.mult, ALU.subtract).then_inc(s["fp_lo"], 1)
                            else:
                                dve.tensor_tensor(f_k[:, i // 2, 1], bank[n % 2][:], f_k[:, i // 2, 0].bitcast(F32),
                                                  ALU.subtract).then_inc(s["fp_lo"], 1)
                        for i in range(HALF * T * half, HALF * T * (half + 1)):
                            h, t = i // T, i % T
                            n = (t + 1) * P
                            dve.wait_ge(s["fs"], at("fs", i + 1))
                            if i >= 2:
                                dve.wait_ge(s["fs_max"], at("fs_max", i - 1))
                            dve.sem_inc(passed, 1)
                            dve.tensor_tensor_reduce(wide[:, i % 2, 0:n], bank[i % 2][:, 0:n], w["cut_row"][:, S - n:S], 1.0, -3.4e38,
                                                     ALU.add, ALU.max, fm_tok[:, t, h:h + 1]).then_inc(s["fs_max"], 1)
                        dve.wait_ge(s["fs_max"], at("fs_max", HALF * T * (half + 1)))
                        if half:
                            dve.wait_ge(s["fm_t"], at("fm_t", 1))
                        m = fm_tok[:, :, HALF * half:HALF * (half + 1)]
                        link(dve.tensor_scalar(fm_parts[:, :, 0, :], m, -1.0, None, ALU.mult))
                        link(dve.scalar_tensor_tensor(fm_rest[:], m, -1.0, fm_parts[:, :, 0, :], ALU.mult, ALU.subtract))
                        link(dve.tensor_copy(fm_parts[:, :, 1, :], fm_rest[:]))
                        dve.tensor_tensor(fm_parts[:, :, 2, :], fm_rest[:], fm_parts[:, :, 1, :], ALU.subtract).then_inc(s["fm_cut"], 1)
                        if half == 0:
                            for i in range(T * EF):
                                t, e = i // EF, i % EF
                                v = vals[:, t, :, 0:FD]
                                heads = slice(t * HF, (t + 1) * HF)
                                if e == 0:
                                    dve.wait_ge(s["ve_first"], at("ve_first", t + 1))
                                else:
                                    done = t * (EF - 1) + e
                                    dve.wait_ge(s["ve"], at("ve", i + 1))
                                    dve.sem_inc(passed, 1)
                                    dve.copy_predicated(v, oh[:, heads, e].bitcast(U32).unsqueeze(2).to_broadcast([P, HF, FD]),
                                                        bank[PROB0 + i % 3][:].rearrange("p (h k) -> p h k", h=HF)).then_inc(s["ve_sel"], 1)
                                    dve.wait_ge(s["ve_sel"], at("ve_sel", done))
                                if e == EF - 1:
                                    dve.tensor_tensor(v, v, gsm[:, 0, heads].unsqueeze(2).to_broadcast([P, HF, FD]), ALU.mult).then_inc(s["vals_in"], 1)

                        def f_norm(h):
                            dve.wait_ge(s["fpv"], at("fpv", T * (h + 1)))
                            if h >= 2:
                                dve.wait_ge(s["g_in"], at("g_in", PAIRS * (h - 1)))
                            link(dve.reciprocal(wide[0:FD, 2, :], bank[7 - h % 2][FD:P, :]))
                            dve.tensor_tensor(wide[0:FD, 3 + h % 2, :], bank[7 - h % 2][0:FD, :], wide[0:FD, 2, :], ALU.mult).then_inc(s["fo_lo"], 1)
                            dve.wait_ge(s["fo_lo"], at("fo_lo", h + 1))

                        def f_gate(h):
                            dve.wait_ge(s["fo_hi"], at("fo_hi", h + 1))
                            for pr in range(PAIRS):
                                c = h * PAIRS + pr
                                dve.wait_ge(s["mask"], at("mask", c + 1))
                                if c >= 2:
                                    dve.wait_ge(s["oe"], at("oe", c - 1))
                                dve.tensor_tensor(wide[:, c % 2, :], bank[c % 2][:], wide[:, 3 + h % 2, :], ALU.mult).then_inc(s["g_in"], 1)

                        for h in range(HALF * half, HALF * (half + 1)):
                            if h % HALF:
                                f_gate(h - 1)
                            f_norm(h)
                        f_gate(HALF * half + HALF - 1)
                    dve.wait_ge(s["fo_t"], at("fo_t", 1))
                    link(dve.tensor_tensor(flat_y, bank[MISC][:], flat_x, ALU.add))
                    layer_norm(2, x_next)

                if upto >= 3:
                    p_ = lambda i: probs[:, i, :]
                    dve.wait_ge(s["g_exp"], at("g_exp", 1))
                    link(dve.tensor_scalar(p_(0), p_(0), 1.0, None, ALU.add))
                    link(dve.reciprocal(p_(2), p_(0)))
                    link(dve.scalar_tensor_tensor(p_(3), p_(2), float(2 * D) ** -0.5, bank[0][:], ALU.mult, ALU.mult))
                    dve.wait_ge(s["g_exp"], at("g_exp", 2))
                    link(dve.tensor_scalar(p_(1), p_(1), 1.0, None, ALU.add))
                    link(dve.reciprocal(p_(4), p_(1)))
                    link(dve.tensor_scalar(pre, p_(4), -1.0, 1.0, ALU.mult, ALU.add))
                    link(dve.memset(suf, 1.0))
                    link(dve.tensor_scalar(p_(0), pre, 0.5, None, ALU.is_gt))
                    link(dve.tensor_scalar(p_(1), pre, 0.5, None, ALU.is_lt))
                    link(dve.tensor_tensor(p_(5), p_(0), p_(1), ALU.subtract))
                    link(dve.tensor_tensor_scan(p_(6), suf, p_(5), 0.0, ALU.mult, ALU.add))
                    link(dve.tensor_tensor(p_(0), p_(5), p_(5), ALU.mult))
                    link(dve.tensor_scalar(p_(1), p_(0), -2.0, 1.0, ALU.mult, ALU.add))
                    link(dve.tensor_tensor_scan(p_(7), p_(1), suf, 1.0, ALU.mult, ALU.mult))
                    link(dve.tensor_scalar(p_(0), p_(6), PI, None, ALU.mult))
                    link(dve.scalar_tensor_tensor(p_(2), p_(6), -PI1, p_(0), ALU.mult, ALU.add))
                    link(dve.scalar_tensor_tensor(p_(0), p_(6), -PI2, p_(2), ALU.mult, ALU.add))
                    link(dve.scalar_tensor_tensor(p_(2), p_(6), -PI3, p_(0), ALU.mult, ALU.add))
                    link(dve.tensor_tensor(p_(0), p_(2), p_(2), ALU.mult))
                    link(dve.tensor_scalar(p_(1), p_(0), -1.0 / 6, 1.0, ALU.mult, ALU.add))
                    link(dve.tensor_tensor(p_(5), p_(1), p_(2), ALU.mult))
                    link(dve.tensor_scalar(p_(6), p_(0), -0.5, 1.0, ALU.mult, ALU.add))
                    sin_cos = probs[:, 0:2, :]
                    link(dve.tensor_tensor(p_(0), p_(6), p_(7), ALU.mult))
                    link(dve.tensor_tensor(p_(1), p_(5), p_(7), ALU.mult))
                    twice = lambda a: a.unsqueeze(1).to_broadcast([P, 2, S])
                    link(dve.tensor_tensor(qc, sin_cos, twice(p_(3)), ALU.mult))
                    dve.tensor_tensor(kc, sin_cos, twice(p_(4)), ALU.mult).then_inc(s["lv_in"], 1)
                    dve.wait_ge(s["lv_in"], at("lv_in", 1))

                    def take_level(lv):
                        dve.wait_ge(s["lv_mm"], at("lv_mm", lv + 1))
                        src = bank[6 + lv % 2]
                        mask = w["level_mask"][:, min(lv, IN_TILE), :].unsqueeze(1).to_broadcast([P, T, P])
                        four = lambda a: a.rearrange("p (c i) -> p c i", c=T)
                        if lv == 0:
                            ins_ = dve.tensor_tensor(four(at_diag), four(src[:]), mask, ALU.mult)
                        elif lv <= IN_TILE:
                            dve.sem_inc(passed, 1)
                            ins_ = dve.copy_predicated(four(at_diag), mask.bitcast(U32), four(src[:]))
                        elif lv == IN_TILE + 1:
                            ins_ = dve.tensor_copy(at_near, src[:, 0:2 * P])
                        else:
                            ins_ = dve.tensor_copy(at_far, src[:])
                        ins_.then_inc(s["lv_out"], 1)

                    for lv in range(1, LEVELS + 1):
                        hs = 1 << (lv - 1)
                        halves = lambda a: a.rearrange("p (n two i) -> p n two i", two=2, i=hs)
                        n = S // (2 * hs)
                        if lv >= 3:
                            dve.wait_ge(s["lv_mm"], at("lv_mm", lv - 1))
                        for c in range(2):
                            link(dve.tensor_tensor(halves(q_lv[lv % 2][:, c])[:, :, 1], halves(qc[:, c])[:, :, 1],
                                                   halves(pre)[:, :, 1], ALU.mult))
                        link(dve.tensor_tensor(halves(k_lv[lv % 2][:, 0])[:, :, 0], halves(kc[:, 0])[:, :, 0],
                                               halves(suf)[:, :, 0], ALU.mult))
                        dve.tensor_tensor(halves(k_lv[lv % 2][:, 1])[:, :, 0], halves(kc[:, 1])[:, :, 0],
                                          halves(suf)[:, :, 0], ALU.mult).then_inc(s["lv_in"], 1)
                        if lv < LEVELS:
                            link(dve.tensor_tensor(halves(suf)[:, :, 0], halves(suf)[:, :, 0],
                                                   halves(pre)[:, :, 1, hs - 1:hs].to_broadcast([P, n, hs]), ALU.mult))
                            link(dve.tensor_tensor(halves(pre)[:, :, 1], halves(pre)[:, :, 1],
                                                   halves(pre)[:, :, 0, hs - 1:hs].to_broadcast([P, n, hs]), ALU.mult))
                        if lv >= 2:
                            dve.wait_ge(s["lv_out"], at("lv_out", lv - 1))
                        take_level(lv - 1)
                    take_level(LEVELS)
                    dve.wait_ge(s["gg_e"], at("gg_e", 1))
                    link(dve.tensor_scalar(wide[:, 2, :], wide[:, 3, :], 1.0, None, ALU.add))
                    link(dve.reciprocal(wide[:, 3, :], wide[:, 2, :]))
                    dve.wait_ge(s["g_o"], at("g_o", 1))
                    link(dve.tensor_tensor(flat_y, bank[4][:], wide[:, 3, :], ALU.mult))
                    layer_norm(3, wide[:, 2, :].rearrange("p (t d) -> p t d", t=T))
                    dve.tensor_tensor(wide[:, 3, :].rearrange("p (t d) -> p t d", t=T), wide[:, 2, :].rearrange("p (t d) -> p t d", t=T),
                                      w["gn_row"][:].unsqueeze(1).to_broadcast([P, T, P]), ALU.mult).then_inc(s["gn"], 1)
                    dve.wait_ge(s["gla_p"], at("gla_p", 1))
                    link(dve.tensor_tensor(flat_y, bank[0][:], flat_x, ALU.add))
                    layer_norm(4, x_next)

                if upto >= 4:
                    r = lambda i: rt[:, i]
                    by_tile = lambda a: a.unsqueeze(2).to_broadcast([P, T, EM])
                    dve.wait_ge(s["r_p"], at("r_p", 1))
                    link(dve.tensor_tensor(r(2), bank[5][:, 0:T * EM].rearrange("p (t e) -> p t e", t=T),
                                           w["br_row"][:].unsqueeze(1).to_broadcast([P, T, EM]), ALU.add))
                    link(dve.tensor_reduce(rt1[:, 0, :], r(2), AX.X, ALU.max))
                    dve.tensor_tensor(r(0), r(2), by_tile(rt1[:, 0, :]), ALU.subtract).then_inc(s["r_m"], 1)
                    dve.wait_ge(s["r_e"], at("r_e", 1))
                    link(dve.tensor_reduce(rt1[:, 1, :], r(1), AX.X, ALU.add))
                    link(dve.reciprocal(rt1[:, 2, :], rt1[:, 1, :]))
                    link(dve.tensor_tensor(r(2), r(1), by_tile(rt1[:, 2, :]), ALU.mult))
                    first_max(r(2), rt1[:, 0, :], r(0), r(1), rt1[:, 1, :], r(3))
                    link(dve.scalar_tensor_tensor(r(4), r(3), -2.0, r(2), ALU.mult, ALU.add))
                    first_max(r(4), rt1[:, 0, :], r(0), r(1), rt1[:, 1, :], r(5))
                    link(dve.tensor_tensor(r(0), r(3), r(5), ALU.add))
                    link(dve.tensor_tensor(r(1), r(0), r(2), ALU.mult))
                    link(dve.tensor_reduce(rt1[:, 0, :], r(1), AX.X, ALU.add))
                    link(dve.reciprocal(rt1[:, 1, :], rt1[:, 0, :]))
                    link(dve.tensor_tensor(r(0), r(1), by_tile(rt1[:, 1, :]), ALU.mult))
                    link(dve.tensor_copy(r_tok[:, :, 0, :], r(0)))
                    dve.tensor_tensor(r_tok[:, :, 1, :], r(0), r_tok[:, :, 0, :].bitcast(F32), ALU.subtract).then_inc(s["r_done"], 1)

                    def weigh_expert(e):
                        dve.wait_ge(s["oe_b"], at("oe_b", e + 1))
                        dve.wait_ge(s["rb"], at("rb", e + 1))
                        to = wide[:, 2, :] if e == 0 else wide[:, 3, :]
                        dve.tensor_tensor(to, bank[6 + e % 2][:], wide[:, e % 2, :], ALU.mult).then_inc(s["moe_mul"], 1)
                        dve.wait_ge(s["moe_mul"], at("moe_mul", e + 1))
                        if e:
                            total = dve.tensor_tensor(wide[:, 2, :], wide[:, 2, :], wide[:, 3, :], ALU.add)
                            if e < EM - 1:
                                link(total)
                            else:
                                total.then_inc(s["moe_acc"], 1)

                    for e in range(EM):
                        for i in (HC * e + 1, HC * e + 3):
                            dve.wait_ge(s["w1"], at("w1", i + 1))
                            if i >= RING:
                                dve.wait_ge(s["w2"], at("w2", i - RING + 1))
                            dve.tensor_scalar(probs[:, i % RING, :], bank[i % 3][:], w["b1c"][:, i:i + 1], 0.0,
                                              ALU.add, ALU.max).then_inc(s["relu_v"], 1)
                        if e:
                            weigh_expert(e - 1)
                    weigh_expert(EM - 1)
                    dve.wait_ge(s["mo_t"], at("mo_t", 1))
                    link(dve.tensor_tensor(flat_y, bank[5][:], flat_x, ALU.add))
                    layer_norm(5, x_next)
                if counts is not None:
                    counts.append(chain[0])


n_loads = [0]
CONSTS = 11


def host_constants():
    c = {}
    eye = np.eye(P, dtype=np.float32)
    c["ident"] = eye
    c["ramp"] = np.tile(np.arange(EF, 0, -1, dtype=np.float32), (P, 1))
    picks = np.zeros((P, HE + EM + HALF), np.float32)
    for r in range(P):
        picks[r, r % HE] = 1
        if r < 2 * EM:
            picks[r, HE + r % EM] = 1
        if r < PARTS * HALF:
            picks[r, HE + EM + r % HALF] = 1
    c["picks"] = picks
    cut = np.zeros((P, S), np.float32)
    cut[:, S - P:] = np.where(np.arange(P)[None, :] > np.arange(P)[:, None], np.float32(NEG), np.float32(0))
    c["cut_row"] = cut
    j, i = np.arange(P)[:, None], np.arange(P)[None, :]
    masks = [(j == i)]
    for l in range(IN_TILE):
        hs = 1 << l
        masks.append(((j // (2 * hs)) == (i // (2 * hs))) & ((j // hs) % 2 == 0) & ((i // hs) % 2 == 1))
    c["level_mask"] = np.stack(masks, axis=1).astype(np.float32)
    return c


def laid_out(i):
    C = np.ascontiguousarray
    row = lambda v: C(np.broadcast_to(v, (P, v.shape[0])))
    a = {}
    x = i["L0_attn_x"]
    a["x"], a["xT"] = x, C(x.transpose(0, 2, 1))
    for n, m in (("wq0", "Wq"), ("wk0", "Wk"), ("wv0", "Wv"), ("wo0", "Wo")):
        a[n] = C(i[f"L0_attn_{m}"].T)
    a["bv_row"], a["bo_row"] = row(i["L0_attn_bv"]), row(i["L0_attn_bo"])
    a["cols"] = C(np.stack([i["L0_attn_bq"], i["L0_attn_bk"], i["L0_attn_norm_q_w"], i["L0_attn_norm_k_w"]], axis=1))
    for n, m in (("gwq", "wq"), ("gwk", "wk"), ("gwv", "wv"), ("gwo", "wo"), ("gwg1", "wg1"), ("gwg2", "wg2")):
        a[n] = i[f"L1_attn_{m}"]
    a["gn_row"] = row(i["L1_attn_norm_w"])
    for n, m in (("fwq", "w_q"), ("fwk", "w_k")):
        m = i[f"L0_ffn_{m}"].reshape(D, HF, 1, FD)
        a[n] = C(np.broadcast_to(m, (D, HF, 2, FD)).reshape(D, HF, 2 * FD))
    a["fgate"] = i["L0_ffn_w_gate"]
    a["ve"] = C(i["L0_ffn_value_experts"].transpose(2, 0, 1, 3).reshape(D, EF, HF * FD))
    oe = i["L0_ffn_output_experts"].reshape(PAIRS, 2, HF, FD, D)
    a["oe"] = C(oe.transpose(1, 3, 2, 0, 4).reshape(P, HF * PAIRS, D))
    a["w1"] = C(i["L1_ffn_W1"].transpose(1, 0, 2))
    a["w2"] = C(i["L1_ffn_W2"].reshape(EM * HC, P, D).transpose(1, 0, 2))
    a["b1c"] = C(i["L1_ffn_b1"].reshape(EM * HC, P).T)
    a["b2c"] = C(i["L1_ffn_b2"].T)
    a["wr"], a["br_row"] = i["L1_ffn_Wr"], row(i["L1_ffn_br"])
    a.update(host_constants())
    return a


def kernel(**inputs):
    import concourse.bacc as bacc
    from concourse.bass_utils import run_bass_kernel_spmd as run

    arrays = laid_out({k: np.asarray(v) for k, v in inputs.items()})
    nc = bacc.Bacc("TRN2", target_bir_lowering=False, num_devices=1)
    ins = {n: nc.dram_tensor(n + "_in", a.shape, mybir.dt.from_np(a.dtype), kind="ExternalInput").ap() for n, a in arrays.items()}
    out = nc.dram_tensor("out_dram", (B, S, D), F32, kind="ExternalOutput").ap()
    build(nc, ins, out)
    r = run(nc, [{n + "_in": a for n, a in arrays.items()}], core_ids=[0])
    return r.results[0]["out_dram"]
```

```python
from contextlib import ExitStack

import numpy as np
import concourse.bass as bass
from concourse import mybir

F32, BF16, F32R, U32 = mybir.dt.float32, mybir.dt.bfloat16, mybir.dt.float32r, mybir.dt.uint32
ALU, ACT, AX = mybir.AluOpType, mybir.ActivationFunctionType, mybir.AxisListType

B, S, D = 4, 512, 128
P = 128
T = S // P
H0, HD = 16, 8
GROUP = 4
GROUPS = H0 // GROUP
PARTS = 3
PROD_ROWS = PARTS * PARTS * HD
STACK_ROWS = PROD_ROWS + PARTS
VW = 32
SLOTS = GROUP * T + 2
LEAD = SLOTS + 8
RING_A = 4
HF, FD, EF = 8, 64, 8
HE = HF * EF
HALF = HF // 2
GH = HALF * EF
TILES_H = HALF * T
PAD = 96
PAIRS = EF // 2
OUT_LAG = 8
NEG = -3.0e38
LEVELS = 9
IN_TILE = 7
PI1, PI2, PI3 = 3.140625, 9.67502593994140625e-4, 1.509957990978376e-7
PI = 3.1415927410125732
F_DOWN, F_UP = 1.1e-7, -1.7e-7
EM, HID = 8, 512
HC = HID // P
RING = 4

A0, A1, A2 = 0, 1, 2
B3, B4, B5, B6, B7 = 3, 4, 5, 6, 7

PER = dict(
    ones_in=1, x_in=32, xb=1, proj=3, proj_v=1, lin=4, msq=2, rs=4, qk_split=2, q_scr_out=48, k_scr_out=48, stack_in=16 * 4,
    vaug=4, s_out=H0 * T, s_max=H0 * T, m_t=GROUPS, m_rows=GROUPS, m_out=GROUPS * 16, m_in0=16, m_in1=16, m_in2=16,
    m_in3=16, st_out=H0 * T, st_exp=H0 * T, pv=H0 * T, o_sb=GROUPS, o_t=GROUPS, o_norm=GROUPS, at_t=1, at_sb=1,
    attn_y=1, l0_var=1, l0_rs=2, l0_out=1, l0_turn=1, l0_done=1, l0_link=44,
    fp=2 * HF, fp_hi=2 * HF, fp_lo=2 * HF, gate_p=1, gate_e=1, gate_done=1, gm_t=1, gm_sb=2,
    fs=HF * T, fs_max=HF * T, fm_cut=2, fm_t=2, fm_sb=2, ve=T * EF, ve_first=T, ve_sel=T * (EF - 1), vals_in=T,
    vals_one=1, fst=HF * T, fst_exp=HF * T, fst_cut=HF * T, fpv=HF * T, f_ln=HF, f_rec=HF, fo_lo=HF, fo_hi=HF,
    mask=HF * PAIRS, g_in=HF * PAIRS, oe=HF * PAIRS, fo_sb=1, fo_t=1, ffn_var=1, ffn_rs=2, ffn_out=1, ffn_turn=1,
    ffn_done=1, ffn_link=40,
    g_proj=4, g_exp=2, g_ln=2, g_sig=2, g_v=1, g_h1=1, lv_in=LEVELS + 1, lv_mm=LEVELS + 1, lv_out=LEVELS + 1, g_o=1,
    gg_p=1, gg_e=3, gn=1, gn_t=1, gn_sb=1, gla_p=1, gla_var=2, gla_rs=4, gla_out=2, gla_turn=1, gla_done=1,
    gla_link=80,
    r_p=1, r_m=1, r_e=1, r_done=1, r_t=1, r_sb=1, w1=EM * HC, relu_a=EM * HC // 2, relu_v=EM * HC // 2,
    w2=EM * HC, rb=EM, oe_b=EM, moe_mul=EM, moe_acc=1, mo_t=1, moe_var=1, moe_rs=2, moe_done=1, moe_link=40,
    stored=16,
)
PER_PAIR = dict(ve_in=16, oe_in=16, w1_in=16, w2_in=16)

LN_UNITS = 5
HALF_UNITS = [0.9] * (2 * HALF) + [0.5] + [0.7] * TILES_H + [1, 1.5]
UNIT_TIMES = dict(
    l0=[2, 2, 2, 3, 3, 3, 3, 3, 5, 1] + [0.7] * LEAD + [1.2] * (GROUPS * SLOTS) + [2, 2] + [1] * LN_UNITS,
    ffn=[1] + HALF_UNITS + [0.95] * (T * EF) + [1] + [2.6] * (TILES_H + OUT_LAG + 1)
    + HALF_UNITS + [2.6] * (TILES_H + OUT_LAG + 1) + [1, 1] + [1] * LN_UNITS,
    gla=[2, 1.5, 1.5] + [0.7] * 21 + [2.6] + [0.7, 0.7, 0.7, 2.2] * LEVELS + [1, 2] + [1] * 3 + [1, 1, 1] + [1] * LN_UNITS,
    moe=[1, 1, 1] + [2.0] * (EM * HC) + [1, 1, 1] + [1] * LN_UNITS,
)


def unit_order(a, b):
    order, at = [], dict(a=0.0, b=0.0)
    left = dict(a=list(UNIT_TIMES[a]), b=list(UNIT_TIMES[b]))
    total = {n: sum(u) for n, u in left.items()}
    while left["a"] or left["b"]:
        turn = "a" if left["a"] and (not left["b"] or at["a"] / total["a"] <= at["b"] / total["b"]) else "b"
        order.append(turn)
        at[turn] += left[turn].pop(0)
    return order


def alone(name, stage):
    units = sum(1 for _ in stage)
    assert units == len(UNIT_TIMES[name]), (name, units, len(UNIT_TIMES[name]))


def side_by_side(name_a, stage_a, name_b, stage_b):
    for turn in unit_order(name_a, name_b):
        next(stage_a if turn == "a" else stage_b)
    for name, stage in ((name_a, stage_a), (name_b, stage_b)):
        assert next(stage, None) is None, name


def two_by_two(eng, pairs, l0, ffn, gla, moe):
    alone("l0", l0((0, 0)))
    with eng.Fori(0, pairs) as p:
        side_by_side("l0", l0((p, 1)), "ffn", ffn((p, 0)))
        side_by_side("gla", gla((p, 0)), "ffn", ffn((p, 1)))
        side_by_side("gla", gla((p, 1)), "moe", moe((p, 0)))
        with eng.If(p < pairs - 1):
            side_by_side("l0", l0((0, 2)), "moe", moe((0, 1), refill=True))
    alone("moe", moe((pairs - 1, 1)))


def counter(batch):
    pair, which = batch

    def at(name, n):
        if name in PER_PAIR:
            return pair * PER_PAIR[name] + n
        return pair * (2 * PER[name]) + (which * PER[name] + n)
    return at


def build(nc, ins, out, upto=4, steps=None, counts=None, NB=B):
    nc.disable_value_cache = True
    with ExitStack() as ctx:
        def sb(name, shape, dt=F32):
            return ctx.enter_context(nc.sbuf_tensor(name, shape, dt))

        s = {n: ctx.enter_context(nc.semaphore(n)) for n in [*PER, *PER_PAIR]}
        m_in = [s["m_in0"], s["m_in1"], s["m_in2"], s["m_in3"]]
        loaded = ctx.enter_context(nc.semaphore("loaded"))
        const_ready = ctx.enter_context(nc.semaphore("const_ready"))
        passed = ctx.enter_context(nc.semaphore("passed"))
        class_b_idle = ctx.enter_context(nc.semaphore("class_b_idle"))

        bank = [ctx.enter_context(nc.psum_tensor(f"bank{i}", [P, 512], F32)) for i in range(8)]
        q_scr = nc.dram_tensor("q_scr", (PARTS, HD, H0, S), BF16).ap()
        m_scr = nc.dram_tensor("m_scr", (GROUPS, PARTS, GROUP * T, P), BF16).ap()
        k_scr = nc.dram_tensor("k_scr", (PARTS, HD, H0, S), BF16).ap()

        w = {}
        loads = []

        def weight(name, shape, dt=F32):
            t = sb(name, shape, dt)
            w[name] = t
            loads.append((t, ins[name]))

        for name in ("wq0", "wk0", "wv0", "wo0", "gwq", "gwk", "gwv", "gwg1", "gwg2", "gwo", "ident", "bv_row",
                     "bo_row", "gn_row"):
            weight(name, [P, P])
        weight("cols", [P, 4])
        weight("fwq", [P, HF, P])
        weight("fwk", [P, HF, P])
        weight("fgate", [P, HE])
        weight("b1c", [P, EM * HC])
        weight("b2c", [P, EM])
        weight("wr", [P, EM])
        weight("br_row", [P, EM])
        weight("ramp", [P, EF])
        weight("picks", [P, GH + EM + HALF])
        weight("cut_row", [P, S])
        weight("level_mask", [P, IN_TILE + 1, P])
        pick_wide = sb("pick_wide", [PAD, GH * FD], F32R)
        pick_e = sb("pick_e", [PAD, EM], F32R)
        pick_h = sb("pick_h", [PAD, HALF], BF16)
        ident_b = sb("ident_b", [P, P], BF16)
        ones = sb("ones", [P, P])
        experts = sb("experts", [P, 16 * S])
        w["ve"] = w["w1"] = experts[:, 0:8 * S].rearrange("p (e n) -> p e n", e=EF)
        w["oe"] = w["w2"] = experts[:, 8 * S:].rearrange("p (c n) -> p c n", n=P)
        q_scale = sb("q_scale", [P, 1])
        eps = sb("eps", [P, 2])

        x_tok = sb("x_tok", [P, 2, T, P])
        x_chan = sb("x_chan", [P, 2, S])

        ln_a = dict(st=sb("ln_st_a", [P, T, 6]), mv=sb("ln_mv_a", [P, T, 2]), r=sb("ln_r_a", [P, 2, T]))
        vaug = sb("vaug", [P, T, H0, VW])
        tiles_a = sb("tiles_a", [P, 6, S])
        region = sb("region", [P, 16 * S])
        stack = region[:, :].bitcast(BF16).rearrange("r (n h s) -> r n h s", n=2, h=H0)
        probs_a = sb("probs_a", [P, RING_A, S])
        parts = probs_a[:, 0:PARTS, :].bitcast(BF16).rearrange("p n s -> p (n s)").rearrange("p (n c s) -> p n c s", n=2, c=PARTS)
        m_tok = sb("m_tok", [P, H0 * T])
        m_row = sb("m_row", [GROUP * T, GROUPS, PARTS, P], BF16)
        m_rest = sb("m_rest", [P, 2, P])
        heads_out = tiles_a[:, 0, :].rearrange("p (t d) -> p t d", t=T)
        gla_tiles = region[:].rearrange("p (n s) -> p n s", s=S)
        q_lv, k_lv = (gla_tiles[:, 0:2], gla_tiles[:, 2:4]), (gla_tiles[:, 4:6], gla_tiles[:, 6:8])
        qc, kc, pre, suf, at_diag, v_tok = (gla_tiles[:, 8:10], gla_tiles[:, 10:12], gla_tiles[:, 12], gla_tiles[:, 13],
                                            gla_tiles[:, 14], gla_tiles[:, 15])
        at_far, at_near, h1T = probs_a[:, 0], probs_a[:, 1, 0:2 * P], probs_a[:, 2]

        ln_b = dict(st=sb("ln_st_b", [P, T, 6]), mv=sb("ln_mv_b", [P, T, 2]), r=sb("ln_r_b", [P, 2, T]))
        tiles_b = sb("tiles_b", [P, 6, S])
        probs_b = sb("probs_b", [P, RING, S])
        f_q = sb("f_q", [P, HALF, S], F32R)
        f_k = sb("f_k", [P, HALF, 2, S], F32R)
        vals = sb("vals", [P, T, HF, P])
        gm_tok = sb("gm_tok", [P, T, 2, 2, GH], F32R)
        gmT = sb("gmT", [PAD, 2, S], F32R)
        oh = sb("oh", [P, T * HF, EF])
        gs = tiles_b[:, 3:5].rearrange("p a b -> p (a b)")[:, 0:3 * T * HE].rearrange("p (n c) -> p n c", n=3)
        gsm = sb("gsm", [P, 2, T * HF])
        fm_tok = sb("fm_tok", [P, T, HF])
        fm_parts = sb("fm_parts", [P, T, PARTS, HALF], BF16)
        fm_rest = sb("fm_rest", [P, T, HALF])
        fmT = sb("fmT", [PAD, S], BF16)
        rT = sb("rT", [PAD, S], F32R)
        r_tok = sb("r_tok", [P, T, 2, EM], F32R)
        rt = sb("rt", [P, 6, T, EM])
        rt1 = sb("rt1", [P, 4, T])

        block = ctx.enter_context(nc.Block())

        @block.sync
        def _(sp):
            for t, src in loads:
                sp.dma_start(t[:], src).then_inc(loaded, 16)
            n_loads[0] = len(loads)
            sp.dma_start(experts[:, 0:8 * S], ins["ve"].rearrange("p e n -> p (e n)")).then_inc(s["ve_in"], 16)
            sp.dma_start(experts[:, 8 * S:], ins["oe"].rearrange("p c n -> p (c n)")).then_inc(s["oe_in"], 16)

            def number(batch):
                return batch[0] * 2 + batch[1]

            def l0(batch):
                at, par, b = counter(batch), batch[1] % 2, number(batch)
                src = ins["xT"][bass.ds(b, 1)].rearrange("o p n -> (o p) n")
                sp.dma_start(x_chan[:, par], src).then_inc(s["x_in"], 16)
                src = ins["x"][bass.ds(b, 1)].rearrange("o (t p) d -> p (o t) d", p=P)
                sp.dma_start(x_tok[:, par], src).then_inc(s["x_in"], 16)
                for _ in range(4):
                    yield
                for n, scr in enumerate((q_scr, k_scr)):
                    sp.wait_ge(s["qk_split"], at("qk_split", n + 1))
                    for c in range(PARTS):
                        sp.dma_start(scr[c].rearrange("d h s -> h d s"), parts[:, n, c, :]).then_inc(s["q_scr_out" if n == 0 else "k_scr_out"], 16)
                    yield
                sp.wait_ge(s["q_scr_out"], at("q_scr_out", 48))
                for c in range(PARTS):
                    dst = stack[PARTS * HD * c:PARTS * HD * (c + 1), 0].rearrange("r h s -> r (h s)")
                    src = q_scr[c].rearrange("d h s -> d (h s)").unsqueeze(0).to_broadcast([PARTS, HD, H0 * S])
                    sp.dma_start(dst, src).then_inc(s["stack_in"], 16)
                yield
                sp.wait_ge(s["k_scr_out"], at("k_scr_out", 48))
                sp.wait_ge(s["ones_in"], at("ones_in", 1))
                src = k_scr.rearrange("c d h s -> (c d) (h s)").unsqueeze(0).to_broadcast([PARTS, PARTS * HD, H0 * S])
                sp.dma_start(stack[0:PROD_ROWS, 1].rearrange("r h s -> r (h s)"), src).then_inc(s["stack_in"], 16)
                yield
                for _ in range(2):
                    yield
                for u in range(GROUPS * SLOTS + LEAD):
                    g, i = divmod(u, SLOTS)
                    if i == SLOTS - 1 and g < GROUPS:
                        sp.wait_ge(s["m_rows"], at("m_rows", g + 1))
                        sp.dma_start(m_scr[g].rearrange("c r p -> r c p"), m_row[:, g]).then_inc(s["m_out"], 16)
                    if i == 2 and 0 < g <= GROUPS:
                        g -= 1
                        sp.wait_ge(s["m_out"], at("m_out", 16 * (g + 1)))
                        sp.dma_start(stack[PROD_ROWS:STACK_ROWS, 0, GROUP * g:GROUP * (g + 1), :].rearrange("c h s -> c (h s)"),
                                     m_scr[g].rearrange("c r p -> c (r p)")).then_inc(m_in[g], 16)
                    yield
                for _ in range(2 + LN_UNITS):
                    yield

            def ffn(batch):
                at = counter(batch)
                for u in range(len(UNIT_TIMES["ffn"])):
                    if u == len(UNIT_TIMES["ffn"]) - 4 and batch[1]:
                        sp.wait_ge(s["oe"], at("oe", HF * PAIRS))
                        sp.dma_start(experts[:, 0:8 * S], ins["w1"].rearrange("p e n -> p (e n)")).then_inc(s["w1_in"], 16)
                        sp.dma_start(experts[:, 8 * S:], ins["w2"].rearrange("p c n -> p (c n)")).then_inc(s["w2_in"], 16)
                    yield

            def gla(batch):
                for _ in range(len(UNIT_TIMES["gla"])):
                    yield

            def moe(batch, refill=False):
                at, par, b = counter(batch), batch[1] % 2, number(batch)
                for u in range(len(UNIT_TIMES["moe"]) - 1):
                    if refill and u == len(UNIT_TIMES["moe"]) - 4:
                        sp.wait_ge(s["w2"], at("w2", EM * HC))
                        sp.dma_start(experts[:, 0:8 * S], ins["ve"].rearrange("p e n -> p (e n)")).then_inc(s["ve_in"], 16)
                        sp.dma_start(experts[:, 8 * S:], ins["oe"].rearrange("p c n -> p (c n)")).then_inc(s["oe_in"], 16)
                    yield
                sp.wait_ge(s["moe_done"], at("moe_done", 1))
                dst = out[bass.ds(b, 1)].rearrange("o (t p) d -> p (o t) d", p=P)
                sp.dma_start(dst, x_tok[:, par]).then_inc(s["stored"], 16)
                sp.wait_ge(s["stored"], at("stored", 16))
                sp.sem_inc(passed, 1)
                yield

            two_by_two(sp, NB // 2, l0, ffn, gla, moe)

        def s_bank(u, n):
            return A0 + n % 2 if u < LEAD - 1 else A0

        def class_a_free(eng, stage, batch):
            pair, which = batch
            if stage == "l0":
                if which == 1:
                    eng.wait_ge(s["l0_done"], counter((pair, 0))("l0_done", 1))
                elif which == 2:
                    eng.wait_ge(s["gla_done"], counter((pair, 1))("gla_done", 1))
            elif which == 0:
                eng.wait_ge(s["l0_done"], counter((pair, 1))("l0_done", 1))
                eng.wait_ge(s["ffn_done"], counter((pair, 0))("ffn_done", 1))
            else:
                eng.wait_ge(s["gla_done"], counter((pair, 0))("gla_done", 1))
                eng.wait_ge(s["ffn_done"], counter((pair, 1))("ffn_done", 1))

        def class_b_free(eng, stage, batch):
            pair, which = batch
            if stage == "ffn":
                eng.wait_ge(s["l0_done"], counter(batch)("l0_done", 1))
                if which == 0:
                    eng.wait_ge(class_b_idle, pair + 1)
                else:
                    eng.wait_ge(s["ffn_done"], counter((pair, 0))("ffn_done", 1))
            else:
                eng.wait_ge(s["gla_done"], counter(batch)("gla_done", 1))
                if which == 0:
                    eng.wait_ge(s["ffn_done"], counter((pair, 1))("ffn_done", 1))
                else:
                    eng.wait_ge(s["moe_done"], counter((pair, 0))("moe_done", 1))

        @block.gpsimd
        def _(pool):
            pool.memset(ones[:], 1.0).then_inc(const_ready, 1)
            pool.memset(vaug[:], 1.0).then_inc(const_ready, 1)
            pool.memset(fmT[:], 0.0).then_inc(const_ready, 1)
            pool.memset(rT[:].bitcast(U32), 0).then_inc(const_ready, 1)
            pool.memset(gmT[:].bitcast(U32), 0).then_inc(const_ready, 1)
            pool.memset(eps[:, 0:1], 1e-6).then_inc(const_ready, 1)
            pool.memset(eps[:, 1:2], 1e-5).then_inc(const_ready, 1)
            pool.memset(vals[:, :, :, FD:P], 1.0).then_inc(const_ready, 1)
            pool.wait_ge(const_ready, CONSTS)
            pool.sem_inc(class_b_idle, 1)

            def l0(batch):
                at, par = counter(batch), batch[1] % 2
                class_a_free(pool, "l0", batch)
                pool.sem_inc(passed, 1)
                pool.memset(stack[64:STACK_ROWS, 1], 1.0).then_inc(s["ones_in"], 1)
                pool.wait_ge(s["ones_in"], at("ones_in", 1))
                pool.wait_ge(s["x_in"], at("x_in", 32))
                pool.tensor_tensor(x_tok[:, par], x_tok[:, par], w["bo_row"][:].unsqueeze(1).to_broadcast([P, T, P]), ALU.add).then_inc(s["xb"], 1)
                for _ in range(len(UNIT_TIMES["l0"])):
                    yield

            def ffn(batch):
                at = counter(batch)
                class_b_free(pool, "ffn", batch)
                yield from waits(1 + len(HALF_UNITS) + T * EF + 1)
                for half in range(2):
                    if half:
                        yield from waits(len(HALF_UNITS))
                    for u in range(TILES_H + OUT_LAG + 1):
                        if u < TILES_H:
                            j = TILES_H * half + u
                            pool.wait_ge(s["fst_exp"], at("fst_exp", j + 1))
                            pool.sem_inc(passed, 1)
                            pool.affine_select(out=probs_b[:, j % RING, 0:P], in_=probs_b[:, j % RING, 0:P],
                                               compare_op=ALU.is_ge, fill=0.0, base=0, pattern=[[1, P]],
                                               channel_multiplier=-1).then_inc(s["fst_cut"], 1)
                        yield
                yield from waits(2 + LN_UNITS)

            def gla(batch):
                yield from waits(len(UNIT_TIMES["gla"]))

            def moe(batch, refill=False):
                yield from waits(len(UNIT_TIMES["moe"]))

            two_by_two(pool, NB // 2, l0, ffn, gla, moe)

        @block.tensor
        def _(pe):
            pe.wait_ge(loaded, 16 * n_loads[0])
            pe.wait_ge(const_ready, CONSTS)

            def mm(o, l, r, start=True, stop=True):
                return pe.matmul(o, lhsT=l, rhs=r, start=start, stop=stop, skip_group_check=True)

            def turn_tiles(dst, src):
                for t in range(T):
                    last = pe.transpose(dst[:, t * P:(t + 1) * P], src(t), w["ident"][:])
                return last

            def l0(batch):
                at, par = counter(batch), batch[1] % 2
                xT = x_chan[:, par]
                class_a_free(pe, "l0", batch)
                pe.wait_ge(s["x_in"], at("x_in", 32))
                mm(bank[A0][:], w["wq0"][:], xT).then_inc(s["proj"], 1)
                mm(bank[A1][:], w["wk0"][:], xT).then_inc(s["proj"], 1)
                yield
                for t in range(T):
                    last = mm(bank[A2][:, t * P:(t + 1) * P], xT[:, t * P:(t + 1) * P], w["wv0"][:])
                last.then_inc(s["proj"], 1)
                yield
                for n in range(2):
                    pe.wait_ge(s["lin"], at("lin", 2 * n + 2))
                    mm(bank[A0 + n][:], ones[:], tiles_a[:, 2 + n, :]).then_inc(s["msq"], 1)
                    yield
                yield from waits(5)
                pe.wait_ge(s["stack_in"], at("stack_in", 64))
                pe.wait_ge(s["vaug"], at("vaug", 4))
                pe.wait_ge(s["rs"], at("rs", 2))
                yield
                for u in range(LEAD + GROUPS * SLOTS):
                    g, i = divmod(u, SLOTS)
                    if g < GROUPS and i < GROUP * T:
                        n = g * GROUP * T + i
                        h, t = divmod(n, T)
                        seen = n - 1 if u < LEAD - 1 else n
                        if seen > 0:
                            pe.wait_ge(s["s_max"], at("s_max", seen))
                        if i == 0 and g:
                            pe.wait_ge(s["m_rows"], at("m_rows", g))
                        mm(bank[s_bank(u, n)][:], stack[0:PROD_ROWS, 0, h, t * P:(t + 1) * P],
                           stack[0:PROD_ROWS, 1, h, :]).then_inc(s["s_out"], 1)
                    elif g < GROUPS and i == GROUP * T:
                        pe.wait_ge(s["s_max"], at("s_max", GROUP * T * (g + 1)))
                        pe.transpose(bank[A0][0:GROUP * T, 0:P], m_tok[:, GROUP * T * g:GROUP * T * (g + 1)],
                                     w["ident"][:]).then_inc(s["m_t"], 1)
                    if u >= LEAD:
                        g, i = divmod(u - LEAD, SLOTS)
                        j = g * GROUP * T + i
                        if i == 0:
                            pe.wait_ge(m_in[g], at(f"m_in{g}", 16))
                            if g:
                                pe.wait_ge(s["o_norm"], at("o_norm", g))
                        if i < GROUP * T:
                            h, kt = GROUP * g + i % GROUP, i // GROUP
                            if j:
                                pe.wait_ge(s["st_exp"], at("st_exp", j))
                            else:
                                pe.wait_ge(s["s_max"], at("s_max", LEAD - 2))
                            mm(bank[A1][:], stack[0:STACK_ROWS, 1, h, kt * P:(kt + 1) * P],
                               stack[0:STACK_ROWS, 0, h, :]).then_inc(s["st_out"], 1)
                        if 1 <= i <= GROUP * T:
                            hh, kt = (i - 1) % GROUP, (i - 1) // GROUP
                            pe.wait_ge(s["st_exp"], at("st_exp", j))
                            if i == 1 and g:
                                pe.wait_ge(s["o_sb"], at("o_sb", g))
                            mm(bank[A2][32 * hh:32 * (hh + 1), :], vaug[:, kt, GROUP * g + hh, :], probs_a[:, (j - 1) % RING_A, :],
                               start=(kt == 0), stop=(kt == T - 1)).then_inc(s["pv"], 1)
                        if i == SLOTS - 1:
                            pe.wait_ge(s["o_sb"], at("o_sb", g + 1))
                            turn_tiles(bank[A1], lambda t: tiles_a[:, 4 + g % 2, t * P:(t + 1) * P]).then_inc(s["o_t"], 1)
                    yield
                pe.wait_ge(s["o_norm"], at("o_norm", GROUPS))
                turn_tiles(bank[A0], lambda t: heads_out[:, t, :]).then_inc(s["at_t"], 1)
                yield
                pe.wait_ge(s["at_sb"], at("at_sb", 1))
                for t in range(T):
                    last = mm(bank[A1][:, t * P:(t + 1) * P], tiles_a[:, 1, t * P:(t + 1) * P], w["wo0"][:])
                last.then_inc(s["attn_y"], 1)
                yield
                yield from waits(3)
                pe.wait_ge(s["l0_out"], at("l0_out", 1))
                turn_tiles(bank[A0], lambda t: x_tok[:, par, t, :]).then_inc(s["l0_turn"], 1)
                yield
                yield

            def ffn(batch):
                at, par = counter(batch), batch[1] % 2
                xT = x_chan[:, par]
                class_b_free(pe, "ffn", batch)
                for t in range(T):
                    last = mm(bank[B5][:, t * HE:(t + 1) * HE], xT[:, t * P:(t + 1) * P], w["fgate"][:])
                last.then_inc(s["gate_p"], 1)
                yield
                for half in range(2):
                    if half:
                        pe.wait_ge(s["g_in"], at("g_in", HALF * PAIRS))
                        pe.wait_ge(s["fo_lo"], at("fo_lo", HALF))
                    for i in range(2 * HALF):
                        n = 2 * HALF * half + i
                        if i >= 3:
                            pe.wait_ge(s["fp_lo"], at("fp_lo", n - 2))
                        elif n == 2:
                            pe.wait_ge(s["gate_e"], at("gate_e", 1))
                        mm(bank[B3 + i % 3][:], (w["fwk"] if i % 2 else w["fwq"])[:, HALF * half + i // 2, :],
                           xT).then_inc(s["fp"], 1)
                        yield
                    yield
                    for u in range(TILES_H):
                        i = TILES_H * half + u
                        hh, t = divmod(u, T)
                        n = (t + 1) * P
                        if u < 3:
                            pe.wait_ge(s["fp_lo"], at("fp_lo", 2 * HALF * (half + 1)))
                        else:
                            pe.wait_ge(s["fs_max"], at("fs_max", i - 2))
                        mm(bank[B3 + u % 3][:, 0:n], f_q[:, hh, t * P:n], f_k[:, hh, 0, 0:n], True, False)
                        mm(bank[B3 + u % 3][:, 0:n], f_q[:, hh, t * P:n], f_k[:, hh, 1, 0:n], False, True).then_inc(s["fs"], 1)
                        yield
                    pe.wait_ge(s["fm_cut"], at("fm_cut", half + 1))
                    for t in range(T):
                        last = pe.transpose(bank[B5][:].bitcast(BF16)[0:PARTS * HALF, t * P:(t + 1) * P],
                                            fm_parts[:, t].rearrange("p a c -> p (a c)"), ident_b[:])
                    last.then_inc(s["fm_t"], 1)
                    yield
                    pe.wait_ge(s["fm_sb"], at("fm_sb", half + 1))
                    if half == 0:
                        pe.wait_ge(s["gate_done"], at("gate_done", 1))
                        turn_tiles(bank[B5], lambda t: gm_tok[:, t].rearrange("p h a c -> p (h a c)").bitcast(F32)).then_inc(s["gm_t"], 1)
                    yield
                    if half == 0:
                        pe.wait_ge(s["ve_in"], at("ve_in", 16))
                        for i in range(T * EF):
                            t, e = divmod(i, EF)
                            if i == 2:
                                pe.wait_ge(s["gm_sb"], at("gm_sb", 2))
                            if i >= 3:
                                o = i - 3
                                if o % EF == 0:
                                    pe.wait_ge(s["ve_first"], at("ve_first", o // EF + 1))
                                else:
                                    pe.wait_ge(s["ve_sel"], at("ve_sel", o // EF * (EF - 1) + o % EF))
                            mm(bank[B3 + i % 3][:], xT[:, t * P:(t + 1) * P], w["ve"][:, e, :]).then_inc(s["ve"], 1)
                            yield
                        pe.wait_ge(s["vals_in"], at("vals_in", T))
                        pe.wait_ge(s["oe_in"], at("oe_in", 16))
                        yield
                    for u in range(TILES_H + OUT_LAG + 1):
                        c = HALF * PAIRS * half + u - OUT_LAG
                        if u < TILES_H:
                            hh, kt = divmod(u, T)
                            j, n = TILES_H * half + u, S - kt * P
                            if u:
                                pe.wait_ge(s["fst_exp"], at("fst_exp", j))
                            elif half == 0:
                                pe.wait_ge(s["gm_sb"], at("gm_sb", 2))
                            o = bank[B5][:, 0:n]
                            mm(o, f_k[:, hh, 0, kt * P:(kt + 1) * P], f_q[:, hh, kt * P:S], True, False)
                            mm(o, f_k[:, hh, 1, kt * P:(kt + 1) * P], f_q[:, hh, kt * P:S], False, False)
                            mm(o, pick_h[:, hh:hh + 1].to_broadcast([PAD, P]), fmT[:, kt * P:S], False, True).then_inc(s["fst"], 1)
                        if u > OUT_LAG:
                            pe.wait_ge(s["g_in"], at("g_in", c))
                            mm(bank[B7][:], w["oe"][:, c - 1, :], tiles_b[:, (c - 1) % 2, :], c == 1, c == HF * PAIRS).then_inc(s["oe"], 1)
                        if OUT_LAG <= u < TILES_H + OUT_LAG:
                            if u == OUT_LAG and half:
                                pe.wait_ge(s["fs_max"], at("fs_max", TILES_H * 2))
                            chunk = c % (HALF * PAIRS)
                            mm(bank[B3][:], pick_wide[:, P * chunk:P * (chunk + 1)], gmT[:, half]).then_inc(s["mask"], 1)
                        if 1 <= u <= TILES_H:
                            hh, kt = divmod(u - 1, T)
                            h, j = HALF * half + hh, TILES_H * half + u - 1
                            if kt == 0 and hh >= 2:
                                pe.wait_ge(s["fo_lo"], at("fo_lo", h - 1))
                            elif u == 1:
                                pe.wait_ge(s["fs_max"], at("fs_max", TILES_H * (half + 1)))
                            pe.wait_ge(s["fst_cut"], at("fst_cut", j + 1))
                            mm(bank[B4 + 2 * (h % 2)][:, kt * P:S], vals[:, kt, h, :], probs_b[:, j % RING, 0:S - kt * P],
                               kt == 0, kt == T - 1).then_inc(s["fpv"], 1)
                        yield
                yield
                pe.wait_ge(s["fo_sb"], at("fo_sb", 1))
                turn_tiles(bank[B5], lambda t: tiles_b[:, 5, t * P:(t + 1) * P]).then_inc(s["fo_t"], 1)
                yield
                yield from waits(3)
                pe.wait_ge(s["ffn_out"], at("ffn_out", 1))
                turn_tiles(bank[B3], lambda t: x_tok[:, par, t, :]).then_inc(s["ffn_turn"], 1)
                yield
                yield

            def gla(batch):
                at, par = counter(batch), batch[1] % 2
                xT = x_chan[:, par]
                class_a_free(pe, "gla", batch)
                mm(bank[A0][:], w["gwq"][:], xT).then_inc(s["g_proj"], 1)
                mm(bank[A1][:], w["gwk"][:], xT).then_inc(s["g_proj"], 1)
                mm(bank[A2][:], w["gwg1"][:], xT).then_inc(s["g_proj"], 1)
                yield
                pe.wait_ge(s["g_h1"], at("g_h1", 1))
                for t in range(T):
                    last = mm(bank[A2][:, t * P:(t + 1) * P], xT[:, t * P:(t + 1) * P], w["gwv"][:])
                last.then_inc(s["g_proj"], 1)
                yield
                pe.wait_ge(s["g_v"], at("g_v", 1))
                for t in range(T):
                    last = mm(bank[A2][:, t * P:(t + 1) * P], h1T[:, t * P:(t + 1) * P], w["gwg2"][:])
                last.then_inc(s["gg_p"], 1)
                yield
                yield from waits(21)
                for lv in range(LEVELS + 1):
                    if lv:
                        yield from waits(3)
                    pe.wait_ge(s["lv_in"], at("lv_in", lv + 1))
                    if lv >= 2:
                        pe.wait_ge(s["lv_out"], at("lv_out", lv - 1))
                    q, k = (qc, kc) if lv == 0 else (q_lv[lv % 2], k_lv[lv % 2])
                    if lv <= IN_TILE:
                        blocks = [(c * P, c * P, P, c * P) for c in range(T)]
                    elif lv == IN_TILE + 1:
                        blocks = [(0, P, P, 0), (2 * P, 3 * P, P, P)]
                    else:
                        blocks = [(0, 2 * P, 2 * P, 0), (P, 2 * P, 2 * P, 2 * P)]
                    for j0, i0, n, o in blocks:
                        for c in range(2):
                            last = mm(bank[A0 + lv % 2][:, o:o + n], k[:, c, j0:j0 + P], q[:, c, i0:i0 + n], c == 0, c == 1)
                    last.then_inc(s["lv_mm"], 1)
                    yield
                yield
                pe.wait_ge(s["lv_out"], at("lv_out", LEVELS + 1))
                pe.wait_ge(s["gg_e"], at("gg_e", 1))
                for i in range(T):
                    for j in range(i + 1):
                        if i == j:
                            a = at_diag[:, i * P:(i + 1) * P]
                        elif i // 2 == j // 2:
                            a = at_near[:, (i // 2) * P:(i // 2 + 1) * P]
                        else:
                            a = at_far[:, 2 * P * j + (i - 2) * P:2 * P * j + (i - 1) * P]
                        last = mm(bank[A2][:, i * P:(i + 1) * P], a, v_tok[:, j * P:(j + 1) * P], j == 0, j == i)
                last.then_inc(s["g_o"], 1)
                yield
                yield from waits(3)
                pe.wait_ge(s["gn"], at("gn", 1))
                turn_tiles(bank[A0], lambda t: tiles_a[:, 3, t * P:(t + 1) * P]).then_inc(s["gn_t"], 1)
                yield
                yield
                pe.wait_ge(s["gn_sb"], at("gn_sb", 1))
                for t in range(T):
                    last = mm(bank[A1][:, t * P:(t + 1) * P], tiles_a[:, 0, t * P:(t + 1) * P], w["gwo"][:])
                last.then_inc(s["gla_p"], 1)
                yield
                yield from waits(3)
                pe.wait_ge(s["gla_out"], at("gla_out", 2))
                turn_tiles(bank[A0], lambda t: x_tok[:, par, t, :]).then_inc(s["gla_turn"], 1)
                yield
                yield

            def moe(batch, refill=False):
                at, par = counter(batch), batch[1] % 2
                xT = x_chan[:, par]
                class_b_free(pe, "moe", batch)
                for t in range(T):
                    last = mm(bank[B5][:, t * EM:(t + 1) * EM], xT[:, t * P:(t + 1) * P], w["wr"][:])
                last.then_inc(s["r_p"], 1)
                yield

                def relu_done(i):
                    name = "relu_v" if i % 2 else "relu_a"
                    return s[name], at(name, i // 2 + 1)

                def up(i):
                    if i >= 2:
                        pe.wait_ge(*relu_done(i - 2))
                    mm(bank[B3 + i % 2][:], w["w1"][:, i // HC, (i % HC) * P:(i % HC + 1) * P], xT).then_inc(s["w1"], 1)

                def rows(e):
                    if e == 0:
                        pe.wait_ge(s["r_sb"], at("r_sb", 1))
                    else:
                        pe.wait_ge(s["moe_mul"], at("moe_mul", e))
                    mm(bank[B5][:], pick_e[:, e:e + 1].to_broadcast([PAD, P]), rT[:]).then_inc(s["rb"], 1)

                pe.wait_ge(s["w1_in"], at("w1_in", 16))
                up(0)
                yield
                pe.wait_ge(s["w2_in"], at("w2_in", 16))
                yield
                for i in range(EM * HC):
                    e, c = divmod(i, HC)
                    if i + 1 < EM * HC:
                        up(i + 1)
                    pe.wait_ge(*relu_done(i))
                    if c == 0 and e >= 2:
                        pe.wait_ge(s["oe_b"], at("oe_b", e - 1))
                    mm(bank[B6 + e % 2][:], w["w2"][:, i, :], probs_b[:, i % RING, :], c == 0, c == HC - 1).then_inc(s["w2"], 1)
                    if i == 3:
                        pe.wait_ge(s["r_done"], at("r_done", 1))
                        for t in range(T):
                            last = pe.transpose(bank[B5][0:2 * EM, t * P:(t + 1) * P],
                                                r_tok[:, t].rearrange("p a c -> p (a c)").bitcast(F32), w["ident"][:])
                        last.then_inc(s["r_t"], 1)
                    if c == 0 and e:
                        rows(e - 1)
                    yield
                rows(EM - 1)
                yield
                yield
                pe.wait_ge(s["moe_acc"], at("moe_acc", 1))
                turn_tiles(bank[B3], lambda t: tiles_b[:, 2, t * P:(t + 1) * P]).then_inc(s["mo_t"], 1)
                yield
                yield from waits(LN_UNITS)

            two_by_two(pe, NB // 2, l0, ffn, gla, moe)

        @block.scalar
        def _(act):
            act.preload_act_table_set("natural_log_exp_and_others")
            act.wait_ge(loaded, 16 * n_loads[0])
            act.wait_ge(const_ready, CONSTS)

            def rstd_rows(at, stage, ln, n=1):
                act.wait_ge(s[stage + "_var"], at(stage + "_var", n))
                act.activation(ln["r"][:, 0, :], ln["mv"][:, :, 1], ACT.Ln, bias=eps[:, 1:2]).then_inc(s[stage + "_rs"], 1)
                act.wait_ge(s[stage + "_rs"], at(stage + "_rs", 2 * n - 1))
                act.activation(ln["r"][:, 1, :], ln["r"][:, 0, :], ACT.Exp, scale=-0.5).then_inc(s[stage + "_rs"], 1)

            def l0(batch):
                at, par = counter(batch), batch[1] % 2
                class_a_free(act, "l0", batch)
                for n in range(2):
                    act.wait_ge(s["proj"], at("proj", n + 1))
                    act.activation(tiles_a[:, n, :], bank[A0 + n][:], ACT.Identity, bias=w["cols"][:, n:n + 1]).then_inc(s["lin"], 1)
                    act.activation(tiles_a[:, 2 + n, :], bank[A0 + n][:], ACT.Square, bias=w["cols"][:, n:n + 1]).then_inc(s["lin"], 1)
                    yield
                for n in range(2):
                    act.wait_ge(s["msq"], at("msq", n + 1))
                    act.activation(tiles_a[:, 4 + n, :], bank[A0 + n][:], ACT.Ln, bias=eps[:, 0:1], scale=1.0 / D).then_inc(s["rs"], 1)
                    if n:
                        for m in range(2):
                            act.wait_ge(s["rs"], at("rs", 2))
                            act.activation(tiles_a[:, 2 + m, :], tiles_a[:, 4 + m, :], ACT.Exp, scale=-0.5).then_inc(s["rs"], 1)
                    yield
                yield from waits(6)
                for u in range(LEAD + GROUPS * SLOTS):
                    if u >= LEAD:
                        g, i = divmod(u - LEAD, SLOTS)
                        j = g * GROUP * T + i
                        if i < GROUP * T:
                            act.wait_ge(s["st_out"], at("st_out", j + 1))
                            if j >= RING_A:
                                act.wait_ge(s["pv"], at("pv", j - RING_A + 1))
                            act.activation(probs_a[:, j % RING_A, :], bank[A1][:], ACT.Exp).then_inc(s["st_exp"], 1)
                    yield
                act.wait_ge(s["at_t"], at("at_t", 1))
                act.activation(tiles_a[:, 1, :], bank[A0][:], ACT.Copy).then_inc(s["at_sb"], 1)
                yield
                yield
                yield
                rstd_rows(at, "l0", ln_a)
                yield
                yield from waits(2)
                act.wait_ge(s["l0_turn"], at("l0_turn", 1))
                act.activation(x_chan[:, par], bank[A0][:], ACT.Copy).then_inc(s["l0_done"], 1)
                yield

            def ffn(batch):
                at, par = counter(batch), batch[1] % 2
                class_b_free(act, "ffn", batch)
                act.wait_ge(s["gate_p"], at("gate_p", 1))
                act.activation(gs[:, 0, :], bank[B5][:, 0:T * HE], ACT.Exp, scale=-1.0).then_inc(s["gate_e"], 1)
                yield
                for half in range(2):
                    for i in range(2 * HALF):
                        act.wait_ge(s["fp"], at("fp", 2 * HALF * half + i + 1))
                        if i % 2 == 0:
                            act.activation(f_q[:, i // 2], bank[B3 + i % 3][:], ACT.Copy, scale=float(FD) ** -0.5).then_inc(s["fp_hi"], 1)
                        else:
                            act.activation(f_k[:, i // 2, 0], bank[B3 + i % 3][:], ACT.Copy).then_inc(s["fp_hi"], 1)
                        yield
                    yield from waits(1 + TILES_H)
                    act.wait_ge(s["fm_t"], at("fm_t", half + 1))
                    act.activation(fmT[0:PARTS * HALF, :], bank[B5][:].bitcast(BF16)[0:PARTS * HALF, 0:S], ACT.Copy).then_inc(s["fm_sb"], 1)
                    yield
                    if half == 0:
                        act.wait_ge(s["gm_t"], at("gm_t", 1))
                        for k in range(2):
                            act.activation(gmT[0:2 * GH, k], bank[B5][2 * GH * k:2 * GH * (k + 1), :], ACT.Copy).then_inc(s["gm_sb"], 1)
                    yield
                    if half == 0:
                        for i in range(T * EF):
                            if i % EF == 0:
                                t = i // EF
                                act.wait_ge(s["ve"], at("ve", i + 1))
                                act.activation(vals[:, t, :, 0:FD], bank[B3 + i % 3][:].rearrange("p (h k) -> p h k", h=HF),
                                               ACT.Copy).then_inc(s["ve_first"], 1)
                            yield
                        yield
                    for u in range(TILES_H + OUT_LAG + 1):
                        if u < TILES_H:
                            kt = u % T
                            j, n = TILES_H * half + u, S - kt * P
                            act.wait_ge(s["fst"], at("fst", j + 1))
                            if j >= RING:
                                act.wait_ge(s["fpv"], at("fpv", j - RING + 1))
                            act.activation(probs_b[:, j % RING, 0:n], bank[B5][:, 0:n], ACT.Exp).then_inc(s["fst_exp"], 1)
                        head = u // T - 1
                        h = HALF * half + head
                        if u % T == 1 and 0 <= head < HALF:
                            act.wait_ge(s["fpv"], at("fpv", T * (h + 1)))
                            if h:
                                act.wait_ge(s["fo_lo"], at("fo_lo", h))
                            act.activation(tiles_b[0:FD, 2, :], bank[B4 + 2 * (h % 2)][FD:P, :], ACT.Ln).then_inc(s["f_ln"], 1)
                            act.wait_ge(s["f_ln"], at("f_ln", h + 1))
                            act.activation(tiles_b[0:FD, 2, :], tiles_b[0:FD, 2, :], ACT.Exp, scale=-1.0).then_inc(s["f_rec"], 1)
                        if u % T == 3 and 0 <= head < HALF:
                            act.wait_ge(s["fo_lo"], at("fo_lo", h + 1))
                            act.activation(tiles_b[FD:P, 3 + h % 2, :], tiles_b[0:FD, 3 + h % 2, :], ACT.Copy).then_inc(s["fo_hi"], 1)
                        yield
                act.wait_ge(s["oe"], at("oe", HF * PAIRS))
                act.activation(tiles_b[:, 5, :], bank[B7][:], ACT.Copy).then_inc(s["fo_sb"], 1)
                yield
                yield
                yield
                rstd_rows(at, "ffn", ln_b)
                yield
                yield from waits(2)
                act.wait_ge(s["ffn_turn"], at("ffn_turn", 1))
                act.activation(x_chan[:, par], bank[B3][:], ACT.Copy).then_inc(s["ffn_done"], 1)
                yield

            def gla(batch):
                at, par = counter(batch), batch[1] % 2
                g_ = lambda i: gla_tiles[:, i]
                class_a_free(act, "gla", batch)
                act.wait_ge(s["g_proj"], at("g_proj", 3))
                act.activation(h1T, bank[A2][:], ACT.Copy).then_inc(s["g_h1"], 1)
                for n in range(2):
                    act.activation(g_(n), bank[A0 + n][:], ACT.Exp, scale=-1.0).then_inc(s["g_exp"], 1)
                yield
                for n in range(2):
                    act.wait_ge(s["g_exp"], at("g_exp", n + 1))
                    act.activation(g_(4 + n), g_(n), ACT.Ln, bias=1.0).then_inc(s["g_ln"], 1)
                act.wait_ge(s["g_proj"], at("g_proj", 4))
                act.activation(v_tok, bank[A2][:], ACT.Copy).then_inc(s["g_v"], 1)
                yield
                for n in range(2):
                    act.wait_ge(s["g_ln"], at("g_ln", n + 1))
                    act.activation(g_(2 + n), g_(4 + n), ACT.Exp, scale=-1.0).then_inc(s["g_sig"], 1)
                yield
                act.wait_ge(s["gg_p"], at("gg_p", 1))
                act.activation(tiles_a[:, 3, :], bank[A2][:], ACT.Exp, scale=-1.0).then_inc(s["gg_e"], 1)
                act.wait_ge(s["gg_e"], at("gg_e", 1))
                act.activation(tiles_a[:, 4, :], tiles_a[:, 3, :], ACT.Ln, bias=1.0).then_inc(s["gg_e"], 1)
                act.wait_ge(s["gg_e"], at("gg_e", 2))
                act.activation(tiles_a[:, 5, :], tiles_a[:, 4, :], ACT.Exp, scale=-1.0).then_inc(s["gg_e"], 1)
                yield from waits(21 + 1 + 4 * LEVELS)
                yield from waits(4)
                rstd_rows(at, "gla", ln_a, 1)
                yield
                yield
                act.wait_ge(s["gn_t"], at("gn_t", 1))
                act.activation(tiles_a[:, 0, :], bank[A0][:], ACT.Copy).then_inc(s["gn_sb"], 1)
                yield
                yield
                yield
                yield
                rstd_rows(at, "gla", ln_a, 2)
                yield
                yield from waits(2)
                act.wait_ge(s["gla_turn"], at("gla_turn", 1))
                act.activation(x_chan[:, par], bank[A0][:], ACT.Copy).then_inc(s["gla_done"], 1)
                yield

            def moe(batch, refill=False):
                at, par = counter(batch), batch[1] % 2
                class_b_free(act, "moe", batch)
                yield

                def relu(i):
                    act.wait_ge(s["w1"], at("w1", i + 1))
                    if i >= RING:
                        act.wait_ge(s["w2"], at("w2", i - RING + 1))
                    act.activation(probs_b[:, i % RING, :], bank[B3 + i % 2][:], ACT.Relu, bias=w["b1c"][:, i:i + 1]).then_inc(s["relu_a"], 1)

                def out_bias(e):
                    act.wait_ge(s["w2"], at("w2", HC * (e + 1)))
                    if e >= 2:
                        act.wait_ge(s["moe_mul"], at("moe_mul", e - 1))
                    act.activation(tiles_b[:, e % 2, :], bank[B6 + e % 2][:], ACT.Identity, bias=w["b2c"][:, e:e + 1]).then_inc(s["oe_b"], 1)

                relu(0)
                yield
                act.wait_ge(s["r_m"], at("r_m", 1))
                act.activation(rt[:, 1], rt[:, 0], ACT.Exp).then_inc(s["r_e"], 1)
                yield
                for i in range(EM * HC):
                    e, c = divmod(i, HC)
                    if (i + 1) % 2 == 0 and i + 1 < EM * HC:
                        relu(i + 1)
                    if i == 3:
                        act.wait_ge(s["r_t"], at("r_t", 1))
                        act.activation(rT[0:2 * EM, :], bank[B5][0:2 * EM, :], ACT.Copy).then_inc(s["r_sb"], 1)
                    if c == 0 and e:
                        out_bias(e - 1)
                    yield
                out_bias(EM - 1)
                yield
                yield
                yield
                yield
                rstd_rows(at, "moe", ln_b)
                yield
                yield from waits(3)

            two_by_two(act, NB // 2, l0, ffn, gla, moe)

        @block.vector
        def _(dve):
            dve.wait_ge(loaded, 16 * n_loads[0])
            dve.tensor_copy(ident_b[:], w["ident"][:]).then_inc(const_ready, 1)
            dve.tensor_scalar(q_scale[:], w["cols"][:, 2:3], float(HD) ** -0.5, None, ALU.mult).then_inc(const_ready, 1)
            dve.tensor_copy(pick_wide[:].rearrange("p (r k) -> p r k", k=FD),
                            w["picks"][0:PAD, 0:GH].unsqueeze(2).to_broadcast([PAD, GH, FD])).then_inc(const_ready, 1)
            dve.tensor_copy(pick_e[:], w["picks"][0:PAD, GH:GH + EM]).then_inc(const_ready, 1)
            dve.tensor_copy(pick_h[:], w["picks"][0:PAD, GH + EM:]).then_inc(const_ready, 1)
            dve.wait_ge(const_ready, CONSTS)

            def chain_of(at, stage):
                links = [0]

                def link(i):
                    links[0] += 1
                    i.then_inc(s[stage + "_link"], 1)
                    dve.wait_ge(s[stage + "_link"], at(stage + "_link", links[0]))

                def close():
                    dve.sem_inc(s[stage + "_link"], PER[stage + "_link"] - links[0])
                return link, close

            def layer_norm(at, link, stage, ln, src, into, n=1, scale_row=None):
                for t in range(T):
                    link(dve.bn_stats(ln["st"][:, t, :], src[:, t, :]))
                dve.sem_inc(passed, 1)
                for t in range(T):
                    last = dve.bn_aggr(ln["mv"][:, t, :], ln["st"][:, t, :])
                last.then_inc(s[stage + "_var"], 1)
                yield
                yield
                dve.wait_ge(s[stage + "_rs"], at(stage + "_rs", 2 * n))
                done = "moe_done" if stage == "moe" else stage + "_out"
                for t in range(T):
                    last = dve.tensor_scalar(into[:, t, :], src[:, t, :], ln["mv"][:, t, 0:1], ln["r"][:, 1, t:t + 1],
                                             ALU.subtract, ALU.mult)
                last.then_inc(s[done], 1)
                dve.wait_ge(s[done], at(done, n))

            def first_max(link, src, top, eq, cand, top2, onehot):
                n = src.shape[1]
                wide_ = lambda a: a.unsqueeze(2).to_broadcast([P, n, EF])
                link(dve.tensor_reduce(top, src, AX.X, ALU.max))
                link(dve.tensor_tensor(eq, src, wide_(top), ALU.is_equal))
                link(dve.tensor_tensor(cand, eq, w["ramp"][:].unsqueeze(1).to_broadcast([P, n, EF]), ALU.mult))
                link(dve.tensor_reduce(top2, cand, AX.X, ALU.max))
                link(dve.tensor_tensor(onehot, cand, wide_(top2), ALU.is_equal))

            def l0(batch):
                at, par = counter(batch), batch[1] % 2
                link, close = chain_of(at, "l0")
                x = x_tok[:, par]
                class_a_free(dve, "l0", batch)
                yield
                dve.wait_ge(s["proj"], at("proj", 3))
                for t in range(T):
                    dve.tensor_tensor(vaug[:, t, :, 0:HD], bank[A2][:, t * P:(t + 1) * P].rearrange("p (h d) -> p h d", d=HD),
                                      w["bv_row"][:].rearrange("p (h d) -> p h d", d=HD), ALU.add).then_inc(s["vaug"], 1)
                yield
                yield
                for n in range(2):
                    yield
                    if n == 0:
                        pass
                    dve.wait_ge(s["rs"], at("rs", 3 + n))
                    nrm, rest_ = tiles_a[:, 4 + n, :], tiles_a[:, 2 + n, :]
                    link(dve.scalar_tensor_tensor(nrm, tiles_a[:, n, :], q_scale[:, 0:1] if n == 0 else w["cols"][:, 3:4],
                                                  tiles_a[:, 2 + n, :], ALU.mult, ALU.mult))
                    link(dve.tensor_copy(parts[:, n, 0, :], nrm))
                    link(dve.tensor_tensor(rest_, nrm, parts[:, n, 0, :], ALU.subtract))
                    link(dve.tensor_copy(parts[:, n, 1, :], rest_))
                    dve.tensor_tensor(parts[:, n, 2, :], rest_, parts[:, n, 1, :], ALU.subtract).then_inc(s["qk_split"], 1)
                yield from waits(5)
                for u in range(LEAD + GROUPS * SLOTS):
                    g, i = divmod(u, SLOTS)
                    if g < GROUPS and i < GROUP * T:
                        n = g * GROUP * T + i
                        dve.wait_ge(s["s_out"], at("s_out", n + 1))
                        dve.tensor_reduce(m_tok[:, n:n + 1], bank[s_bank(u, n)][:], AX.X, ALU.max).then_inc(s["s_max"], 1)
                    elif g < GROUPS and i == GROUP * T:
                        dve.wait_ge(s["m_t"], at("m_t", g + 1))
                        src, k = bank[A0][0:GROUP * T, 0:P], GROUP * T
                        link(dve.tensor_scalar(m_row[:, g, 0, :], src, -1.0, None, ALU.mult))
                        link(dve.scalar_tensor_tensor(m_rest[0:k, 0, :], src, -1.0, m_row[:, g, 0, :], ALU.mult, ALU.subtract))
                        link(dve.tensor_copy(m_row[:, g, 1, :], m_rest[0:k, 0, :]))
                        dve.tensor_tensor(m_row[:, g, 2, :], m_rest[0:k, 0, :], m_row[:, g, 1, :], ALU.subtract).then_inc(s["m_rows"], 1)
                    if u >= LEAD:
                        g, i = divmod(u - LEAD, SLOTS)
                        if i == GROUP * T:
                            dve.wait_ge(s["pv"], at("pv", GROUP * T * (g + 1)))
                            dve.tensor_copy(tiles_a[:, 4 + g % 2, :], bank[A2][:]).then_inc(s["o_sb"], 1)
                        if i == SLOTS - 1:
                            dve.wait_ge(s["o_t"], at("o_t", g + 1))
                            v = bank[A1][:].rearrange("p (t h c) -> p t h c", t=T, c=VW)
                            rec = m_rest[:, 1, 0:GROUP * T].rearrange("p (t h) -> p t h", t=T)
                            link(dve.reciprocal(rec, v[:, :, :, HD]))
                            dve.tensor_tensor(heads_out[:, :, g * 32:(g + 1) * 32].rearrange("p t (h d) -> p t h d", d=HD),
                                              v[:, :, :, 0:HD], rec.unsqueeze(3).to_broadcast([P, T, GROUP, HD]),
                                              ALU.mult).then_inc(s["o_norm"], 1)
                    yield
                yield
                yield
                dve.wait_ge(s["attn_y"], at("attn_y", 1))
                dve.wait_ge(s["xb"], at("xb", 1))
                flat = x.rearrange("p t d -> p (t d)")
                link(dve.tensor_tensor(flat, bank[A1][:], flat, ALU.add))
                yield from layer_norm(at, link, "l0", ln_a, x, x)
                close()
                yield
                yield from waits(2)

            def ffn(batch):
                at, par = counter(batch), batch[1] % 2
                link, close = chain_of(at, "ffn")
                x = x_tok[:, par]
                class_b_free(dve, "ffn", batch)
                dve.wait_ge(s["gate_e"], at("gate_e", 1))
                g3 = lambda i: gs[:, i, :].rearrange("p (n e) -> p n e", e=EF)
                top, top2 = gsm[:, 0, :], gsm[:, 1, :]
                by_head = lambda a: a.unsqueeze(2).to_broadcast([P, T * HF, EF])
                part = lambda a: gm_tok[:, :, :, a, :]
                gsrc = gs[:, 1, :].rearrange("p (t h c) -> p t h c", t=T, h=2)
                gate_steps = [
                    lambda: link(dve.reciprocal(gs[:, 2, :], gs[:, 1, :])),
                    lambda: link(dve.tensor_reduce(top, g3(2), AX.X, ALU.max)),
                    lambda: link(dve.tensor_tensor(g3(1), g3(2), by_head(top), ALU.is_equal)),
                    lambda: link(dve.tensor_tensor(g3(0), g3(1), w["ramp"][:].unsqueeze(1).to_broadcast([P, T * HF, EF]), ALU.mult)),
                    lambda: link(dve.tensor_reduce(top2, g3(0), AX.X, ALU.max)),
                    lambda: link(dve.tensor_tensor(oh[:], g3(0), by_head(top2), ALU.is_equal)),
                    lambda: link(dve.tensor_tensor(gs[:, 1, :], gs[:, 2, :], oh[:].rearrange("p n e -> p (n e)"), ALU.mult)),
                    lambda: link(dve.tensor_copy(part(0), gsrc)),
                    lambda: dve.tensor_tensor(part(1), gsrc, part(0).bitcast(F32), ALU.subtract).then_inc(s["gate_done"], 1),
                ]
                link(dve.tensor_scalar(gs[:, 1, :], gs[:, 0, :], 1.0, None, ALU.add))
                yield
                for half in range(2):
                    for i in range(2 * HALF + 1):
                        if i:
                            n = 2 * HALF * half + i
                            j = i - 1
                            dve.wait_ge(s["fp_hi"], at("fp_hi", n))
                            if j % 2 == 0:
                                hi = f_q[FD:P, j // 2]
                                dve.scalar_tensor_tensor(hi, bank[B3 + j % 3][FD:P, :], float(FD) ** -0.5, hi.bitcast(F32),
                                                         ALU.mult, ALU.subtract).then_inc(s["fp_lo"], 1)
                            else:
                                dve.tensor_tensor(f_k[:, j // 2, 1], bank[B3 + j % 3][:], f_k[:, j // 2, 0].bitcast(F32),
                                                  ALU.subtract).then_inc(s["fp_lo"], 1)
                        if half == 0:
                            gate_steps[i]()
                        yield
                    for u in range(TILES_H):
                        i = TILES_H * half + u
                        h, t = divmod(i, T)
                        n = (t + 1) * P
                        dve.wait_ge(s["fs"], at("fs", i + 1))
                        if i >= 2:
                            dve.wait_ge(s["fs_max"], at("fs_max", i - 1))
                        dve.sem_inc(passed, 1)
                        dve.tensor_tensor_reduce(tiles_b[:, i % 2, 0:n], bank[B3 + u % 3][:, 0:n], w["cut_row"][:, S - n:S], 1.0, -3.4e38,
                                                 ALU.add, ALU.max, fm_tok[:, t, h:h + 1]).then_inc(s["fs_max"], 1)
                        yield
                    dve.wait_ge(s["fs_max"], at("fs_max", TILES_H * (half + 1)))
                    m = fm_tok[:, :, HALF * half:HALF * (half + 1)]
                    link(dve.tensor_scalar(fm_parts[:, :, 0, :], m, -1.0, None, ALU.mult))
                    link(dve.scalar_tensor_tensor(fm_rest[:], m, -1.0, fm_parts[:, :, 0, :], ALU.mult, ALU.subtract))
                    link(dve.tensor_copy(fm_parts[:, :, 1, :], fm_rest[:]))
                    dve.tensor_tensor(fm_parts[:, :, 2, :], fm_rest[:], fm_parts[:, :, 1, :], ALU.subtract).then_inc(s["fm_cut"], 1)
                    yield
                    yield
                    if half == 0:
                        for i in range(T * EF):
                            t, e = divmod(i, EF)
                            v = vals[:, t, :, 0:FD]
                            heads = slice(t * HF, (t + 1) * HF)
                            if e == 0:
                                dve.wait_ge(s["ve_first"], at("ve_first", t + 1))
                            else:
                                dve.wait_ge(s["ve"], at("ve", i + 1))
                                dve.sem_inc(passed, 1)
                                dve.copy_predicated(v, oh[:, heads, e].bitcast(U32).unsqueeze(2).to_broadcast([P, HF, FD]),
                                                    bank[B3 + i % 3][:].rearrange("p (h k) -> p h k", h=HF)).then_inc(s["ve_sel"], 1)
                                dve.wait_ge(s["ve_sel"], at("ve_sel", t * (EF - 1) + e))
                            if e == EF - 1:
                                dve.tensor_tensor(v, v, gsm[:, 0, heads].unsqueeze(2).to_broadcast([P, HF, FD]), ALU.mult).then_inc(s["vals_in"], 1)
                            yield
                        yield
                    for u in range(TILES_H + OUT_LAG + 1):
                        if u % T == 2 and T < u <= TILES_H + T:
                            h = HALF * half + u // T - 1
                            dve.wait_ge(s["f_rec"], at("f_rec", h + 1))
                            if h >= 2:
                                dve.wait_ge(s["g_in"], at("g_in", PAIRS * (h - 1)))
                            dve.tensor_tensor(tiles_b[0:FD, 3 + h % 2, :], bank[B4 + 2 * (h % 2)][0:FD, :], tiles_b[0:FD, 2, :], ALU.mult).then_inc(s["fo_lo"], 1)
                        if OUT_LAG <= u < TILES_H + OUT_LAG:
                            c = HALF * PAIRS * half + u - OUT_LAG
                            h = c // PAIRS
                            if c % PAIRS == 0:
                                dve.wait_ge(s["fo_hi"], at("fo_hi", h + 1))
                            dve.wait_ge(s["mask"], at("mask", c + 1))
                            if c >= 2:
                                dve.wait_ge(s["oe"], at("oe", c - 1))
                            dve.tensor_tensor(tiles_b[:, c % 2, :], bank[B3][:], tiles_b[:, 3 + h % 2, :], ALU.mult).then_inc(s["g_in"], 1)
                        yield
                yield
                yield
                dve.wait_ge(s["fo_t"], at("fo_t", 1))
                flat = x.rearrange("p t d -> p (t d)")
                link(dve.tensor_tensor(flat, bank[B5][:], flat, ALU.add))
                yield from layer_norm(at, link, "ffn", ln_b, x, x)
                close()
                yield
                yield from waits(2)

            def gla(batch):
                at, par = counter(batch), batch[1] % 2
                link, close = chain_of(at, "gla")
                x = x_tok[:, par]
                g_ = lambda i: gla_tiles[:, i]
                class_a_free(dve, "gla", batch)
                yield
                yield
                dve.wait_ge(s["g_ln"], at("g_ln", 2))
                link(dve.tensor_scalar(g_(0), bank[A1][:], F_UP, None, ALU.is_lt))
                link(dve.tensor_scalar(g_(1), bank[A1][:], F_DOWN, None, ALU.is_gt))
                yield
                for op in (
                    lambda: dve.memset(suf, 1.0),
                    lambda: dve.tensor_tensor(g_(6), g_(0), g_(1), ALU.subtract),
                    lambda: dve.tensor_tensor_scan(g_(7), suf, g_(6), 0.0, ALU.mult, ALU.add),
                    lambda: dve.tensor_tensor(g_(0), g_(6), g_(6), ALU.mult),
                    lambda: dve.tensor_scalar(g_(1), g_(0), -2.0, 1.0, ALU.mult, ALU.add),
                    lambda: dve.tensor_tensor_scan(g_(8), g_(1), suf, 1.0, ALU.mult, ALU.mult),
                    lambda: dve.tensor_scalar(g_(0), g_(7), PI, None, ALU.mult),
                    lambda: dve.scalar_tensor_tensor(g_(1), g_(7), -PI1, g_(0), ALU.mult, ALU.add),
                    lambda: dve.scalar_tensor_tensor(g_(0), g_(7), -PI2, g_(1), ALU.mult, ALU.add),
                    lambda: dve.scalar_tensor_tensor(g_(1), g_(7), -PI3, g_(0), ALU.mult, ALU.add),
                    lambda: dve.tensor_tensor(g_(0), g_(1), g_(1), ALU.mult),
                    lambda: dve.tensor_scalar(g_(6), g_(0), -1.0 / 6, 1.0, ALU.mult, ALU.add),
                    lambda: dve.tensor_tensor(g_(7), g_(6), g_(1), ALU.mult),
                    lambda: dve.tensor_scalar(g_(6), g_(0), -0.5, 1.0, ALU.mult, ALU.add),
                    lambda: dve.tensor_tensor(g_(0), g_(6), g_(8), ALU.mult),
                    lambda: dve.tensor_tensor(g_(1), g_(7), g_(8), ALU.mult),
                ):
                    link(op())
                    yield
                dve.wait_ge(s["g_sig"], at("g_sig", 2))
                link(dve.scalar_tensor_tensor(g_(4), g_(2), float(2 * D) ** -0.5, bank[A0][:], ALU.mult, ALU.mult))
                yield
                link(dve.tensor_scalar(pre, g_(3), -1.0, 1.0, ALU.mult, ALU.add))
                yield
                twice = lambda a: a.unsqueeze(1).to_broadcast([P, 2, S])
                sin_cos = gla_tiles[:, 0:2]
                link(dve.tensor_tensor(qc, sin_cos, twice(g_(4)), ALU.mult))
                yield
                dve.tensor_tensor(kc, sin_cos, twice(g_(3)), ALU.mult).then_inc(s["lv_in"], 1)
                dve.wait_ge(s["lv_in"], at("lv_in", 1))
                yield
                yield
                yield

                def take_level(lv):
                    dve.wait_ge(s["lv_mm"], at("lv_mm", lv + 1))
                    src = bank[A0 + lv % 2]
                    mask = w["level_mask"][:, min(lv, IN_TILE), :].unsqueeze(1).to_broadcast([P, T, P])
                    four = lambda a: a.rearrange("p (c i) -> p c i", c=T)
                    if lv == 0:
                        i = dve.tensor_tensor(four(at_diag), four(src[:]), mask, ALU.mult)
                    elif lv <= IN_TILE:
                        dve.sem_inc(passed, 1)
                        i = dve.copy_predicated(four(at_diag), mask.bitcast(U32), four(src[:]))
                    elif lv == IN_TILE + 1:
                        i = dve.tensor_copy(at_near, src[:, 0:2 * P])
                    else:
                        i = dve.tensor_copy(at_far, src[:])
                    i.then_inc(s["lv_out"], 1)

                for lv in range(1, LEVELS + 1):
                    hs = 1 << (lv - 1)
                    halves = lambda a: a.rearrange("p (n two i) -> p n two i", two=2, i=hs)
                    n = S // (2 * hs)
                    if lv >= 3:
                        dve.wait_ge(s["lv_mm"], at("lv_mm", lv - 1))
                    for c in range(2):
                        link(dve.tensor_tensor(halves(q_lv[lv % 2][:, c])[:, :, 1], halves(qc[:, c])[:, :, 1],
                                               halves(pre)[:, :, 1], ALU.mult))
                    yield
                    link(dve.tensor_tensor(halves(k_lv[lv % 2][:, 0])[:, :, 0], halves(kc[:, 0])[:, :, 0],
                                           halves(suf)[:, :, 0], ALU.mult))
                    dve.tensor_tensor(halves(k_lv[lv % 2][:, 1])[:, :, 0], halves(kc[:, 1])[:, :, 0],
                                      halves(suf)[:, :, 0], ALU.mult).then_inc(s["lv_in"], 1)
                    yield
                    if lv < LEVELS:
                        link(dve.tensor_tensor(halves(suf)[:, :, 0], halves(suf)[:, :, 0],
                                               halves(pre)[:, :, 1, hs - 1:hs].to_broadcast([P, n, hs]), ALU.mult))
                        link(dve.tensor_tensor(halves(pre)[:, :, 1], halves(pre)[:, :, 1],
                                               halves(pre)[:, :, 0, hs - 1:hs].to_broadcast([P, n, hs]), ALU.mult))
                    yield
                    if lv >= 2:
                        dve.wait_ge(s["lv_out"], at("lv_out", lv - 1))
                    take_level(lv - 1)
                    yield
                take_level(LEVELS)
                yield
                yield
                dve.wait_ge(s["gg_e"], at("gg_e", 3))
                dve.wait_ge(s["g_o"], at("g_o", 1))
                by_token = lambda i: tiles_a[:, i, :].rearrange("p (t d) -> p t d", t=T)
                link(dve.tensor_tensor(tiles_a[:, 1, :], bank[A2][:], tiles_a[:, 5, :], ALU.mult))
                yield from layer_norm(at, link, "gla", ln_a, by_token(1), by_token(2))
                dve.tensor_tensor(by_token(3), by_token(2), w["gn_row"][:].unsqueeze(1).to_broadcast([P, T, P]), ALU.mult).then_inc(s["gn"], 1)
                yield
                yield from waits(3)
                dve.wait_ge(s["gla_p"], at("gla_p", 1))
                flat = x.rearrange("p t d -> p (t d)")
                link(dve.tensor_tensor(flat, bank[A1][:], flat, ALU.add))
                yield from layer_norm(at, link, "gla", ln_a, x, x, n=2)
                close()
                yield
                yield from waits(2)

            def moe(batch, refill=False):
                at, par = counter(batch), batch[1] % 2
                link, close = chain_of(at, "moe")
                x = x_tok[:, par]
                class_b_free(dve, "moe", batch)
                r = lambda i: rt[:, i]
                by_tile = lambda a: a.unsqueeze(2).to_broadcast([P, T, EM])

                def relu(i):
                    dve.wait_ge(s["w1"], at("w1", i + 1))
                    if i >= RING:
                        dve.wait_ge(s["w2"], at("w2", i - RING + 1))
                    dve.tensor_scalar(probs_b[:, i % RING, :], bank[B3 + i % 2][:], w["b1c"][:, i:i + 1], 0.0,
                                      ALU.add, ALU.max).then_inc(s["relu_v"], 1)

                dve.wait_ge(s["r_p"], at("r_p", 1))
                link(dve.tensor_tensor(r(2), bank[B5][:, 0:T * EM].rearrange("p (t e) -> p t e", t=T),
                                       w["br_row"][:].unsqueeze(1).to_broadcast([P, T, EM]), ALU.add))
                link(dve.tensor_reduce(rt1[:, 0, :], r(2), AX.X, ALU.max))
                dve.tensor_tensor(r(0), r(2), by_tile(rt1[:, 0, :]), ALU.subtract).then_inc(s["r_m"], 1)
                yield
                yield
                yield

                def route():
                    dve.wait_ge(s["r_e"], at("r_e", 1))
                    link(dve.tensor_reduce(rt1[:, 1, :], r(1), AX.X, ALU.add))
                    link(dve.reciprocal(rt1[:, 2, :], rt1[:, 1, :]))
                    link(dve.tensor_tensor(r(2), r(1), by_tile(rt1[:, 2, :]), ALU.mult))
                    first_max(link, r(2), rt1[:, 0, :], r(0), r(1), rt1[:, 1, :], r(3))
                    yield
                    link(dve.scalar_tensor_tensor(r(4), r(3), -2.0, r(2), ALU.mult, ALU.add))
                    first_max(link, r(4), rt1[:, 0, :], r(0), r(1), rt1[:, 1, :], r(5))
                    yield
                    link(dve.tensor_tensor(r(0), r(3), r(5), ALU.add))
                    link(dve.tensor_tensor(r(1), r(0), r(2), ALU.mult))
                    link(dve.tensor_reduce(rt1[:, 0, :], r(1), AX.X, ALU.add))
                    link(dve.reciprocal(rt1[:, 1, :], rt1[:, 0, :]))
                    link(dve.tensor_tensor(r(0), r(1), by_tile(rt1[:, 1, :]), ALU.mult))
                    link(dve.tensor_copy(r_tok[:, :, 0, :], r(0)))
                    dve.tensor_tensor(r_tok[:, :, 1, :], r(0), r_tok[:, :, 0, :].bitcast(F32), ALU.subtract).then_inc(s["r_done"], 1)
                    yield

                def weigh_expert(e):
                    dve.wait_ge(s["oe_b"], at("oe_b", e + 1))
                    dve.wait_ge(s["rb"], at("rb", e + 1))
                    to = tiles_b[:, 2, :] if e == 0 else tiles_b[:, 3, :]
                    dve.tensor_tensor(to, bank[B5][:], tiles_b[:, e % 2, :], ALU.mult).then_inc(s["moe_mul"], 1)
                    dve.wait_ge(s["moe_mul"], at("moe_mul", e + 1))
                    if e:
                        total = dve.tensor_tensor(tiles_b[:, 2, :], tiles_b[:, 2, :], tiles_b[:, 3, :], ALU.add)
                        if e < EM - 1:
                            link(total)
                        else:
                            total.then_inc(s["moe_acc"], 1)

                routing = route()
                for i in range(EM * HC):
                    e, c = divmod(i, HC)
                    if (i + 1) % 2:
                        relu(i + 1)
                    if i < 3:
                        next(routing)
                    if c == 1 and e:
                        weigh_expert(e - 1)
                    yield
                yield
                weigh_expert(EM - 1)
                yield
                yield
                dve.wait_ge(s["mo_t"], at("mo_t", 1))
                flat = x.rearrange("p t d -> p (t d)")
                link(dve.tensor_tensor(flat, bank[B3][:], flat, ALU.add))
                yield from layer_norm(at, link, "moe", ln_b, x, x)
                close()
                if batch[1] == 1:
                    dve.sem_inc(class_b_idle, 1)
                yield
                yield from waits(2)

            two_by_two(dve, NB // 2, l0, ffn, gla, moe)


def waits(n):
    for _ in range(n):
        yield


n_loads = [0]
CONSTS = 13


def host_constants():
    c = {}
    eye = np.eye(P, dtype=np.float32)
    c["ident"] = eye
    c["ramp"] = np.tile(np.arange(EF, 0, -1, dtype=np.float32), (P, 1))
    picks = np.zeros((P, GH + EM + HALF), np.float32)
    for r in range(P):
        if r < 2 * GH:
            picks[r, r % GH] = 1
        if r < 2 * EM:
            picks[r, GH + r % EM] = 1
        if r < PARTS * HALF:
            picks[r, GH + EM + r % HALF] = 1
    c["picks"] = picks
    cut = np.zeros((P, S), np.float32)
    cut[:, S - P:] = np.where(np.arange(P)[None, :] > np.arange(P)[:, None], np.float32(NEG), np.float32(0))
    c["cut_row"] = cut
    j, i = np.arange(P)[:, None], np.arange(P)[None, :]
    masks = [(j == i)]
    for l in range(IN_TILE):
        hs = 1 << l
        masks.append(((j // (2 * hs)) == (i // (2 * hs))) & ((j // hs) % 2 == 0) & ((i // hs) % 2 == 1))
    c["level_mask"] = np.stack(masks, axis=1).astype(np.float32)
    return c


def laid_out(i):
    C = np.ascontiguousarray
    row = lambda v: C(np.broadcast_to(v, (P, v.shape[0])))
    a = {}
    x = i["L0_attn_x"]
    a["x"], a["xT"] = x, C(x.transpose(0, 2, 1))
    for n, m in (("wq0", "Wq"), ("wk0", "Wk"), ("wv0", "Wv"), ("wo0", "Wo")):
        a[n] = C(i[f"L0_attn_{m}"].T)
    a["bv_row"], a["bo_row"] = row(i["L0_attn_bv"]), row(i["L0_attn_bo"])
    a["cols"] = C(np.stack([i["L0_attn_bq"], i["L0_attn_bk"], i["L0_attn_norm_q_w"], i["L0_attn_norm_k_w"]], axis=1))
    for n, m in (("gwq", "wq"), ("gwk", "wk"), ("gwv", "wv"), ("gwo", "wo"), ("gwg1", "wg1"), ("gwg2", "wg2")):
        a[n] = i[f"L1_attn_{m}"]
    a["gn_row"] = row(i["L1_attn_norm_w"])
    for n, m in (("fwq", "w_q"), ("fwk", "w_k")):
        m = i[f"L0_ffn_{m}"].reshape(D, HF, 1, FD)
        a[n] = C(np.broadcast_to(m, (D, HF, 2, FD)).reshape(D, HF, 2 * FD))
    a["fgate"] = i["L0_ffn_w_gate"]
    a["ve"] = C(i["L0_ffn_value_experts"].transpose(2, 0, 1, 3).reshape(D, EF, HF * FD))
    oe = i["L0_ffn_output_experts"].reshape(PAIRS, 2, HF, FD, D)
    a["oe"] = C(oe.transpose(1, 3, 2, 0, 4).reshape(P, HF * PAIRS, D))
    a["w1"] = C(i["L1_ffn_W1"].transpose(1, 0, 2))
    a["w2"] = C(i["L1_ffn_W2"].reshape(EM * HC, P, D).transpose(1, 0, 2))
    a["b1c"] = C(i["L1_ffn_b1"].reshape(EM * HC, P).T)
    a["b2c"] = C(i["L1_ffn_b2"].T)
    a["wr"], a["br_row"] = i["L1_ffn_Wr"], row(i["L1_ffn_br"])
    a.update(host_constants())
    return a


def kernel(**inputs):
    import concourse.bacc as bacc
    from concourse.bass_utils import run_bass_kernel_spmd as run

    arrays = laid_out({k: np.asarray(v) for k, v in inputs.items()})
    nc = bacc.Bacc("TRN2", target_bir_lowering=False, num_devices=1)
    ins = {n: nc.dram_tensor(n + "_in", a.shape, mybir.dt.from_np(a.dtype), kind="ExternalInput").ap() for n, a in arrays.items()}
    out = nc.dram_tensor("out_dram", (B, S, D), F32, kind="ExternalOutput").ap()
    build(nc, ins, out)
    r = run(nc, [{n + "_in": a for n, a in arrays.items()}], core_ids=[0])
    return r.results[0]["out_dram"]
```

```python
from contextlib import ExitStack

import numpy as np
import concourse.bass as bass
from concourse import mybir

F32, BF16, F32R, U32 = mybir.dt.float32, mybir.dt.bfloat16, mybir.dt.float32r, mybir.dt.uint32
ALU, ACT, AX = mybir.AluOpType, mybir.ActivationFunctionType, mybir.AxisListType

B, S, D = 4, 512, 128
P = 128
T = S // P
H0, HD = 16, 8
GROUP = 4
GROUPS = H0 // GROUP
PARTS = 3
PROD_ROWS = PARTS * PARTS * HD
STACK_ROWS = PROD_ROWS + PARTS
VW = 32
SLOTS = GROUP * T + 2
LEAD = SLOTS + 8
RING_A = 4
HF, FD, EF = 8, 64, 8
HE = HF * EF
HALF = HF // 2
GH = HALF * EF
TILES_H = HALF * T
PROJ = [("q", 0), ("k", 0), ("k", 1), ("q", 2), ("k", 2), ("k", 3)]
TAKEN = [2, 3, 4, 6, 7, 8]
PAD = 96
PAIRS = EF // 2
OUT_LAG = 8
NEG = -3.0e38
LEVELS = 9
IN_TILE = 7
PI1, PI2, PI3 = 3.140625, 9.67502593994140625e-4, 1.509957990978376e-7
PI = 3.1415927410125732
F_DOWN, F_UP = 1.1e-7, -1.7e-7
EM, HID = 8, 512
HC = HID // P
RING = 4

A0, A1, A2 = 0, 1, 2
B3, B4, B5, B6, B7 = 3, 4, 5, 6, 7

PER = dict(
    ones_in=1, chan_in=16, tok_in=16, xb=1, proj=3, lin=4, msq=2, rs=4, qk_split=2, q_scr_out=48, k_scr_out=48, stack_in=16 * 4,
    vaug=4, s_out=H0 * T, s_max=H0 * T, m_t=GROUPS, m_rows=GROUPS, m_out=GROUPS * 16, m_in0=16, m_in1=16, m_in2=16,
    m_in3=16, st_out=H0 * T, st_exp=H0 * T, pv=H0 * T, o_sb=GROUPS, o_t=GROUPS, o_norm=GROUPS, at_t=1, at_sb=1,
    attn_y=1, l0_var=1, l0_rs=2, l0_out=1, l0_turn=1, l0_done=1, l0_link=44,
    fp=2 * len(PROJ), fp_hi=2 * HF, fp_lo=2 * HF, gate_p=1, gate_e=1, gate_done=1, gm_t=1, gm_sb=2,
    fs=HF * T, fs_max=HF * T, fm_cut=2, fm_t=2, fm_sb=2, ve=T * EF, ve_first=T, ve_sel=T * (EF - 1), vals_in=T,
    fst=HF * T, fst_exp=HF * T, fst_cut=HF * T, fpv=HF * T, f_ln=HF, f_rec=HF, fo_lo=HF, fo_hi=HF,
    mask=HF * PAIRS, g_in=HF * PAIRS, oe=HF * PAIRS, fo_sb=1, fo_t=1, ffn_var=1, ffn_rs=2, ffn_out=1, ffn_turn=1,
    ffn_done=1, ffn_link=40, ffn_norm_link=1 + T,
    g_proj=4, g_exp=2, g_ln=2, g_sig=2, g_f=1, g_v=1, g_h1=1, lv_in=LEVELS + 1, lv_mm=LEVELS + 1, lv_out=LEVELS + 1, g_o=1,
    gg_p=1, gg_e=3, gn=1, gn_t=1, gn_sb=1, gla_p=1, gla_var=2, gla_rs=4, gla_out=2, gla_turn=1, gla_done=1,
    gla_link=80,
    r_p=1, r_m=1, r_e=1, r_done=1, r_t=1, r_sb=1, w1=EM * HC, relu=EM * HC,
    w2=EM * HC, rb=EM, oe_b=EM, moe_mul=EM, moe_acc=1, mo_t=1, moe_var=1, moe_rs=2, moe_done=1, moe_link=40,
    stored=16,
)
PER_PAIR = dict(ve_in=16, oe_in=16, w1_in=16, w2_in=16)

A_FIRST = 0.929
LN_UNITS = 5
MAX_UNITS = [0.90] * TILES_H + [0.95] * 4
UNIT_TIMES = dict(
    l0=[1.81] * 10 + [1.04] * LEAD + [0.99] * (GROUPS * SLOTS) + [1.01] * (2 + LN_UNITS),
    ffn=[1] + [1.09] * (len(PROJ) + 1) + MAX_UNITS + [0.77] * (T * EF) + [1.57] * 2 + [1.84] * (2 * (TILES_H + OUT_LAG + 1))
    + MAX_UNITS + [1.84] * (2 * (TILES_H + OUT_LAG + 1)) + [1, 1] + [1] * LN_UNITS,
    gla=[1.5] * 3 + [0.75] * 21 + [1.25] + [0.94, 0.94, 0.94, 1.25] * LEVELS + [1.15] * (8 + LN_UNITS),
    moe=[1.85] * 3 + [1.23] * (2 * EM * HC) + [1, 1, 1] + [1] * LN_UNITS,
)


def unit_order(a, b, b_begun, b_kept):
    order, at = [], dict(a=0.0, b=0.0)
    left = dict(a=list(UNIT_TIMES[a]), b=list(UNIT_TIMES[b])[b_begun:len(UNIT_TIMES[b]) - b_kept])
    total = {n: sum(u) for n, u in left.items()}
    while left["a"] or left["b"]:
        turn = "a" if left["a"] and (not left["b"] or at["a"] / total["a"] * A_FIRST <= at["b"] / total["b"]) else "b"
        order.append(turn)
        at[turn] += left[turn].pop(0)
    return order


def alone(name, stage):
    units = sum(1 for _ in stage)
    assert units == len(UNIT_TIMES[name]), (name, units, len(UNIT_TIMES[name]))


def side_by_side(name_a, stage_a, name_b, stage_b, tail=None, keep_tail=False):
    begun = LN_UNITS if tail else 0
    for _ in range(begun):
        next(tail)
        next(stage_b)
    for turn in unit_order(name_a, name_b, begun, LN_UNITS if keep_tail else 0):
        next(stage_a if turn == "a" else stage_b)
    over = [(name_a, stage_a)] if keep_tail else [(name_a, stage_a), (name_b, stage_b)]
    for name, stage in over:
        assert next(stage, None) is None, name
    return stage_b


def two_by_two(eng, pairs, l0, ffn, gla, moe):
    alone("l0", l0((0, 0), first=True))
    with eng.Fori(0, pairs) as p:
        tail = side_by_side("l0", l0((p, 1)), "ffn", ffn((p, 0)), keep_tail=True)
        tail = side_by_side("gla", gla((p, 0)), "ffn", ffn((p, 1)), tail, keep_tail=True)
        side_by_side("gla", gla((p, 1)), "moe", moe((p, 0)), tail)
        with eng.If(p < pairs - 1):
            side_by_side("l0", l0((0, 2)), "moe", moe((0, 1), refill=True))
    alone("moe", moe((pairs - 1, 1)))


def counter(batch):
    pair, which = batch

    def at(name, n):
        if name in PER_PAIR:
            return pair * PER_PAIR[name] + n
        return pair * (2 * PER[name]) + (which * PER[name] + n)
    return at


def build(nc, ins, out):
    nc.disable_value_cache = True
    with ExitStack() as ctx:
        def sb(name, shape, dt=F32):
            return ctx.enter_context(nc.sbuf_tensor(name, shape, dt))

        s = {n: ctx.enter_context(nc.semaphore(n)) for n in [*PER, *PER_PAIR]}
        m_in = [s["m_in0"], s["m_in1"], s["m_in2"], s["m_in3"]]
        first_loaded = ctx.enter_context(nc.semaphore("first_loaded"))
        loaded = ctx.enter_context(nc.semaphore("loaded"))
        const_ready = ctx.enter_context(nc.semaphore("const_ready"))
        passed = ctx.enter_context(nc.semaphore("passed"))
        class_b_idle = ctx.enter_context(nc.semaphore("class_b_idle"))

        bank = [ctx.enter_context(nc.psum_tensor(f"bank{i}", [P, 512], F32)) for i in range(8)]
        q_scr = nc.dram_tensor("q_scr", (PARTS, HD, H0, S), BF16).ap()
        m_scr = nc.dram_tensor("m_scr", (GROUPS, PARTS, GROUP * T, P), BF16).ap()
        k_scr = nc.dram_tensor("k_scr", (PARTS, HD, H0, S), BF16).ap()

        w = {}
        loads = []

        def weight(name, shape, dt=F32):
            t = sb(name, shape, dt)
            w[name] = t
            loads.append((t, ins[name]))

        weight("cols", [P, 4])
        for name in ("wq0", "wk0", "wv0", "bv_row"):
            weight(name, [P, P])
        n_first = len(loads)
        for name in ("ident", "wo0", "bo_row", "gwq", "gwk", "gwv", "gwg1", "gwg2", "gwo", "gn_row"):
            weight(name, [P, P])
        weight("fwq", [P, HF * FD])
        weight("fwk", [P, HF, P])
        weight("fgate", [P, HE])
        weight("b1c", [P, EM * HC])
        weight("b2c", [P, EM])
        weight("wr", [P, EM])
        weight("br_row", [P, EM])
        weight("ramp", [P, EF])
        weight("picks", [P, GH + EM + HALF])
        weight("cut_row", [P, S])
        weight("level_mask", [P, IN_TILE + 1, P])
        pick_wide = sb("pick_wide", [PAD, GH * FD], F32R)
        pick_e = sb("pick_e", [PAD, EM], F32R)
        pick_h = sb("pick_h", [PAD, HALF], BF16)
        ident_b = sb("ident_b", [P, P], BF16)
        ones = sb("ones", [P, P])
        experts = sb("experts", [P, 16 * S])
        w["ve"] = w["w1"] = experts[:, 0:8 * S].rearrange("p (e n) -> p e n", e=EF)
        w["oe"] = w["w2"] = experts[:, 8 * S:].rearrange("p (c n) -> p c n", n=P)
        q_scale = sb("q_scale", [P, 1])
        eps = sb("eps", [P, 2])

        x_tok = sb("x_tok", [P, 2, T, P])
        x_chan = sb("x_chan", [P, 2, S])

        ln_a = dict(st=sb("ln_st_a", [P, T, 6]), mv=sb("ln_mv_a", [P, T, 2]), r=sb("ln_r_a", [P, 2, T]))
        vaug = sb("vaug", [P, T, H0, VW])
        tiles_a = sb("tiles_a", [P, 6, S])
        region = sb("region", [P, 16 * S])
        stack = region[:, :].bitcast(BF16).rearrange("r (n h s) -> r n h s", n=2, h=H0)
        probs_a = sb("probs_a", [P, RING_A, S])
        parts = probs_a[:, 0:PARTS, :].bitcast(BF16).rearrange("p n s -> p (n s)").rearrange("p (n c s) -> p n c s", n=2, c=PARTS)
        m_tok = sb("m_tok", [P, H0 * T])
        m_row = sb("m_row", [GROUP * T, GROUPS, PARTS, P], BF16)
        m_rest = sb("m_rest", [P, 2, P])
        heads_out = tiles_a[:, 0, :].rearrange("p (t d) -> p t d", t=T)
        gla_tiles = region[:].rearrange("p (n s) -> p n s", s=S)
        q_lv, k_lv = (gla_tiles[:, 0:2], gla_tiles[:, 2:4]), (gla_tiles[:, 4:6], gla_tiles[:, 6:8])
        qc, kc, pre, suf, at_diag, v_tok = (gla_tiles[:, 8:10], gla_tiles[:, 10:12], gla_tiles[:, 12], gla_tiles[:, 13],
                                            gla_tiles[:, 14], gla_tiles[:, 15])
        at_far, at_near, h1T = probs_a[:, 0], probs_a[:, 1, 0:2 * P], probs_a[:, 2]

        ln_b = dict(st=sb("ln_st_b", [P, T, 6]), mv=sb("ln_mv_b", [P, T, 2]), r=sb("ln_r_b", [P, 2, T]))
        tiles_b = sb("tiles_b", [P, 6, S])
        probs_b = sb("probs_b", [P, RING, S])
        f_q = sb("f_q", [P, HALF, S], F32R)
        f_k = sb("f_k", [P, HALF, 2, S], F32R)
        vals = sb("vals", [P, T, HF, P])
        gm_tok = sb("gm_tok", [P, T, 2, 2, GH], F32R)
        gmT = sb("gmT", [PAD, 2, S], F32R)
        oh = sb("oh", [P, T * HF, EF])
        gs = tiles_b[:, 3:5].rearrange("p a b -> p (a b)")[:, 0:3 * T * HE].rearrange("p (n c) -> p n c", n=3)
        gsm = sb("gsm", [P, 2, T * HF])
        fm_tok = sb("fm_tok", [P, T, HF])
        fm_parts = sb("fm_parts", [P, T, PARTS, HALF], BF16)
        fm_rest = sb("fm_rest", [P, T, HALF])
        fmT = sb("fmT", [PAD, S], BF16)
        rT = sb("rT", [PAD, S], F32R)
        r_tok = sb("r_tok", [P, T, 2, EM], F32R)
        rt = sb("rt", [P, 6, T, EM])
        rt1 = sb("rt1", [P, 4, T])

        all_loaded = 16 * (len(loads) - n_first)
        block = ctx.enter_context(nc.Block())

        @block.sync
        def _(sp):

            def number(batch):
                return batch[0] * 2 + batch[1]

            def load_channels(b):
                sp.dma_start(x_chan[:, b % 2], ins["xT"][b]).then_inc(s["chan_in"], 16)

            def l0(batch, first=False):
                at, par, b = counter(batch), batch[1] % 2, number(batch)
                if first:
                    load_channels(0)
                src = ins["x"][bass.ds(b, 1)].rearrange("o (t p) d -> p (o t) d", p=P)
                sp.dma_start(x_tok[:, par], src).then_inc(s["tok_in"], 16)
                if first:
                    for t, src in loads[:n_first]:
                        sp.dma_start(t[:], src).then_inc(first_loaded, 16)
                    for t, src in loads[n_first:]:
                        sp.dma_start(t[:], src).then_inc(loaded, 16)
                yield from waits(4)
                for n, scr in enumerate((q_scr, k_scr)):
                    sp.wait_ge(s["qk_split"], at("qk_split", n + 1))
                    for c in range(PARTS):
                        sp.dma_start(scr[c].rearrange("d h s -> h d s"), parts[:, n, c, :]).then_inc(s["q_scr_out" if n == 0 else "k_scr_out"], 16)
                    yield
                sp.wait_ge(s["q_scr_out"], at("q_scr_out", 48))
                for c in range(PARTS):
                    dst = stack[PARTS * HD * c:PARTS * HD * (c + 1), 0].rearrange("r h s -> r (h s)")
                    src = q_scr[c].rearrange("d h s -> d (h s)").unsqueeze(0).to_broadcast([PARTS, HD, H0 * S])
                    sp.dma_start(dst, src).then_inc(s["stack_in"], 16)
                yield
                sp.wait_ge(s["k_scr_out"], at("k_scr_out", 48))
                sp.wait_ge(s["ones_in"], at("ones_in", 1))
                src = k_scr.rearrange("c d h s -> (c d) (h s)").unsqueeze(0).to_broadcast([PARTS, PARTS * HD, H0 * S])
                sp.dma_start(stack[0:PROD_ROWS, 1].rearrange("r h s -> r (h s)"), src).then_inc(s["stack_in"], 16)
                yield
                if first:
                    sp.dma_start(experts[:, 0:8 * S], ins["ve"].rearrange("p e n -> p (e n)")).then_inc(s["ve_in"], 16)
                    sp.dma_start(experts[:, 8 * S:], ins["oe"].rearrange("p c n -> p (c n)")).then_inc(s["oe_in"], 16)
                    load_channels(1)
                for _ in range(2):
                    yield
                for u in range(GROUPS * SLOTS + LEAD):
                    g, i = divmod(u, SLOTS)
                    if i == SLOTS - 1 and g < GROUPS:
                        sp.wait_ge(s["m_rows"], at("m_rows", g + 1))
                        sp.dma_start(m_scr[g].rearrange("c r p -> r c p"), m_row[:, g]).then_inc(s["m_out"], 16)
                    if i == 2 and 0 < g <= GROUPS:
                        g -= 1
                        sp.wait_ge(s["m_out"], at("m_out", 16 * (g + 1)))
                        sp.dma_start(stack[PROD_ROWS:STACK_ROWS, 0, GROUP * g:GROUP * (g + 1), :].rearrange("c h s -> c (h s)"),
                                     m_scr[g].rearrange("c r p -> c (r p)")).then_inc(m_in[g], 16)
                    yield
                yield from waits(2 + LN_UNITS)

            def ffn(batch):
                at = counter(batch)
                valued = 2 + len(PROJ) + len(MAX_UNITS) + T * EF
                yield from waits(valued)
                if batch[1]:
                    sp.wait_ge(s["ve"], at("ve", T * EF))
                    sp.dma_start(experts[:, 0:8 * S], ins["w1"].rearrange("p e n -> p (e n)")).then_inc(s["w1_in"], 16)
                yield from waits(len(UNIT_TIMES["ffn"]) - valued - LN_UNITS - 2)
                if batch[1]:
                    sp.wait_ge(s["oe"], at("oe", HF * PAIRS))
                    sp.dma_start(experts[:, 8 * S:], ins["w2"].rearrange("p c n -> p (c n)")).then_inc(s["w2_in"], 16)
                yield from waits(2 + LN_UNITS)

            def gla(batch):
                for _ in range(len(UNIT_TIMES["gla"])):
                    yield

            def moe(batch, refill=False):
                at, par, b = counter(batch), batch[1] % 2, number(batch)
                tail = 3 + LN_UNITS
                yield from waits(len(UNIT_TIMES["moe"]) - tail)
                sp.wait_ge(s["w1"], at("w1", EM * HC))
                sp.sem_inc(passed, 1)
                if refill:
                    load_channels(batch[1] + 2)
                    sp.wait_ge(s["w2"], at("w2", EM * HC))
                    sp.dma_start(experts[:, 0:8 * S], ins["ve"].rearrange("p e n -> p (e n)")).then_inc(s["ve_in"], 16)
                    sp.dma_start(experts[:, 8 * S:], ins["oe"].rearrange("p c n -> p (c n)")).then_inc(s["oe_in"], 16)
                elif batch[1] == 0:
                    with sp.If(batch[0] < B // 2 - 1):
                        load_channels(2)
                yield from waits(tail - 1)
                sp.wait_ge(s["moe_done"], at("moe_done", 1))
                dst = out[bass.ds(b, 1)].rearrange("o (t p) d -> p (o t) d", p=P)
                sp.dma_start(dst, x_tok[:, par]).then_inc(s["stored"], 16)
                sp.wait_ge(s["stored"], at("stored", 16))
                sp.sem_inc(passed, 1)
                yield

            two_by_two(sp, B // 2, l0, ffn, gla, moe)

        def mask_bank(half, u):
            return B5 if half and u > TILES_H and (u - TILES_H) % 2 else B3

        def proj_bank(half, i):
            return (B5, B4)[i % 2] if half else B3 + i % 3

        def early_proj(half, u):
            i = u - TILES_H - 1
            return i if half == 0 and 0 <= i < len(PROJ) else None

        def s_bank(batch, first, u, n):
            if first:
                return B3 + n % 3, n - 2
            if batch[1] == 2:
                return (A0, B7)[n % 2], n - 1
            return (A0 + n % 2, n - 1) if u < LEAD - 1 else (A0, n)

        def st_bank(first, j):
            return ((A1, B6)[j % 2], j - 1) if first else (A1, j)

        def turn_bank(first):
            return B7 if first else A1

        def class_a_free(eng, stage, batch):
            pair, which = batch
            if stage == "l0":
                if which == 1:
                    eng.wait_ge(s["l0_done"], counter((pair, 0))("l0_done", 1))
                elif which == 2:
                    eng.wait_ge(s["gla_done"], counter((pair, 1))("gla_done", 1))
            elif which == 0:
                eng.wait_ge(s["l0_done"], counter((pair, 1))("l0_done", 1))
                eng.wait_ge(s["ffn_done"], counter((pair, 0))("ffn_done", 1))
            else:
                eng.wait_ge(s["gla_done"], counter((pair, 0))("gla_done", 1))
                eng.wait_ge(s["ffn_done"], counter((pair, 1))("ffn_done", 1))

        def class_b_free(eng, stage, batch):
            pair, which = batch
            if stage == "ffn":
                eng.wait_ge(s["l0_done"], counter(batch)("l0_done", 1))
                if which == 0:
                    eng.wait_ge(class_b_idle, pair + 1)
                else:
                    eng.wait_ge(s["ffn_var"], counter((pair, 0))("ffn_var", 1))
            else:
                eng.wait_ge(s["gla_done"], counter(batch)("gla_done", 1))
                if which == 0:
                    eng.wait_ge(s["ffn_var"], counter((pair, 1))("ffn_var", 1))
                else:
                    eng.wait_ge(s["moe_done"], counter((pair, 0))("moe_done", 1))

        @block.gpsimd
        def _(pool):
            pool.memset(ones[:], 1.0).then_inc(const_ready, 1)
            pool.memset(vaug[:], 1.0).then_inc(const_ready, 1)
            pool.memset(fmT[:], 0.0).then_inc(const_ready, 1)
            pool.memset(rT[:].bitcast(U32), 0).then_inc(const_ready, 1)
            pool.memset(gmT[:].bitcast(U32), 0).then_inc(const_ready, 1)
            pool.memset(eps[:, 0:1], 1e-6).then_inc(const_ready, 1)
            pool.memset(eps[:, 1:2], 1e-5).then_inc(const_ready, 1)
            pool.memset(vals[:, :, :, FD:P], 1.0).then_inc(const_ready, 1)
            pool.wait_ge(const_ready, POOL_CONSTS + 1)
            pool.sem_inc(class_b_idle, 1)

            def l0(batch, first=False):
                at, par = counter(batch), batch[1] % 2
                class_a_free(pool, "l0", batch)
                pool.sem_inc(passed, 1)
                pool.memset(stack[64:STACK_ROWS, 1], 1.0).then_inc(s["ones_in"], 1)
                pool.wait_ge(s["ones_in"], at("ones_in", 1))
                pool.wait_ge(s["tok_in"], at("tok_in", 16))
                if first:
                    pool.wait_ge(loaded, all_loaded)
                pool.tensor_tensor(x_tok[:, par], x_tok[:, par], w["bo_row"][:].unsqueeze(1).to_broadcast([P, T, P]), ALU.add).then_inc(s["xb"], 1)
                for _ in range(len(UNIT_TIMES["l0"])):
                    yield

            def ffn(batch):
                at = counter(batch)
                class_b_free(pool, "ffn", batch)
                yield from waits(2 + len(PROJ) + len(MAX_UNITS))
                for i in range(T * EF):
                    t, e = divmod(i, EF)
                    if e == EF - 1:
                        v, heads = vals[:, t, :, 0:FD], slice(t * HF, (t + 1) * HF)
                        pool.wait_ge(s["ve_sel"], at("ve_sel", (t + 1) * (EF - 1)))
                        pool.tensor_tensor(v, v, gsm[:, 0, heads].unsqueeze(2).to_broadcast([P, HF, FD]), ALU.mult).then_inc(s["vals_in"], 1)
                    yield
                yield from waits(2)
                for half in range(2):
                    if half:
                        yield from waits(len(MAX_UNITS))
                    for u in range(TILES_H + OUT_LAG + 1):
                        if u < TILES_H:
                            j = TILES_H * half + u
                            pool.wait_ge(s["fst_exp"], at("fst_exp", j + 1))
                            pool.sem_inc(passed, 1)
                            pool.affine_select(out=probs_b[:, j % RING, 0:P], in_=probs_b[:, j % RING, 0:P],
                                               compare_op=ALU.is_ge, fill=0.0, base=0, pattern=[[1, P]],
                                               channel_multiplier=-1).then_inc(s["fst_cut"], 1)
                        yield
                        yield
                yield from waits(2 + LN_UNITS)

            def gla(batch):
                yield from waits(len(UNIT_TIMES["gla"]))

            def moe(batch, refill=False):
                yield from waits(len(UNIT_TIMES["moe"]))

            two_by_two(pool, B // 2, l0, ffn, gla, moe)

        @block.tensor
        def _(pe):
            pe.wait_ge(first_loaded, 16 * n_first)
            pe.wait_ge(const_ready, POOL_CONSTS + 1)

            def mm(o, l, r, start=True, stop=True):
                return pe.matmul(o, lhsT=l, rhs=r, start=start, stop=stop, skip_group_check=True)

            def turn_tiles(dst, src):
                for t in range(T):
                    last = pe.transpose(dst[:, t * P:(t + 1) * P], src(t), w["ident"][:])
                return last

            def l0(batch, first=False):
                at, par = counter(batch), batch[1] % 2
                xT = x_chan[:, par]
                class_a_free(pe, "l0", batch)
                pe.wait_ge(s["chan_in"], at("chan_in", 16))
                mm(bank[A0][:], w["wq0"][:], xT).then_inc(s["proj"], 1)
                mm(bank[A1][:], w["wk0"][:], xT).then_inc(s["proj"], 1)
                yield
                for t in range(T):
                    last = mm(bank[A2][:, t * P:(t + 1) * P], xT[:, t * P:(t + 1) * P], w["wv0"][:])
                last.then_inc(s["proj"], 1)
                yield
                for n in range(2):
                    pe.wait_ge(s["lin"], at("lin", 2 * n + 2))
                    mm(bank[A0 + n][:], ones[:], tiles_a[:, 2 + n, :]).then_inc(s["msq"], 1)
                    yield
                yield from waits(5)
                if first:
                    pe.wait_ge(loaded, all_loaded)
                    pe.wait_ge(const_ready, CONSTS)
                pe.wait_ge(s["stack_in"], at("stack_in", 64))
                pe.wait_ge(s["vaug"], at("vaug", 4))
                pe.wait_ge(s["rs"], at("rs", 2))
                yield
                for u in range(LEAD + GROUPS * SLOTS):
                    g, i = divmod(u, SLOTS)
                    if g < GROUPS and i < GROUP * T:
                        n = g * GROUP * T + i
                        h, t = divmod(n, T)
                        to, gone = s_bank(batch, first, u, n)
                        if gone > 0:
                            pe.wait_ge(s["s_max"], at("s_max", gone))
                        if i == 0 and g and not first:
                            pe.wait_ge(s["m_rows"], at("m_rows", g))
                        mm(bank[to][:], stack[0:PROD_ROWS, 0, h, t * P:(t + 1) * P],
                           stack[0:PROD_ROWS, 1, h, :]).then_inc(s["s_out"], 1)
                    elif g < GROUPS and i == GROUP * T:
                        pe.wait_ge(s["s_max"], at("s_max", GROUP * T * (g + 1)))
                        if g:
                            pe.wait_ge(s["m_rows"], at("m_rows", g))
                        pe.transpose(bank[A0][0:GROUP * T, 0:P], m_tok[:, GROUP * T * g:GROUP * T * (g + 1)],
                                     w["ident"][:]).then_inc(s["m_t"], 1)
                    if u >= LEAD:
                        g, i = divmod(u - LEAD, SLOTS)
                        j = g * GROUP * T + i
                        if i == 0:
                            pe.wait_ge(m_in[g], at(f"m_in{g}", 16))
                            if g and not first:
                                pe.wait_ge(s["o_norm"], at("o_norm", g))
                        if i < GROUP * T:
                            h, kt = GROUP * g + i % GROUP, i // GROUP
                            to, gone = st_bank(first, j)
                            if gone > 0:
                                pe.wait_ge(s["st_exp"], at("st_exp", gone))
                            elif not first:
                                pe.wait_ge(s["s_max"], at("s_max", LEAD - 2))
                            mm(bank[to][:], stack[0:STACK_ROWS, 1, h, kt * P:(kt + 1) * P],
                               stack[0:STACK_ROWS, 0, h, :]).then_inc(s["st_out"], 1)
                        if 1 <= i <= GROUP * T:
                            hh, kt = (i - 1) % GROUP, (i - 1) // GROUP
                            pe.wait_ge(s["st_exp"], at("st_exp", j))
                            if i == 1 and g:
                                pe.wait_ge(s["o_sb"], at("o_sb", g))
                            mm(bank[A2][32 * hh:32 * (hh + 1), :], vaug[:, kt, GROUP * g + hh, :], probs_a[:, (j - 1) % RING_A, :],
                               start=(kt == 0), stop=(kt == T - 1)).then_inc(s["pv"], 1)
                        if i == SLOTS - 1:
                            pe.wait_ge(s["o_sb"], at("o_sb", g + 1))
                            if g and first:
                                pe.wait_ge(s["o_norm"], at("o_norm", g))
                            turn_tiles(bank[turn_bank(first)], lambda t: tiles_a[:, 4 + g % 2, t * P:(t + 1) * P]).then_inc(s["o_t"], 1)
                    yield
                pe.wait_ge(s["o_norm"], at("o_norm", GROUPS))
                turn_tiles(bank[A0], lambda t: heads_out[:, t, :]).then_inc(s["at_t"], 1)
                yield
                pe.wait_ge(s["at_sb"], at("at_sb", 1))
                for t in range(T):
                    last = mm(bank[A1][:, t * P:(t + 1) * P], tiles_a[:, 1, t * P:(t + 1) * P], w["wo0"][:])
                last.then_inc(s["attn_y"], 1)
                yield
                yield from waits(3)
                pe.wait_ge(s["l0_out"], at("l0_out", 1))
                turn_tiles(bank[A0], lambda t: x_tok[:, par, t, :]).then_inc(s["l0_turn"], 1)
                yield
                yield

            def ffn(batch):
                at, par = counter(batch), batch[1] % 2
                xT = x_chan[:, par]
                class_b_free(pe, "ffn", batch)
                for t in range(T):
                    last = mm(bank[B5][:, t * HE:(t + 1) * HE], xT[:, t * P:(t + 1) * P], w["fgate"][:])
                last.then_inc(s["gate_p"], 1)
                yield

                def project(half, i):
                    what, h = PROJ[i]
                    depth = 2 if half else 3
                    if i >= depth:
                        pe.wait_ge(s["fp_lo"], at("fp_lo", 2 * HALF * half + TAKEN[i - depth]))
                    elif half and i == 1:
                        pe.wait_ge(s["fo_lo"], at("fo_lo", HALF - 1))
                    elif half == 0 and i == 2:
                        pe.wait_ge(s["gate_e"], at("gate_e", 1))
                    h += HALF * half
                    mm(bank[proj_bank(half, i)][:], w["fwk"][:, h, :] if what == "k" else w["fwq"][:, h * FD:(h + 2) * FD],
                       xT).then_inc(s["fp"], 1)

                def mask_rows(half, u, c):
                    if u >= TILES_H + OUT_LAG:
                        return
                    if u == OUT_LAG and half:
                        pe.wait_ge(s["fs_max"], at("fs_max", TILES_H * 2))
                    if half and u > TILES_H:
                        pe.wait_ge(s["g_in"], at("g_in", c - 1))
                    elif c:
                        pe.wait_ge(s["g_in"], at("g_in", c))
                    chunk = c % (HALF * PAIRS)
                    mm(bank[mask_bank(half, u)][:], pick_wide[:, P * chunk:P * (chunk + 1)], gmT[:, half]).then_inc(s["mask"], 1)

                for i in range(len(PROJ)):
                    project(0, i)
                    yield
                yield
                for half in range(2):
                    if half:
                        pe.wait_ge(s["g_in"], at("g_in", HALF * PAIRS))
                        pe.wait_ge(s["fo_lo"], at("fo_lo", HALF))
                    for u in range(TILES_H):
                        i = TILES_H * half + u
                        hh, t = divmod(u, T)
                        n = (t + 1) * P
                        if u < 3:
                            pe.wait_ge(s["fp_lo"], at("fp_lo", 2 * HALF * (half + 1)))
                        else:
                            pe.wait_ge(s["fs_max"], at("fs_max", i - 2))
                        mm(bank[B3 + u % 3][:, 0:n], f_q[:, hh, t * P:n], f_k[:, hh, 0, 0:n], True, False)
                        mm(bank[B3 + u % 3][:, 0:n], f_q[:, hh, t * P:n], f_k[:, hh, 1, 0:n], False, True).then_inc(s["fs"], 1)
                        yield
                    yield from waits(2)
                    pe.wait_ge(s["fm_cut"], at("fm_cut", half + 1))
                    for t in range(T):
                        last = pe.transpose(bank[B5][:].bitcast(BF16)[0:PARTS * HALF, t * P:(t + 1) * P],
                                            fm_parts[:, t].rearrange("p a c -> p (a c)"), ident_b[:])
                    last.then_inc(s["fm_t"], 1)
                    yield
                    pe.wait_ge(s["fm_sb"], at("fm_sb", half + 1))
                    if half == 0:
                        pe.wait_ge(s["gate_done"], at("gate_done", 1))
                        turn_tiles(bank[B5], lambda t: gm_tok[:, t].rearrange("p h a c -> p (h a c)").bitcast(F32)).then_inc(s["gm_t"], 1)
                    yield
                    if half == 0:
                        pe.wait_ge(s["ve_in"], at("ve_in", 16))
                        for i in range(T * EF):
                            t, e = divmod(i, EF)
                            if i == 2:
                                pe.wait_ge(s["gm_sb"], at("gm_sb", 2))
                            if i >= 3:
                                o = i - 3
                                if o % EF == 0:
                                    pe.wait_ge(s["ve_first"], at("ve_first", o // EF + 1))
                                else:
                                    pe.wait_ge(s["ve_sel"], at("ve_sel", o // EF * (EF - 1) + o % EF))
                            mm(bank[B3 + i % 3][:], xT[:, t * P:(t + 1) * P], w["ve"][:, e, :]).then_inc(s["ve"], 1)
                            yield
                        yield
                        pe.wait_ge(s["vals_in"], at("vals_in", T))
                        pe.wait_ge(s["oe_in"], at("oe_in", 16))
                        yield
                    for u in range(TILES_H + OUT_LAG + 1):
                        c = HALF * PAIRS * half + u - OUT_LAG
                        if u < TILES_H:
                            hh, kt = divmod(u, T)
                            j, n = TILES_H * half + u, S - kt * P
                            if u:
                                pe.wait_ge(s["fst_exp"], at("fst_exp", j))
                            elif half == 0:
                                pe.wait_ge(s["gm_sb"], at("gm_sb", 2))
                            o = bank[B5][:, 0:n]
                            mm(o, f_k[:, hh, 0, kt * P:(kt + 1) * P], f_q[:, hh, kt * P:S], True, False)
                            mm(o, f_k[:, hh, 1, kt * P:(kt + 1) * P], f_q[:, hh, kt * P:S], False, False)
                            mm(o, pick_h[:, hh:hh + 1].to_broadcast([PAD, P]), fmT[:, kt * P:S], False, True).then_inc(s["fst"], 1)
                        if half and u > TILES_H:
                            mask_rows(half, u, c)
                        if u > OUT_LAG:
                            if c == 1 and batch[1] == 1:
                                pe.wait_ge(s["ffn_done"], counter((batch[0], 0))("ffn_done", 1))
                            pe.wait_ge(s["g_in"], at("g_in", c))
                            mm(bank[B7][:], w["oe"][:, c - 1, :], tiles_b[:, (c - 1) % 2, :], c == 1, c == HF * PAIRS).then_inc(s["oe"], 1)
                        if half == 0 and u > TILES_H:
                            mask_rows(half, u, c)
                        yield
                        if OUT_LAG <= u <= TILES_H:
                            mask_rows(half, u, c)
                        if early_proj(half, u) is not None:
                            project(1, early_proj(half, u))
                        if 1 <= u <= TILES_H:
                            hh, kt = divmod(u - 1, T)
                            h, j = HALF * half + hh, TILES_H * half + u - 1
                            if kt == 0 and hh >= 2:
                                pe.wait_ge(s["fo_lo"], at("fo_lo", h - 1))
                            elif u == 1:
                                pe.wait_ge(s["fs_max"], at("fs_max", TILES_H * (half + 1)))
                            pe.wait_ge(s["fst_cut"], at("fst_cut", j + 1))
                            mm(bank[B4 + 2 * (h % 2)][:, kt * P:S], vals[:, kt, h, :], probs_b[:, j % RING, 0:S - kt * P],
                               kt == 0, kt == T - 1).then_inc(s["fpv"], 1)
                        yield
                yield
                pe.wait_ge(s["fo_sb"], at("fo_sb", 1))
                turn_tiles(bank[B5], lambda t: tiles_b[:, 5, t * P:(t + 1) * P]).then_inc(s["fo_t"], 1)
                yield
                yield from waits(3)
                pe.wait_ge(s["ffn_out"], at("ffn_out", 1))
                turn_tiles(bank[B7], lambda t: x_tok[:, par, t, :]).then_inc(s["ffn_turn"], 1)
                yield
                yield

            def gla(batch):
                at, par = counter(batch), batch[1] % 2
                xT = x_chan[:, par]
                class_a_free(pe, "gla", batch)
                mm(bank[A0][:], w["gwq"][:], xT).then_inc(s["g_proj"], 1)
                mm(bank[A1][:], w["gwk"][:], xT).then_inc(s["g_proj"], 1)
                mm(bank[A2][:], w["gwg1"][:], xT).then_inc(s["g_proj"], 1)
                yield
                pe.wait_ge(s["g_h1"], at("g_h1", 1))
                for t in range(T):
                    last = mm(bank[A2][:, t * P:(t + 1) * P], xT[:, t * P:(t + 1) * P], w["gwv"][:])
                last.then_inc(s["g_proj"], 1)
                yield
                pe.wait_ge(s["g_v"], at("g_v", 1))
                for t in range(T):
                    last = mm(bank[A2][:, t * P:(t + 1) * P], h1T[:, t * P:(t + 1) * P], w["gwg2"][:])
                last.then_inc(s["gg_p"], 1)
                yield
                yield from waits(21)
                for lv in range(LEVELS + 1):
                    if lv:
                        yield from waits(3)
                    pe.wait_ge(s["lv_in"], at("lv_in", lv + 1))
                    if lv >= 2:
                        pe.wait_ge(s["lv_out"], at("lv_out", lv - 1))
                    q, k = (qc, kc) if lv == 0 else (q_lv[lv % 2], k_lv[lv % 2])
                    if lv <= IN_TILE:
                        blocks = [(c * P, c * P, P, c * P) for c in range(T)]
                    elif lv == IN_TILE + 1:
                        blocks = [(0, P, P, 0), (2 * P, 3 * P, P, P)]
                    else:
                        blocks = [(0, 2 * P, 2 * P, 0), (P, 2 * P, 2 * P, 2 * P)]
                    for j0, i0, n, o in blocks:
                        for c in range(2):
                            last = mm(bank[A0 + lv % 2][:, o:o + n], k[:, c, j0:j0 + P], q[:, c, i0:i0 + n], c == 0, c == 1)
                    last.then_inc(s["lv_mm"], 1)
                    yield
                yield
                pe.wait_ge(s["lv_out"], at("lv_out", LEVELS + 1))
                pe.wait_ge(s["gg_e"], at("gg_e", 1))
                for i in range(T):
                    for j in range(i + 1):
                        if i == j:
                            a = at_diag[:, i * P:(i + 1) * P]
                        elif i // 2 == j // 2:
                            a = at_near[:, (i // 2) * P:(i // 2 + 1) * P]
                        else:
                            a = at_far[:, 2 * P * j + (i - 2) * P:2 * P * j + (i - 1) * P]
                        last = mm(bank[A2][:, i * P:(i + 1) * P], a, v_tok[:, j * P:(j + 1) * P], j == 0, j == i)
                last.then_inc(s["g_o"], 1)
                yield
                yield from waits(3)
                pe.wait_ge(s["gn"], at("gn", 1))
                turn_tiles(bank[A0], lambda t: tiles_a[:, 3, t * P:(t + 1) * P]).then_inc(s["gn_t"], 1)
                yield
                yield
                pe.wait_ge(s["gn_sb"], at("gn_sb", 1))
                for t in range(T):
                    last = mm(bank[A1][:, t * P:(t + 1) * P], tiles_a[:, 0, t * P:(t + 1) * P], w["gwo"][:])
                last.then_inc(s["gla_p"], 1)
                yield
                yield from waits(3)
                pe.wait_ge(s["gla_out"], at("gla_out", 2))
                turn_tiles(bank[A0], lambda t: x_tok[:, par, t, :]).then_inc(s["gla_turn"], 1)
                yield
                yield

            def moe(batch, refill=False):
                at, par = counter(batch), batch[1] % 2
                xT = x_chan[:, par]
                class_b_free(pe, "moe", batch)
                for t in range(T):
                    last = mm(bank[B5][:, t * EM:(t + 1) * EM], xT[:, t * P:(t + 1) * P], w["wr"][:])
                last.then_inc(s["r_p"], 1)
                yield

                def up(i):
                    if i >= 2:
                        pe.wait_ge(s["relu"], at("relu", i - 1))
                    mm(bank[B3 + i % 2][:], w["w1"][:, i // HC, (i % HC) * P:(i % HC + 1) * P], xT).then_inc(s["w1"], 1)

                def rows(e):
                    if e == 0:
                        pe.wait_ge(s["r_sb"], at("r_sb", 1))
                    else:
                        pe.wait_ge(s["moe_mul"], at("moe_mul", e))
                    mm(bank[B5][:], pick_e[:, e:e + 1].to_broadcast([PAD, P]), rT[:]).then_inc(s["rb"], 1)

                pe.wait_ge(s["w1_in"], at("w1_in", 16))
                up(0)
                yield
                pe.wait_ge(s["w2_in"], at("w2_in", 16))
                yield
                for i in range(EM * HC):
                    e, c = divmod(i, HC)
                    if i + 1 < EM * HC:
                        up(i + 1)
                    yield
                    pe.wait_ge(s["relu"], at("relu", i + 1))
                    if c == 0 and e:
                        pe.wait_ge(s["oe_b"], at("oe_b", e))
                    mm(bank[B6][:], w["w2"][:, i, :], probs_b[:, i % RING, :], c == 0, c == HC - 1).then_inc(s["w2"], 1)
                    if i == 3:
                        pe.wait_ge(s["r_done"], at("r_done", 1))
                        for t in range(T):
                            last = pe.transpose(bank[B5][0:2 * EM, t * P:(t + 1) * P],
                                                r_tok[:, t].rearrange("p a c -> p (a c)").bitcast(F32), w["ident"][:])
                        last.then_inc(s["r_t"], 1)
                    if c == 0 and e:
                        rows(e - 1)
                    yield
                rows(EM - 1)
                yield
                yield
                pe.wait_ge(s["moe_acc"], at("moe_acc", 1))
                turn_tiles(bank[B3], lambda t: tiles_b[:, 2, t * P:(t + 1) * P]).then_inc(s["mo_t"], 1)
                yield
                yield from waits(LN_UNITS)

            two_by_two(pe, B // 2, l0, ffn, gla, moe)

        @block.scalar
        def _(act):
            act.preload_act_table_set("natural_log_exp_and_others")
            act.wait_ge(first_loaded, 16 * n_first)
            act.wait_ge(const_ready, POOL_CONSTS + 1)

            def rstd_rows(at, stage, ln, n=1):
                act.wait_ge(s[stage + "_var"], at(stage + "_var", n))
                act.activation(ln["r"][:, 0, :], ln["mv"][:, :, 1], ACT.Ln, bias=eps[:, 1:2]).then_inc(s[stage + "_rs"], 1)
                act.wait_ge(s[stage + "_rs"], at(stage + "_rs", 2 * n - 1))
                act.activation(ln["r"][:, 1, :], ln["r"][:, 0, :], ACT.Exp, scale=-0.5).then_inc(s[stage + "_rs"], 1)

            def l0(batch, first=False):
                at, par = counter(batch), batch[1] % 2
                class_a_free(act, "l0", batch)
                for n in range(2):
                    act.wait_ge(s["proj"], at("proj", n + 1))
                    act.activation(tiles_a[:, n, :], bank[A0 + n][:], ACT.Identity, bias=w["cols"][:, n:n + 1]).then_inc(s["lin"], 1)
                    act.activation(tiles_a[:, 2 + n, :], bank[A0 + n][:], ACT.Square, bias=w["cols"][:, n:n + 1]).then_inc(s["lin"], 1)
                    yield
                for n in range(2):
                    act.wait_ge(s["msq"], at("msq", n + 1))
                    act.activation(tiles_a[:, 4 + n, :], bank[A0 + n][:], ACT.Ln, bias=eps[:, 0:1], scale=1.0 / D).then_inc(s["rs"], 1)
                    if n:
                        for m in range(2):
                            act.wait_ge(s["rs"], at("rs", 2))
                            act.activation(tiles_a[:, 2 + m, :], tiles_a[:, 4 + m, :], ACT.Exp, scale=-0.5).then_inc(s["rs"], 1)
                    yield
                yield from waits(6)
                if first:
                    act.wait_ge(loaded, all_loaded)
                for u in range(LEAD + GROUPS * SLOTS):
                    if u >= LEAD:
                        g, i = divmod(u - LEAD, SLOTS)
                        j = g * GROUP * T + i
                        if i < GROUP * T:
                            act.wait_ge(s["st_out"], at("st_out", j + 1))
                            if j >= RING_A:
                                act.wait_ge(s["pv"], at("pv", j - RING_A + 1))
                            act.activation(probs_a[:, j % RING_A, :], bank[st_bank(first, j)[0]][:], ACT.Exp).then_inc(s["st_exp"], 1)
                        if i == GROUP * T:
                            act.wait_ge(s["pv"], at("pv", GROUP * T * (g + 1)))
                            act.activation(tiles_a[:, 4 + g % 2, :], bank[A2][:], ACT.Copy).then_inc(s["o_sb"], 1)
                    yield
                act.wait_ge(s["at_t"], at("at_t", 1))
                act.activation(tiles_a[:, 1, :], bank[A0][:], ACT.Copy).then_inc(s["at_sb"], 1)
                yield
                yield
                yield
                rstd_rows(at, "l0", ln_a)
                yield
                yield from waits(2)
                act.wait_ge(s["l0_turn"], at("l0_turn", 1))
                act.activation(x_chan[:, par], bank[A0][:], ACT.Copy).then_inc(s["l0_done"], 1)
                yield

            def ffn(batch):
                at, par = counter(batch), batch[1] % 2
                class_b_free(act, "ffn", batch)
                act.wait_ge(s["gate_p"], at("gate_p", 1))
                act.activation(gs[:, 0, :], bank[B5][:, 0:T * HE], ACT.Exp, scale=-1.0).then_inc(s["gate_e"], 1)
                yield
                def round_proj(half, i):
                    what, h = PROJ[i]
                    src = bank[proj_bank(half, i)]
                    act.wait_ge(s["fp"], at("fp", len(PROJ) * half + i + 1))
                    if what == "q":
                        for k in range(2):
                            rows = slice(FD * k, FD * (k + 1))
                            act.activation(f_q[rows, h + k], src[rows, :], ACT.Copy, scale=float(FD) ** -0.5).then_inc(s["fp_hi"], 1)
                    else:
                        act.activation(f_k[:, h, 0], src[:], ACT.Copy).then_inc(s["fp_hi"], 1)

                for i in range(len(PROJ)):
                    round_proj(0, i)
                    yield
                yield
                for half in range(2):
                    yield from waits(TILES_H + 2)
                    act.wait_ge(s["fm_t"], at("fm_t", half + 1))
                    act.activation(fmT[0:PARTS * HALF, :], bank[B5][:].bitcast(BF16)[0:PARTS * HALF, 0:S], ACT.Copy).then_inc(s["fm_sb"], 1)
                    yield
                    if half == 0:
                        act.wait_ge(s["gm_t"], at("gm_t", 1))
                        for k in range(2):
                            act.activation(gmT[0:2 * GH, k], bank[B5][2 * GH * k:2 * GH * (k + 1), :], ACT.Copy).then_inc(s["gm_sb"], 1)
                    yield
                    if half == 0:
                        for i in range(T * EF):
                            if i % EF == 0:
                                t = i // EF
                                act.wait_ge(s["ve"], at("ve", i + 1))
                                act.activation(vals[:, t, :, 0:FD], bank[B3 + i % 3][:].rearrange("p (h k) -> p h k", h=HF),
                                               ACT.Copy).then_inc(s["ve_first"], 1)
                            yield
                        yield from waits(2)
                    for u in range(TILES_H + OUT_LAG + 1):
                        if u < TILES_H:
                            kt = u % T
                            j, n = TILES_H * half + u, S - kt * P
                            act.wait_ge(s["fst"], at("fst", j + 1))
                            if j >= RING:
                                act.wait_ge(s["fpv"], at("fpv", j - RING + 1))
                            act.activation(probs_b[:, j % RING, 0:n], bank[B5][:, 0:n], ACT.Exp).then_inc(s["fst_exp"], 1)
                        yield
                        head = u // T - 1
                        h = HALF * half + head
                        if u % T == 1 and 0 <= head < HALF:
                            act.wait_ge(s["fpv"], at("fpv", T * (h + 1)))
                            if h:
                                act.wait_ge(s["fo_lo"], at("fo_lo", h))
                            act.activation(tiles_b[0:FD, 2, :], bank[B4 + 2 * (h % 2)][FD:P, :], ACT.Ln).then_inc(s["f_ln"], 1)
                            act.wait_ge(s["f_ln"], at("f_ln", h + 1))
                            act.activation(tiles_b[0:FD, 2, :], tiles_b[0:FD, 2, :], ACT.Exp, scale=-1.0).then_inc(s["f_rec"], 1)
                        if early_proj(half, u) is not None:
                            round_proj(1, early_proj(half, u))
                        if u % T == 3 and 0 <= head < HALF:
                            act.wait_ge(s["fo_lo"], at("fo_lo", h + 1))
                            act.activation(tiles_b[FD:P, 3 + h % 2, :], tiles_b[0:FD, 3 + h % 2, :], ACT.Copy).then_inc(s["fo_hi"], 1)
                        yield
                act.wait_ge(s["oe"], at("oe", HF * PAIRS))
                act.activation(tiles_b[:, 5, :], bank[B7][:], ACT.Copy).then_inc(s["fo_sb"], 1)
                yield
                yield
                yield
                rstd_rows(at, "ffn", ln_b)
                yield
                yield from waits(2)
                act.wait_ge(s["ffn_turn"], at("ffn_turn", 1))
                act.activation(x_chan[:, par], bank[B7][:], ACT.Copy).then_inc(s["ffn_done"], 1)
                yield

            def gla(batch):
                at, par = counter(batch), batch[1] % 2
                g_ = lambda i: gla_tiles[:, i]
                class_a_free(act, "gla", batch)
                act.wait_ge(s["g_proj"], at("g_proj", 3))
                act.activation(h1T, bank[A2][:], ACT.Copy).then_inc(s["g_h1"], 1)
                for n in range(2):
                    act.activation(g_(n), bank[A0 + n][:], ACT.Exp, scale=-1.0).then_inc(s["g_exp"], 1)
                yield
                for n in range(2):
                    act.wait_ge(s["g_exp"], at("g_exp", n + 1))
                    act.activation(g_(4 + n), g_(n), ACT.Ln, bias=1.0).then_inc(s["g_ln"], 1)
                act.wait_ge(s["g_proj"], at("g_proj", 4))
                act.activation(v_tok, bank[A2][:], ACT.Copy).then_inc(s["g_v"], 1)
                yield
                for n in range(2):
                    act.wait_ge(s["g_ln"], at("g_ln", n + 1))
                    act.activation(g_(2 + n), g_(4 + n), ACT.Exp, scale=-1.0).then_inc(s["g_sig"], 1)
                act.wait_ge(s["g_sig"], at("g_sig", 2))
                act.activation(pre, g_(3), ACT.Identity, scale=-1.0, bias=1.0).then_inc(s["g_f"], 1)
                yield
                act.wait_ge(s["gg_p"], at("gg_p", 1))
                act.activation(tiles_a[:, 3, :], bank[A2][:], ACT.Exp, scale=-1.0).then_inc(s["gg_e"], 1)
                act.wait_ge(s["gg_e"], at("gg_e", 1))
                act.activation(tiles_a[:, 4, :], tiles_a[:, 3, :], ACT.Ln, bias=1.0).then_inc(s["gg_e"], 1)
                act.wait_ge(s["gg_e"], at("gg_e", 2))
                act.activation(tiles_a[:, 5, :], tiles_a[:, 4, :], ACT.Exp, scale=-1.0).then_inc(s["gg_e"], 1)
                yield from waits(21 + 1 + 4 * LEVELS)
                yield from waits(4)
                rstd_rows(at, "gla", ln_a, 1)
                yield
                yield
                act.wait_ge(s["gn_t"], at("gn_t", 1))
                act.activation(tiles_a[:, 0, :], bank[A0][:], ACT.Copy).then_inc(s["gn_sb"], 1)
                yield
                yield
                yield
                yield
                rstd_rows(at, "gla", ln_a, 2)
                yield
                yield from waits(2)
                act.wait_ge(s["gla_turn"], at("gla_turn", 1))
                act.activation(x_chan[:, par], bank[A0][:], ACT.Copy).then_inc(s["gla_done"], 1)
                yield

            def moe(batch, refill=False):
                at, par = counter(batch), batch[1] % 2
                class_b_free(act, "moe", batch)
                yield

                def relu(i):
                    act.wait_ge(s["w1"], at("w1", i + 1))
                    if i >= RING:
                        act.wait_ge(s["w2"], at("w2", i - RING + 1))
                    act.activation(probs_b[:, i % RING, :], bank[B3 + i % 2][:], ACT.Relu, bias=w["b1c"][:, i:i + 1]).then_inc(s["relu"], 1)

                def out_bias(e):
                    act.wait_ge(s["w2"], at("w2", HC * (e + 1)))
                    if e >= 2:
                        act.wait_ge(s["moe_mul"], at("moe_mul", e - 1))
                    act.activation(tiles_b[:, e % 2, :], bank[B6][:], ACT.Identity, bias=w["b2c"][:, e:e + 1]).then_inc(s["oe_b"], 1)

                relu(0)
                yield
                act.wait_ge(s["r_m"], at("r_m", 1))
                act.activation(rt[:, 1], rt[:, 0], ACT.Exp).then_inc(s["r_e"], 1)
                yield
                for i in range(EM * HC):
                    e, c = divmod(i, HC)
                    if c == 0 and e:
                        out_bias(e - 1)
                    if i + 1 < EM * HC:
                        relu(i + 1)
                    yield
                    if i == 3:
                        act.wait_ge(s["r_t"], at("r_t", 1))
                        act.activation(rT[0:2 * EM, :], bank[B5][0:2 * EM, :], ACT.Copy).then_inc(s["r_sb"], 1)
                    yield
                out_bias(EM - 1)
                yield
                yield
                yield
                yield
                rstd_rows(at, "moe", ln_b)
                yield
                yield from waits(3)

            two_by_two(act, B // 2, l0, ffn, gla, moe)

        @block.vector
        def _(dve):
            dve.wait_ge(first_loaded, 16 * n_first)
            dve.tensor_scalar(q_scale[:], w["cols"][:, 2:3], float(HD) ** -0.5, None, ALU.mult).then_inc(const_ready, 1)
            dve.wait_ge(const_ready, POOL_CONSTS + 1)

            def make_constants():
                dve.wait_ge(loaded, all_loaded)
                dve.tensor_copy(ident_b[:], w["ident"][:]).then_inc(const_ready, 1)
                dve.tensor_copy(pick_wide[:].rearrange("p (r k) -> p r k", k=FD),
                                w["picks"][0:PAD, 0:GH].unsqueeze(2).to_broadcast([PAD, GH, FD])).then_inc(const_ready, 1)
                dve.tensor_copy(pick_e[:], w["picks"][0:PAD, GH:GH + EM]).then_inc(const_ready, 1)
                dve.tensor_copy(pick_h[:], w["picks"][0:PAD, GH + EM:]).then_inc(const_ready, 1)
                dve.wait_ge(const_ready, CONSTS)

            def chain_of(at, stage):
                links = [0]

                def link(i):
                    links[0] += 1
                    i.then_inc(s[stage + "_link"], 1)
                    dve.wait_ge(s[stage + "_link"], at(stage + "_link", links[0]))

                def close():
                    dve.sem_inc(s[stage + "_link"], PER[stage + "_link"] - links[0])
                return link, close

            def layer_norm(at, link, stage, ln, src, into, n=1, scale_row=None):
                for t in range(T):
                    link(dve.bn_stats(ln["st"][:, t, :], src[:, t, :]))
                dve.sem_inc(passed, 1)
                for t in range(T):
                    last = dve.bn_aggr(ln["mv"][:, t, :], ln["st"][:, t, :])
                last.then_inc(s[stage + "_var"], 1)
                yield
                yield
                dve.wait_ge(s[stage + "_rs"], at(stage + "_rs", 2 * n))
                done = "moe_done" if stage == "moe" else stage + "_out"
                for t in range(T):
                    last = dve.tensor_scalar(into[:, t, :], src[:, t, :], ln["mv"][:, t, 0:1], ln["r"][:, 1, t:t + 1],
                                             ALU.subtract, ALU.mult)
                last.then_inc(s[done], 1)
                dve.wait_ge(s[done], at(done, n))

            def first_max(link, src, top, eq, cand, top2, onehot):
                n = src.shape[1]
                wide_ = lambda a: a.unsqueeze(2).to_broadcast([P, n, EF])
                link(dve.tensor_reduce(top, src, AX.X, ALU.max))
                link(dve.tensor_tensor(eq, src, wide_(top), ALU.is_equal))
                link(dve.tensor_tensor(cand, eq, w["ramp"][:].unsqueeze(1).to_broadcast([P, n, EF]), ALU.mult))
                link(dve.tensor_reduce(top2, cand, AX.X, ALU.max))
                link(dve.tensor_tensor(onehot, cand, wide_(top2), ALU.is_equal))

            def l0(batch, first=False):
                at, par = counter(batch), batch[1] % 2
                link, close = chain_of(at, "l0")
                x = x_tok[:, par]
                class_a_free(dve, "l0", batch)
                yield
                dve.wait_ge(s["proj"], at("proj", 3))
                for t in range(T):
                    dve.tensor_tensor(vaug[:, t, :, 0:HD], bank[A2][:, t * P:(t + 1) * P].rearrange("p (h d) -> p h d", d=HD),
                                      w["bv_row"][:].rearrange("p (h d) -> p h d", d=HD), ALU.add).then_inc(s["vaug"], 1)
                yield
                yield
                for n in range(2):
                    yield
                    dve.wait_ge(s["rs"], at("rs", 3 + n))
                    nrm, rest_ = tiles_a[:, 4 + n, :], tiles_a[:, 2 + n, :]
                    link(dve.scalar_tensor_tensor(nrm, tiles_a[:, n, :], q_scale[:, 0:1] if n == 0 else w["cols"][:, 3:4],
                                                  tiles_a[:, 2 + n, :], ALU.mult, ALU.mult))
                    link(dve.tensor_copy(parts[:, n, 0, :], nrm))
                    link(dve.tensor_tensor(rest_, nrm, parts[:, n, 0, :], ALU.subtract))
                    link(dve.tensor_copy(parts[:, n, 1, :], rest_))
                    dve.tensor_tensor(parts[:, n, 2, :], rest_, parts[:, n, 1, :], ALU.subtract).then_inc(s["qk_split"], 1)
                if first:
                    make_constants()
                yield from waits(5)
                for u in range(LEAD + GROUPS * SLOTS):
                    g, i = divmod(u, SLOTS)
                    if g < GROUPS and i < GROUP * T:
                        n = g * GROUP * T + i
                        dve.wait_ge(s["s_out"], at("s_out", n + 1))
                        dve.tensor_reduce(m_tok[:, n:n + 1], bank[s_bank(batch, first, u, n)[0]][:], AX.X, ALU.max).then_inc(s["s_max"], 1)
                    elif g < GROUPS and i == GROUP * T:
                        dve.wait_ge(s["m_t"], at("m_t", g + 1))
                        src, k = bank[A0][0:GROUP * T, 0:P], GROUP * T
                        link(dve.tensor_scalar(m_row[:, g, 0, :], src, -1.0, None, ALU.mult))
                        link(dve.scalar_tensor_tensor(m_rest[0:k, 0, :], src, -1.0, m_row[:, g, 0, :], ALU.mult, ALU.subtract))
                        link(dve.tensor_copy(m_row[:, g, 1, :], m_rest[0:k, 0, :]))
                        dve.tensor_tensor(m_row[:, g, 2, :], m_rest[0:k, 0, :], m_row[:, g, 1, :], ALU.subtract).then_inc(s["m_rows"], 1)
                    if u >= LEAD:
                        g, i = divmod(u - LEAD, SLOTS)
                        if i == SLOTS - 1:
                            dve.wait_ge(s["o_t"], at("o_t", g + 1))
                            v = bank[turn_bank(first)][:].rearrange("p (t h c) -> p t h c", t=T, c=VW)
                            rec = m_rest[:, 1, 0:GROUP * T].rearrange("p (t h) -> p t h", t=T)
                            link(dve.reciprocal(rec, v[:, :, :, HD]))
                            dve.tensor_tensor(heads_out[:, :, g * 32:(g + 1) * 32].rearrange("p t (h d) -> p t h d", d=HD),
                                              v[:, :, :, 0:HD], rec.unsqueeze(3).to_broadcast([P, T, GROUP, HD]),
                                              ALU.mult).then_inc(s["o_norm"], 1)
                    yield
                yield
                yield
                dve.wait_ge(s["attn_y"], at("attn_y", 1))
                dve.wait_ge(s["xb"], at("xb", 1))
                flat = x.rearrange("p t d -> p (t d)")
                link(dve.tensor_tensor(flat, bank[A1][:], flat, ALU.add))
                yield from layer_norm(at, link, "l0", ln_a, x, x)
                close()
                yield
                yield from waits(2)

            def ffn(batch):
                at, par = counter(batch), batch[1] % 2
                link, close = chain_of(at, "ffn")
                x = x_tok[:, par]
                class_b_free(dve, "ffn", batch)
                dve.wait_ge(s["gate_e"], at("gate_e", 1))
                g3 = lambda i: gs[:, i, :].rearrange("p (n e) -> p n e", e=EF)
                top, top2 = gsm[:, 0, :], gsm[:, 1, :]
                by_head = lambda a: a.unsqueeze(2).to_broadcast([P, T * HF, EF])
                part = lambda a: gm_tok[:, :, :, a, :]
                gsrc = gs[:, 1, :].rearrange("p (t h c) -> p t h c", t=T, h=2)
                gate_steps = [
                    lambda: link(dve.reciprocal(gs[:, 2, :], gs[:, 1, :])),
                    lambda: link(dve.tensor_reduce(top, g3(2), AX.X, ALU.max)),
                    lambda: link(dve.tensor_tensor(g3(1), g3(2), by_head(top), ALU.is_equal)),
                    lambda: link(dve.tensor_tensor(g3(0), g3(1), w["ramp"][:].unsqueeze(1).to_broadcast([P, T * HF, EF]), ALU.mult)),
                    lambda: link(dve.tensor_reduce(top2, g3(0), AX.X, ALU.max)),
                    lambda: link(dve.tensor_tensor(oh[:], g3(0), by_head(top2), ALU.is_equal)),
                    lambda: link(dve.tensor_tensor(gs[:, 1, :], gs[:, 2, :], oh[:].rearrange("p n e -> p (n e)"), ALU.mult)),
                    lambda: link(dve.tensor_copy(part(0), gsrc)),
                    lambda: dve.tensor_tensor(part(1), gsrc, part(0).bitcast(F32), ALU.subtract).then_inc(s["gate_done"], 1),
                ]
                link(dve.tensor_scalar(gs[:, 1, :], gs[:, 0, :], 1.0, None, ALU.add))
                yield
                def rest_of_proj(half, i):
                    what, h = PROJ[i]
                    src = bank[proj_bank(half, i)]
                    dve.wait_ge(s["fp_hi"], at("fp_hi", 2 * HALF * half + TAKEN[i]))
                    if what == "q":
                        for k in range(2):
                            rows, other = slice(FD * k, FD * (k + 1)), slice(FD * (1 - k), FD * (2 - k))
                            dve.scalar_tensor_tensor(f_q[other, h + k], src[rows, :], float(FD) ** -0.5,
                                                     f_q[rows, h + k].bitcast(F32), ALU.mult, ALU.subtract).then_inc(s["fp_lo"], 1)
                    else:
                        dve.tensor_tensor(f_k[:, h, 1], src[:], f_k[:, h, 0].bitcast(F32), ALU.subtract).then_inc(s["fp_lo"], 1)

                for i in range(len(PROJ) + 1):
                    if i:
                        rest_of_proj(0, i - 1)
                    for step in gate_steps[2 * i:2 * i + 2]:
                        step()
                    yield
                for half in range(2):
                    for u in range(TILES_H):
                        i = TILES_H * half + u
                        h, t = divmod(i, T)
                        n = (t + 1) * P
                        dve.wait_ge(s["fs"], at("fs", i + 1))
                        if i >= 2:
                            dve.wait_ge(s["fs_max"], at("fs_max", i - 1))
                        dve.sem_inc(passed, 1)
                        dve.tensor_tensor_reduce(tiles_b[:, i % 2, 0:n], bank[B3 + u % 3][:, 0:n], w["cut_row"][:, S - n:S], 1.0, -3.4e38,
                                                 ALU.add, ALU.max, fm_tok[:, t, h:h + 1]).then_inc(s["fs_max"], 1)
                        yield
                    dve.wait_ge(s["fs_max"], at("fs_max", TILES_H * (half + 1)))
                    m = fm_tok[:, :, HALF * half:HALF * (half + 1)]
                    link(dve.tensor_scalar(fm_parts[:, :, 0, :], m, -1.0, None, ALU.mult))
                    link(dve.scalar_tensor_tensor(fm_rest[:], m, -1.0, fm_parts[:, :, 0, :], ALU.mult, ALU.subtract))
                    link(dve.tensor_copy(fm_parts[:, :, 1, :], fm_rest[:]))
                    dve.tensor_tensor(fm_parts[:, :, 2, :], fm_rest[:], fm_parts[:, :, 1, :], ALU.subtract).then_inc(s["fm_cut"], 1)
                    yield
                    yield
                    yield
                    yield
                    if half == 0:
                        for i in range(T * EF):
                            t, e = divmod(i, EF)
                            v = vals[:, t, :, 0:FD]
                            heads = slice(t * HF, (t + 1) * HF)
                            if e == 0:
                                dve.wait_ge(s["ve_first"], at("ve_first", t + 1))
                            else:
                                dve.wait_ge(s["ve"], at("ve", i + 1))
                                dve.sem_inc(passed, 1)
                                dve.copy_predicated(v, oh[:, heads, e].bitcast(U32).unsqueeze(2).to_broadcast([P, HF, FD]),
                                                    bank[B3 + i % 3][:].rearrange("p (h k) -> p h k", h=HF)).then_inc(s["ve_sel"], 1)
                                dve.wait_ge(s["ve_sel"], at("ve_sel", t * (EF - 1) + e))
                            yield
                        yield from waits(2)
                    for u in range(TILES_H + OUT_LAG + 1):
                        yield
                        if u % T == 2 and T < u <= TILES_H + T:
                            h = HALF * half + u // T - 1
                            dve.wait_ge(s["f_rec"], at("f_rec", h + 1))
                            if h >= 2:
                                dve.wait_ge(s["g_in"], at("g_in", PAIRS * (h - 1)))
                            dve.tensor_tensor(tiles_b[0:FD, 3 + h % 2, :], bank[B4 + 2 * (h % 2)][0:FD, :], tiles_b[0:FD, 2, :], ALU.mult).then_inc(s["fo_lo"], 1)
                        if OUT_LAG <= u < TILES_H + OUT_LAG:
                            c = HALF * PAIRS * half + u - OUT_LAG
                            h = c // PAIRS
                            if c % PAIRS == 0:
                                dve.wait_ge(s["fo_hi"], at("fo_hi", h + 1))
                            dve.wait_ge(s["mask"], at("mask", c + 1))
                            if c >= 2:
                                dve.wait_ge(s["oe"], at("oe", c - 1))
                            dve.tensor_tensor(tiles_b[:, c % 2, :], bank[mask_bank(half, u)][:], tiles_b[:, 3 + h % 2, :], ALU.mult).then_inc(s["g_in"], 1)
                        if early_proj(half, u - 1) is not None:
                            rest_of_proj(1, early_proj(half, u - 1))
                        yield
                yield
                yield
                dve.wait_ge(s["fo_t"], at("fo_t", 1))
                flat = x.rearrange("p t d -> p (t d)")
                close()
                link, close = chain_of(at, "ffn_norm")
                link(dve.tensor_tensor(flat, bank[B5][:], flat, ALU.add))
                yield from layer_norm(at, link, "ffn", ln_b, x, x)
                yield
                yield from waits(2)

            def gla(batch):
                at, par = counter(batch), batch[1] % 2
                link, close = chain_of(at, "gla")
                x = x_tok[:, par]
                g_ = lambda i: gla_tiles[:, i]
                class_a_free(dve, "gla", batch)
                yield
                yield
                dve.wait_ge(s["g_ln"], at("g_ln", 2))
                link(dve.tensor_scalar(g_(0), bank[A1][:], F_UP, None, ALU.is_lt))
                link(dve.tensor_scalar(g_(1), bank[A1][:], F_DOWN, None, ALU.is_gt))
                yield
                for op in (
                    lambda: dve.memset(suf, 1.0),
                    lambda: dve.tensor_tensor(g_(6), g_(0), g_(1), ALU.subtract),
                    lambda: dve.tensor_tensor_scan(g_(7), suf, g_(6), 0.0, ALU.mult, ALU.add),
                    lambda: dve.tensor_tensor(g_(0), g_(6), g_(6), ALU.mult),
                    lambda: dve.tensor_scalar(g_(1), g_(0), -2.0, 1.0, ALU.mult, ALU.add),
                    lambda: dve.tensor_tensor_scan(g_(8), g_(1), suf, 1.0, ALU.mult, ALU.mult),
                    lambda: dve.tensor_scalar(g_(0), g_(7), PI, None, ALU.mult),
                    lambda: dve.scalar_tensor_tensor(g_(1), g_(7), -PI1, g_(0), ALU.mult, ALU.add),
                    lambda: dve.scalar_tensor_tensor(g_(0), g_(7), -PI2, g_(1), ALU.mult, ALU.add),
                    lambda: dve.scalar_tensor_tensor(g_(1), g_(7), -PI3, g_(0), ALU.mult, ALU.add),
                    lambda: dve.tensor_tensor(g_(0), g_(1), g_(1), ALU.mult),
                    lambda: dve.tensor_scalar(g_(6), g_(0), -1.0 / 6, 1.0, ALU.mult, ALU.add),
                    lambda: dve.tensor_tensor(g_(7), g_(6), g_(1), ALU.mult),
                    lambda: dve.tensor_scalar(g_(6), g_(0), -0.5, 1.0, ALU.mult, ALU.add),
                    lambda: dve.tensor_tensor(g_(0), g_(6), g_(8), ALU.mult),
                    lambda: dve.tensor_tensor(g_(1), g_(7), g_(8), ALU.mult),
                ):
                    link(op())
                    yield
                dve.wait_ge(s["g_sig"], at("g_sig", 2))
                link(dve.scalar_tensor_tensor(g_(4), g_(2), float(2 * D) ** -0.5, bank[A0][:], ALU.mult, ALU.mult))
                yield
                dve.wait_ge(s["g_f"], at("g_f", 1))
                yield
                twice = lambda a: a.unsqueeze(1).to_broadcast([P, 2, S])
                sin_cos = gla_tiles[:, 0:2]
                link(dve.tensor_tensor(qc, sin_cos, twice(g_(4)), ALU.mult))
                yield
                dve.tensor_tensor(kc, sin_cos, twice(g_(3)), ALU.mult).then_inc(s["lv_in"], 1)
                dve.wait_ge(s["lv_in"], at("lv_in", 1))
                yield
                yield
                yield

                def take_level(lv):
                    dve.wait_ge(s["lv_mm"], at("lv_mm", lv + 1))
                    src = bank[A0 + lv % 2]
                    mask = w["level_mask"][:, min(lv, IN_TILE), :].unsqueeze(1).to_broadcast([P, T, P])
                    four = lambda a: a.rearrange("p (c i) -> p c i", c=T)
                    if lv == 0:
                        i = dve.tensor_tensor(four(at_diag), four(src[:]), mask, ALU.mult)
                    elif lv <= IN_TILE:
                        dve.sem_inc(passed, 1)
                        i = dve.copy_predicated(four(at_diag), mask.bitcast(U32), four(src[:]))
                    elif lv == IN_TILE + 1:
                        i = dve.tensor_copy(at_near, src[:, 0:2 * P])
                    else:
                        i = dve.tensor_copy(at_far, src[:])
                    i.then_inc(s["lv_out"], 1)

                for lv in range(1, LEVELS + 1):
                    hs = 1 << (lv - 1)
                    halves = lambda a: a.rearrange("p (n two i) -> p n two i", two=2, i=hs)
                    n = S // (2 * hs)
                    if lv >= 3:
                        dve.wait_ge(s["lv_mm"], at("lv_mm", lv - 1))
                    for c in range(2):
                        link(dve.tensor_tensor(halves(q_lv[lv % 2][:, c])[:, :, 1], halves(qc[:, c])[:, :, 1],
                                               halves(pre)[:, :, 1], ALU.mult))
                    yield
                    link(dve.tensor_tensor(halves(k_lv[lv % 2][:, 0])[:, :, 0], halves(kc[:, 0])[:, :, 0],
                                           halves(suf)[:, :, 0], ALU.mult))
                    dve.tensor_tensor(halves(k_lv[lv % 2][:, 1])[:, :, 0], halves(kc[:, 1])[:, :, 0],
                                      halves(suf)[:, :, 0], ALU.mult).then_inc(s["lv_in"], 1)
                    yield
                    if lv < LEVELS:
                        link(dve.tensor_tensor(halves(suf)[:, :, 0], halves(suf)[:, :, 0],
                                               halves(pre)[:, :, 1, hs - 1:hs].to_broadcast([P, n, hs]), ALU.mult))
                        link(dve.tensor_tensor(halves(pre)[:, :, 1], halves(pre)[:, :, 1],
                                               halves(pre)[:, :, 0, hs - 1:hs].to_broadcast([P, n, hs]), ALU.mult))
                    yield
                    if lv >= 2:
                        dve.wait_ge(s["lv_out"], at("lv_out", lv - 1))
                    take_level(lv - 1)
                    yield
                take_level(LEVELS)
                yield
                yield
                dve.wait_ge(s["gg_e"], at("gg_e", 3))
                dve.wait_ge(s["g_o"], at("g_o", 1))
                by_token = lambda i: tiles_a[:, i, :].rearrange("p (t d) -> p t d", t=T)
                link(dve.tensor_tensor(tiles_a[:, 1, :], bank[A2][:], tiles_a[:, 5, :], ALU.mult))
                yield from layer_norm(at, link, "gla", ln_a, by_token(1), by_token(2))
                dve.tensor_tensor(by_token(3), by_token(2), w["gn_row"][:].unsqueeze(1).to_broadcast([P, T, P]), ALU.mult).then_inc(s["gn"], 1)
                yield
                yield from waits(3)
                dve.wait_ge(s["gla_p"], at("gla_p", 1))
                flat = x.rearrange("p t d -> p (t d)")
                link(dve.tensor_tensor(flat, bank[A1][:], flat, ALU.add))
                yield from layer_norm(at, link, "gla", ln_a, x, x, n=2)
                close()
                yield
                yield from waits(2)

            def moe(batch, refill=False):
                at, par = counter(batch), batch[1] % 2
                link, close = chain_of(at, "moe")
                x = x_tok[:, par]
                class_b_free(dve, "moe", batch)
                r = lambda i: rt[:, i]
                by_tile = lambda a: a.unsqueeze(2).to_broadcast([P, T, EM])

                dve.wait_ge(s["r_p"], at("r_p", 1))
                link(dve.tensor_tensor(r(2), bank[B5][:, 0:T * EM].rearrange("p (t e) -> p t e", t=T),
                                       w["br_row"][:].unsqueeze(1).to_broadcast([P, T, EM]), ALU.add))
                link(dve.tensor_reduce(rt1[:, 0, :], r(2), AX.X, ALU.max))
                dve.tensor_tensor(r(0), r(2), by_tile(rt1[:, 0, :]), ALU.subtract).then_inc(s["r_m"], 1)
                yield
                yield
                yield

                def route():
                    dve.wait_ge(s["r_e"], at("r_e", 1))
                    link(dve.tensor_reduce(rt1[:, 1, :], r(1), AX.X, ALU.add))
                    link(dve.reciprocal(rt1[:, 2, :], rt1[:, 1, :]))
                    link(dve.tensor_tensor(r(2), r(1), by_tile(rt1[:, 2, :]), ALU.mult))
                    first_max(link, r(2), rt1[:, 0, :], r(0), r(1), rt1[:, 1, :], r(3))
                    yield
                    link(dve.scalar_tensor_tensor(r(4), r(3), -2.0, r(2), ALU.mult, ALU.add))
                    first_max(link, r(4), rt1[:, 0, :], r(0), r(1), rt1[:, 1, :], r(5))
                    yield
                    link(dve.tensor_tensor(r(0), r(3), r(5), ALU.add))
                    link(dve.tensor_tensor(r(1), r(0), r(2), ALU.mult))
                    link(dve.tensor_reduce(rt1[:, 0, :], r(1), AX.X, ALU.add))
                    link(dve.reciprocal(rt1[:, 1, :], rt1[:, 0, :]))
                    link(dve.tensor_tensor(r(0), r(1), by_tile(rt1[:, 1, :]), ALU.mult))
                    link(dve.tensor_copy(r_tok[:, :, 0, :], r(0)))
                    dve.tensor_tensor(r_tok[:, :, 1, :], r(0), r_tok[:, :, 0, :].bitcast(F32), ALU.subtract).then_inc(s["r_done"], 1)
                    yield

                def weigh_expert(e):
                    dve.wait_ge(s["oe_b"], at("oe_b", e + 1))
                    dve.wait_ge(s["rb"], at("rb", e + 1))
                    to = tiles_b[:, 2, :] if e == 0 else tiles_b[:, 3, :]
                    dve.tensor_tensor(to, bank[B5][:], tiles_b[:, e % 2, :], ALU.mult).then_inc(s["moe_mul"], 1)
                    dve.wait_ge(s["moe_mul"], at("moe_mul", e + 1))
                    if e:
                        total = dve.tensor_tensor(tiles_b[:, 2, :], tiles_b[:, 2, :], tiles_b[:, 3, :], ALU.add)
                        if e < EM - 1:
                            link(total)
                        else:
                            total.then_inc(s["moe_acc"], 1)

                routing = route()
                for i in range(EM * HC):
                    e, c = divmod(i, HC)
                    yield
                    if i < 3:
                        next(routing)
                    if c == 1 and e:
                        weigh_expert(e - 1)
                    yield
                yield
                weigh_expert(EM - 1)
                yield
                yield
                dve.wait_ge(s["mo_t"], at("mo_t", 1))
                flat = x.rearrange("p t d -> p (t d)")
                link(dve.tensor_tensor(flat, bank[B3][:], flat, ALU.add))
                yield from layer_norm(at, link, "moe", ln_b, x, x)
                close()
                if batch[1] == 1:
                    dve.sem_inc(class_b_idle, 1)
                yield
                yield from waits(2)

            two_by_two(dve, B // 2, l0, ffn, gla, moe)


def waits(n):
    for _ in range(n):
        yield


POOL_CONSTS, DVE_CONSTS = 8, 5
CONSTS = POOL_CONSTS + DVE_CONSTS


def host_constants():
    c = {}
    eye = np.eye(P, dtype=np.float32)
    c["ident"] = eye
    c["ramp"] = np.tile(np.arange(EF, 0, -1, dtype=np.float32), (P, 1))
    picks = np.zeros((P, GH + EM + HALF), np.float32)
    for r in range(P):
        if r < 2 * GH:
            picks[r, r % GH] = 1
        if r < 2 * EM:
            picks[r, GH + r % EM] = 1
        if r < PARTS * HALF:
            picks[r, GH + EM + r % HALF] = 1
    c["picks"] = picks
    cut = np.zeros((P, S), np.float32)
    cut[:, S - P:] = np.where(np.arange(P)[None, :] > np.arange(P)[:, None], np.float32(NEG), np.float32(0))
    c["cut_row"] = cut
    j, i = np.arange(P)[:, None], np.arange(P)[None, :]
    masks = [(j == i)]
    for l in range(IN_TILE):
        hs = 1 << l
        masks.append(((j // (2 * hs)) == (i // (2 * hs))) & ((j // hs) % 2 == 0) & ((i // hs) % 2 == 1))
    c["level_mask"] = np.stack(masks, axis=1).astype(np.float32)
    return c


def laid_out(i):
    C = np.ascontiguousarray
    row = lambda v: C(np.broadcast_to(v, (P, v.shape[0])))
    a = {}
    x = i["L0_attn_x"]
    a["x"], a["xT"] = x, C(x.transpose(0, 2, 1))
    for n, m in (("wq0", "Wq"), ("wk0", "Wk"), ("wv0", "Wv"), ("wo0", "Wo")):
        a[n] = C(i[f"L0_attn_{m}"].T)
    a["bv_row"], a["bo_row"] = row(i["L0_attn_bv"]), row(i["L0_attn_bo"])
    a["cols"] = C(np.stack([i["L0_attn_bq"], i["L0_attn_bk"], i["L0_attn_norm_q_w"], i["L0_attn_norm_k_w"]], axis=1))
    for n, m in (("gwq", "wq"), ("gwk", "wk"), ("gwv", "wv"), ("gwo", "wo"), ("gwg1", "wg1"), ("gwg2", "wg2")):
        a[n] = i[f"L1_attn_{m}"]
    a["gn_row"] = row(i["L1_attn_norm_w"])
    a["fwq"] = i["L0_ffn_w_q"]
    a["fwk"] = C(np.broadcast_to(i["L0_ffn_w_k"].reshape(D, HF, 1, FD), (D, HF, 2, FD)).reshape(D, HF, 2 * FD))
    a["fgate"] = i["L0_ffn_w_gate"]
    a["ve"] = C(i["L0_ffn_value_experts"].transpose(2, 0, 1, 3).reshape(D, EF, HF * FD))
    oe = i["L0_ffn_output_experts"].reshape(PAIRS, 2, HF, FD, D)
    a["oe"] = C(oe.transpose(1, 3, 2, 0, 4).reshape(P, HF * PAIRS, D))
    a["w1"] = C(i["L1_ffn_W1"].transpose(1, 0, 2))
    a["w2"] = C(i["L1_ffn_W2"].reshape(EM * HC, P, D).transpose(1, 0, 2))
    a["b1c"] = C(i["L1_ffn_b1"].reshape(EM * HC, P).T)
    a["b2c"] = C(i["L1_ffn_b2"].T)
    a["wr"], a["br_row"] = i["L1_ffn_Wr"], row(i["L1_ffn_br"])
    a.update(host_constants())
    return a


def kernel(**inputs):
    import concourse.bacc as bacc
    from concourse.bass_utils import run_bass_kernel_spmd as run

    arrays = laid_out({k: np.asarray(v) for k, v in inputs.items()})
    nc = bacc.Bacc("TRN2", target_bir_lowering=False, num_devices=1)
    ins = {n: nc.dram_tensor(n + "_in", a.shape, mybir.dt.from_np(a.dtype), kind="ExternalInput").ap() for n, a in arrays.items()}
    out = nc.dram_tensor("out_dram", (B, S, D), F32, kind="ExternalOutput").ap()
    build(nc, ins, out)
    r = run(nc, [{n + "_in": a for n, a in arrays.items()}], core_ids=[0])
    return r.results[0]["out_dram"]
```
